# Optimizing a Trainium2 kernel written in Bass

```python
import numpy as np
import jax
import jax.numpy as jnp

def _softmax(x, axis=-1):
    return jax.nn.softmax(x, axis=axis)

def _gelu(x):
    return jax.nn.gelu(x, approximate=True)

def _silu(x):
    return jax.nn.silu(x)

def _sigmoid(x):
    return jax.nn.sigmoid(x)

def _layernorm(x, axis=-1, eps=1e-05):
    m = jnp.mean(x, axis=axis, keepdims=True)
    v = jnp.var(x, axis=axis, keepdims=True)
    return (x - m) / jnp.sqrt(v + eps)

def _scatter_add(tgt, idx, src, axis=0):
    return tgt.at[idx].add(src)

def _segment_sum(src, seg, n):
    return jax.ops.segment_sum(src, seg, n)
kernel_name = 'mk_xattn_ffn_d2_seqx_r4_ba8db4'

def setup_inputs(seed: int=0):
    np.random.seed(seed)
    _w = jnp.asarray

    def _rec_inputs():
        import jax
        import jax.numpy as jnp
        _rk = jax.random.key(seed)
        x = -0.000125 + 0.9999 * jax.random.normal(jax.random.fold_in(_rk, 1), (4, 512, 512), jnp.float32)
        _lenS = 512 - jax.random.randint(jax.random.fold_in(_rk, 7), (4,), 0, max(1, 512 // 4) + 1, jnp.int32)
        _lenS2 = 512 - jax.random.randint(jax.random.fold_in(_rk, 8), (4,), 0, max(1, 512 // 4) + 1, jnp.int32)
        _ctx_2048P = jax.random.normal(jax.random.fold_in(_rk, 11), (4, 16, 512), jnp.float32)
        _ctx_2048c = jax.random.dirichlet(jax.random.fold_in(_rk, 511), 0.3 * jnp.ones((16,), jnp.float32), (4, 512))
        _ctx_2048t = jnp.einsum('bsk,bkd->bsd', _ctx_2048c, _ctx_2048P)
        _ctx_2048t = _ctx_2048t * jax.lax.rsqrt(jnp.mean(jnp.square(_ctx_2048t)) + 1e-12) * 0.953939
        ctx_2048 = -0.00010331 + 0.999899 * (_ctx_2048t + 0.3 * jax.random.normal(jax.random.fold_in(_rk, 611), (4, 512, 512), jnp.float32))
        _validS = jnp.arange(512)[None, :] < _lenS[:, None]
        _validS2 = jnp.arange(512)[None, :] < _lenS2[:, None]
        _causal = jnp.tril(jnp.ones((512, 512), dtype=bool))
        mask_Bx1xS2_ff0 = jnp.where(jnp.ones((4, 1, 512), dtype=bool), 0.0, -1000000000.0).astype(jnp.float32)
        return (x, ctx_2048, mask_Bx1xS2_ff0)
    x, ctx_2048, mask_Bx1xS2_ff0 = _rec_inputs()

    def _L0_xattn_setup():
        import jax, jax.numpy as jnp
        import numpy as np
        FP8_E4M3_MAX = 448.0
        EPS = 1e-12

        def _fp8_quant_dequant(x):
            amax = jnp.max(jnp.abs(x))
            scale = FP8_E4M3_MAX / jnp.maximum(amax, EPS)
            q = jnp.clip(x * scale, -FP8_E4M3_MAX, FP8_E4M3_MAX).astype(jnp.float8_e4m3fn)
            return q.astype(jnp.float32) / scale
        key = jax.random.key(seed)
        k1, k2 = jax.random.split(key)
        B, M, K, N = (32, 128, 512, 512)
        inp = jax.random.normal(k1, (B, M, K), dtype=jnp.float32)
        weight = jax.random.normal(k2, (B, K, N), dtype=jnp.float32)
        bias = jnp.zeros((B, 1, N), dtype=jnp.float32)
        return {'input': inp, 'weight': weight, 'bias': bias}
    _L0_xattn_all = _L0_xattn_setup()
    _L0_xattn_in = {k: v for k, v in _L0_xattn_all.items() if k in ()}
    del _L0_xattn_all

    def _L0_ffn_setup():
        import jax, jax.numpy as jnp
        import numpy as np
        K_TOP = 2
        key = jax.random.key(seed)
        ks = jax.random.split(key, 6)
        s = 0.02
        B, S, H, D = (4, 256, 512, 256)
        E_SH, E_RT = (2, 16)
        return {'x': jax.random.normal(ks[0], (B, S, H), dtype=jnp.float32), 'Wsh_up': jax.random.normal(ks[1], (E_SH, H, D), dtype=jnp.float32) * s, 'Wsh_down': jax.random.normal(ks[2], (E_SH, D, H), dtype=jnp.float32) * s, 'Wrt_up': jax.random.normal(ks[3], (E_RT, H, D), dtype=jnp.float32) * s, 'Wrt_down': jax.random.normal(ks[4], (E_RT, D, H), dtype=jnp.float32) * s, 'W_router': jax.random.normal(ks[5], (H, E_RT), dtype=jnp.float32) * s}
    _L0_ffn_all = _L0_ffn_setup()
    _L0_ffn_in = {k: v for k, v in _L0_ffn_all.items() if k in ('Wsh_up', 'Wsh_down', 'Wrt_up', 'Wrt_down', 'W_router')}
    del _L0_ffn_all

    def _L1_xattn_setup():
        import jax, jax.numpy as jnp
        import numpy as np
        B, S, D = (8, 256, 512)
        H, HD = (16, 128)
        key = jax.random.key(seed)
        ks = jax.random.split(key, 6)
        fan_in = 1.0 / np.sqrt(D)
        return {'inputs_q': jax.random.normal(ks[0], (B, S, D), jnp.float32), 'inputs_kv': jax.random.normal(ks[1], (B, S, D), jnp.float32), 'Wq': jax.random.normal(ks[2], (D, H * HD), jnp.float32) * fan_in, 'Wk': jax.random.normal(ks[3], (D, H * HD), jnp.float32) * fan_in, 'Wv': jax.random.normal(ks[4], (D, H * HD), jnp.float32) * fan_in, 'Wo': jax.random.normal(ks[5], (H * HD, D), jnp.float32) * (1.0 / np.sqrt(H * HD))}
    _L1_xattn_all = _L1_xattn_setup()
    _L1_xattn_in = {k: v for k, v in _L1_xattn_all.items() if k in ('Wq', 'Wk', 'Wv', 'Wo')}
    del _L1_xattn_all

    def _L1_ffn_setup():
        import jax, jax.numpy as jnp
        import numpy as np
        B, S, D, H = (4, 512, 512, 2048)

        def fwht(x):
            orig_shape = x.shape
            n = orig_shape[-1]
            x = x.reshape(-1, n)
            h = 1
            while h < n:
                xb = x.reshape(-1, n // (2 * h), 2, h)
                a = xb[:, :, 0, :]
                b = xb[:, :, 1, :]
                x = jnp.stack([a + b, a - b], axis=2).reshape(-1, n)
                h *= 2
            scale = jnp.asarray(1.0 / np.sqrt(n), dtype=x.dtype)
            return (x * scale).reshape(orig_shape)
        key = jax.random.key(seed)
        kx, k1, k2, k3 = jax.random.split(key, 4)
        x = jax.random.normal(kx, (B, S, D), dtype=jnp.float32)
        W1 = jax.random.normal(k1, (H, D), dtype=jnp.float32) * (1.0 / np.sqrt(D))
        W2 = jax.random.normal(k2, (D, H), dtype=jnp.float32) * (1.0 / np.sqrt(H))
        W3 = jax.random.normal(k3, (H, D), dtype=jnp.float32) * (1.0 / np.sqrt(D))
        return {'x': x, 'W1': W1, 'W2': W2, 'W3': W3}
    _L1_ffn_all = _L1_ffn_setup()
    _L1_ffn_in = {k: v for k, v in _L1_ffn_all.items() if k in ('W1', 'W2', 'W3')}
    del _L1_ffn_all
    return {'x': x, 'ctx_2048': ctx_2048, 'mask_Bx1xS2_ff0': mask_Bx1xS2_ff0, 'L0_ffn_Wsh_up': _L0_ffn_in['Wsh_up'], 'L0_ffn_Wsh_down': _L0_ffn_in['Wsh_down'], 'L0_ffn_Wrt_up': _L0_ffn_in['Wrt_up'], 'L0_ffn_Wrt_down': _L0_ffn_in['Wrt_down'], 'L0_ffn_W_router': _L0_ffn_in['W_router'], 'L1_xattn_Wq': _L1_xattn_in['Wq'], 'L1_xattn_Wk': _L1_xattn_in['Wk'], 'L1_xattn_Wv': _L1_xattn_in['Wv'], 'L1_xattn_Wo': _L1_xattn_in['Wo'], 'L1_ffn_W1': _L1_ffn_in['W1'], 'L1_ffn_W2': _L1_ffn_in['W2'], 'L1_ffn_W3': _L1_ffn_in['W3']}

def reference(x, ctx_2048, mask_Bx1xS2_ff0, L0_ffn_Wsh_up, L0_ffn_Wsh_down, L0_ffn_Wrt_up, L0_ffn_Wrt_down, L0_ffn_W_router, L1_xattn_Wq, L1_xattn_Wk, L1_xattn_Wv, L1_xattn_Wo, L1_ffn_W1, L1_ffn_W2, L1_ffn_W3):
    import jax
    import jax.numpy as jnp

    def _L0_xattn_ref(input, weight, bias):
        import jax, jax.numpy as jnp
        import numpy as np
        FP8_E4M3_MAX = 448.0
        EPS = 1e-12

        def _fp8_quant_dequant(x):
            amax = jnp.max(jnp.abs(x))
            scale = FP8_E4M3_MAX / jnp.maximum(amax, EPS)
            q = jnp.clip(x * scale, -FP8_E4M3_MAX, FP8_E4M3_MAX).astype(jnp.float8_e4m3fn)
            return q.astype(jnp.float32) / scale
        x_dq = _fp8_quant_dequant(input)
        w_dq = _fp8_quant_dequant(weight)
        out = jnp.einsum('bmk,bkn->bmn', x_dq, w_dq)
        out = out + bias
        return out

    def _L0_ffn_ref(x, Wsh_up, Wsh_down, Wrt_up, Wrt_down, W_router):
        import jax, jax.numpy as jnp
        import numpy as np
        K_TOP = 2
        B, S, H = x.shape
        E_rt = Wrt_up.shape[0]
        xt = x.reshape(B * S, H)
        sh_mid = jax.nn.gelu(jnp.einsum('th,ehd->ted', xt, Wsh_up), approximate=False)
        shared_out = jnp.einsum('ted,edh->th', sh_mid, Wsh_down)
        probs = jax.nn.softmax(xt @ W_router, axis=-1)
        top_v, top_i = jax.lax.top_k(probs, K_TOP)
        gate = jnp.sum(jax.nn.one_hot(top_i, E_rt, dtype=xt.dtype) * top_v[..., None], axis=1)
        rt_mid = jax.nn.gelu(jnp.einsum('th,ehd->ted', xt, Wrt_up), approximate=False)
        routed_out = jnp.einsum('ted,edh->th', rt_mid * gate[:, :, None], Wrt_down)
        return (shared_out + routed_out).reshape(B, S, H)

    def _L1_xattn_ref(inputs_q, inputs_kv, Wq, Wk, Wv, Wo):
        import jax, jax.numpy as jnp
        import numpy as np
        B, S, D = (8, 256, 512)
        H, HD = (16, 128)
        b, sq, _ = inputs_q.shape
        skv = inputs_kv.shape[1]
        q = (inputs_q @ Wq).reshape(b, sq, H, HD) * (1.0 / np.sqrt(HD))
        k = (inputs_kv @ Wk).reshape(b, skv, H, HD)
        v = (inputs_kv @ Wv).reshape(b, skv, H, HD)
        scores = jnp.einsum('bqhd,bkhd->bhqk', q, k)
        attn = jax.nn.softmax(scores, axis=-1)
        ctx = jnp.einsum('bhqk,bkhd->bqhd', attn, v).reshape(b, sq, H * HD)
        return ctx @ Wo

    def _L1_ffn_ref(x, W1, W2, W3):
        import jax, jax.numpy as jnp
        import numpy as np
        B, S, D, H = (4, 512, 512, 2048)

        def fwht(x):
            orig_shape = x.shape
            n = orig_shape[-1]
            x = x.reshape(-1, n)
            h = 1
            while h < n:
                xb = x.reshape(-1, n // (2 * h), 2, h)
                a = xb[:, :, 0, :]
                b = xb[:, :, 1, :]
                x = jnp.stack([a + b, a - b], axis=2).reshape(-1, n)
                h *= 2
            scale = jnp.asarray(1.0 / np.sqrt(n), dtype=x.dtype)
            return (x * scale).reshape(orig_shape)
        up_gate = jnp.einsum('bsd,hd->bsh', x, W1)
        up_lin = jnp.einsum('bsd,hd->bsh', x, W3)
        hidden = jax.nn.silu(up_gate) * up_lin
        hidden = fwht(hidden)
        out = jnp.einsum('bsh,dh->bsd', hidden, W2)
        return out
    x = x + _L0_xattn_ref(_layernorm(x, axis=-1), ctx_2048, mask_Bx1xS2_ff0)
    x = x + _L0_ffn_ref(_layernorm(x, axis=-1), L0_ffn_Wsh_up, L0_ffn_Wsh_down, L0_ffn_Wrt_up, L0_ffn_Wrt_down, L0_ffn_W_router)
    x = x + _L1_xattn_ref(_layernorm(x, axis=-1), ctx_2048, L1_xattn_Wq, L1_xattn_Wk, L1_xattn_Wv, L1_xattn_Wo)
    x = x + _L1_ffn_ref(_layernorm(x, axis=-1), L1_ffn_W1, L1_ffn_W2, L1_ffn_W3)
    return x

_drawn_inputs = setup_inputs


def setup_inputs(seed=0):
    import zlib

    import numpy as np

    out = dict(_drawn_inputs(seed))
    spreads = {}
    factors = {'L0_ffn_Wsh_up': 8.0,
     'L0_ffn_Wsh_down': 8.0,
     'L0_ffn_Wrt_up': 8.0,
     'L0_ffn_Wrt_down': 8.0,
     'L0_ffn_W_router': 8.0,
     'L1_xattn_Wq': 5.689,
     'L1_xattn_Wk': 5.665}
    for name, (base, spread) in spreads.items():
        noise = np.random.default_rng([zlib.crc32(name.encode()), seed]).standard_normal(out[name].shape)
        drawn = base * np.exp(spread * noise) if base else spread * noise
        out[name] = jnp.asarray(drawn.astype(out[name].dtype))
    for name, factor in factors.items():
        out[name] = (out[name] * factor).astype(out[name].dtype)
    return out
```

```python
from contextlib import ExitStack

import concourse.bass as bass
from concourse import mybir

F32 = mybir.dt.float32
F32R = mybir.dt.float32r
BF16 = mybir.dt.bfloat16
U32 = mybir.dt.uint32
ALU = mybir.AluOpType
ACT = mybir.ActivationFunctionType
AX = mybir.AxisListType

P = 128
B, S, D = 4, 512, 512
KD = D // P
TB = S // P
NT = B * TB
EPS = 1e-5

FP8_MAX = 448.0
FP8_AMAX_EPS = 1e-12
FP8_MIN_NORMAL = 2.0 ** -6
ROUND_MAGIC = 1.5 * 2.0 ** 20
EXPONENT_BITS = 0x7F800000

E_SH, E_RT, DE = 2, 16, 256
E_ALL = E_SH + E_RT
KE = DE // P
H, HD = 16, 128
PAIRS = B // 2
FH = 2048
GH = 256
KG = GH // P
NG = FH // GH


def three_pass(pe, out, w_hi, w_lo, x_hi, x_lo, k_tiles):
    for k in range(k_tiles):
        for j, (w, x) in enumerate(((w_hi, x_hi), (w_hi, x_lo), (w_lo, x_hi))):
            ins = pe.matmul(out, w(k), x(k), start=(k == 0 and j == 0), stop=(k == k_tiles - 1 and j == 2))
    return ins


def f32(ap):
    return ap.bitcast(F32)


def inverse_root(dve, link, var, root, rough, work, rstd):
    link(dve.reciprocal(rough, root))
    link(dve.scalar_tensor_tensor(out=work, in0=rough, scalar=-0.5, in1=rough, op0=ALU.mult, op1=ALU.mult))
    link(dve.tensor_tensor(work, work, var, ALU.mult))
    link(dve.scalar_tensor_tensor(out=rstd, in0=work, scalar=1.5, in1=rough, op0=ALU.add, op1=ALU.mult))


class Alloc:

    def __init__(self, nc, ctx, tag):
        self.nc, self.ctx, self.tag = nc, ctx, tag

    def sb(self, name, shape, dt=F32):
        return self.ctx.enter_context(self.nc.sbuf_tensor(f"{self.tag}_{name}", [P] + shape, dt))

    def ps(self, name, shape, dt=F32):
        return self.ctx.enter_context(self.nc.psum_tensor(f"{self.tag}_{name}", [P] + shape, dt))

    def sem(self, name):
        return self.ctx.enter_context(self.nc.semaphore(f"{self.tag}_{name}"))


class LayerNorm:

    def __init__(self, al, x_res, ident, banks):
        self.x_res, self.ident, self.banks = x_res, ident, banks
        self.stats = al.sb("ln_stats", [TB, 6])
        self.mean_var = al.sb("ln_mean_var", [TB, 2])
        self.var, self.root, self.rough = al.sb("ln_var", [TB]), al.sb("ln_root", [TB]), al.sb("ln_rough", [TB])
        self.work, self.rstd = al.sb("ln_work", [TB]), al.sb("ln_rstd", [TB])
        self.xn = al.sb("ln_xn", [TB, D])
        self.chain = al.sem("ln_chain")
        self.var_ready = al.sem("ln_var_ready")
        self.root_ready = al.sem("ln_root_ready")
        self.xn_ready = al.sem("ln_xn_ready")
        self.turned = al.sem("ln_turned")
        self.hi_ready = al.sem("ln_hi_ready")
        self.lo_ready = al.sem("ln_lo_ready")
        self.links = 0

    def link(self, dve, ins):
        self.links += 1
        ins.then_inc(self.chain, 1)
        dve.wait_ge(self.chain, self.links)

    def vector_stats(self, dve, g):
        for j in range(TB):
            ins = dve.bn_stats(self.stats[:, j, :], self.x_res[:, TB * g + j, :])
        self.link(dve, ins)
        for j in range(TB):
            ins = dve.bn_aggr(self.mean_var[:, j, :], self.stats[:, j, :])
        self.link(dve, ins)
        dve.tensor_scalar(self.var[:, :], self.mean_var[:, :, 1], EPS, None, ALU.add).then_inc(self.var_ready, 1)

    def scalar_root(self, act, nth):
        act.wait_ge(self.var_ready, nth + 1)
        act.activation(self.root[:, :], self.var[:, :], ACT.Sqrt).then_inc(self.root_ready, 1)

    def vector_norm(self, dve, g, nth):
        dve.wait_ge(self.root_ready, nth + 1)
        inverse_root(dve, lambda ins: self.link(dve, ins), self.var[:, :], self.root[:, :], self.rough[:, :],
                     self.work[:, :], self.rstd[:, :])
        if nth > 0:
            dve.wait_ge(self.turned, TB * nth)
        for j in range(TB):
            dve.tensor_scalar(self.xn[:, j, :], self.x_res[:, TB * g + j, :], self.mean_var[:, j, 0:1],
                              self.rstd[:, j:j + 1], ALU.subtract, ALU.mult).then_inc(self.xn_ready, 1)

    def tensor_turn(self, pe, nth):
        for j in range(TB):
            pe.wait_ge(self.xn_ready, TB * nth + j + 1)
            if nth > 0:
                pe.wait_ge(self.lo_ready, TB * (nth - 1) + j + 1)
            for k in range(KD):
                ins = pe.transpose(self.banks[j][:, k * P:(k + 1) * P], self.xn[:, j, k * P:(k + 1) * P],
                                   self.ident[:, :])
            ins.then_inc(self.turned, 1)

    def scalar_hi(self, act, nth, xT_hi, slot):
        for j in range(TB):
            act.wait_ge(self.turned, TB * nth + j + 1)
            c = (TB * slot + j) * P
            act.activation(xT_hi[:, :, c:c + P], self.banks[j].rearrange("p (k t) -> p k t", k=KD),
                           ACT.Copy).then_inc(self.hi_ready, 1)

    def scalar_all(self, act, xT_hi):
        self.scalar_root(act, 0)
        for n in range(B):
            if n + 1 < B:
                self.scalar_root(act, n + 1)
            self.scalar_hi(act, n, xT_hi, n)

    def vector_lo(self, dve, nth, xT_hi, xT_lo, slot):
        for j in range(TB):
            dve.wait_ge(self.hi_ready, TB * nth + j + 1)
            c = (TB * slot + j) * P
            dve.tensor_tensor(xT_lo[:, :, c:c + P], self.banks[j].rearrange("p (k t) -> p k t", k=KD),
                              f32(xT_hi[:, :, c:c + P]), ALU.subtract).then_inc(self.lo_ready, 1)

    def vector_all(self, dve, groups, xT_hi, xT_lo):
        self.vector_stats(dve, groups[0])
        self.vector_norm(dve, groups[0], 0)
        for n in range(len(groups)):
            if n + 1 < len(groups):
                self.vector_stats(dve, groups[n + 1])
                self.vector_norm(dve, groups[n + 1], n + 1)
            self.vector_lo(dve, n, xT_hi, xT_lo, n)


def batch_product_phase(nc, x, ctx_in, bias, W2, consts, W2_scratch, x_res, ident, had):
    with ExitStack() as ctx:
        al = Alloc(nc, ctx, "a")
        raw = al.sb("ctx_raw", [NT, D])
        xn = al.sb("xn", [NT, D])
        scaled = al.sb("scaled", [2, TB, D])
        magic = al.sb("magic", [TB, D])
        lifted = al.sb("lifted", [TB, D])
        xq = al.sb("xq", [TB, D], BF16)
        cq = al.sb("cq", [2, TB, D], BF16)
        xqT = al.sb("xqT", [KD, S], BF16)
        bias_bc = al.sb("bias_bc", [B, D])
        ident_bf = al.sb("ident_bf", [P], BF16)
        had_raw = al.sb("had_raw", [P])
        stats = al.sb("stats", [TB, 6])
        mean_var = al.sb("mean_var", [TB, 2])
        var, root, rough = al.sb("var", [TB]), al.sb("root", [TB]), al.sb("rough", [TB])
        work, rstd = al.sb("work", [TB]), al.sb("rstd", [TB])
        amax_parts = al.sb("amax_parts", [2, B])
        amax = al.sb("amax", [2])
        amax_all = al.sb("amax_all", [2])
        inv_amax = al.sb("inv_amax", [2])
        scale = al.sb("scale", [2])
        unscale = al.sb("unscale", [2])
        w2a = al.sb("w2a", [FH])
        w2b = al.sb("w2b", [FH])
        banks = [al.ps(f"out{t}", [D]) for t in range(TB)]
        turn = [al.ps(f"turn{t}", [KD * P], BF16) for t in range(TB)]

        x_in = [al.sem(f"x_in{g}") for g in range(B)]
        c_in = [al.sem(f"c_in{g}") for g in range(B)]
        const_in = al.sem("const_in")
        bias_in = al.sem("bias_in")
        const_ready = al.sem("const_ready")
        chain = al.sem("chain")
        var_ready = al.sem("var_ready")
        root_ready = al.sem("root_ready")
        amax_ready = al.sem("amax_ready")
        amax_over = al.sem("amax_over")
        scale_ready = al.sem("scale_ready")
        scaled_ready = al.sem("scaled_ready")
        lifted_ready = al.sem("lifted_ready")
        quant_ready = al.sem("quant_ready")
        turned = al.sem("turned")
        turned_out = al.sem("turned_out")
        product = al.sem("product")
        added = al.sem("added")
        w2_in = al.sem("w2_in")
        w2_step = al.sem("w2_step")
        w2_out = al.sem("w2_out")

        block = ctx.enter_context(nc.Block())
        tiles = lambda a, g: a[g].rearrange("(t p) d -> p t d", p=P)

        @block.sync
        def _(sp):
            for g in range(B):
                sp.dma_start(x_res[:, TB * g:TB * g + TB, :], tiles(x, g)).then_inc(x_in[g], 16)
            sp.dma_start(ident[:, :], consts[0]).then_inc(const_in, 16)
            sp.dma_start(had_raw[:, :], consts[1]).then_inc(const_in, 16)
            for b in range(B):
                sp.dma_start(bias_bc[:, b, :], bias[b].partition_broadcast(P)).then_inc(bias_in, 16)
            for c in range(D // P):
                if c > 0:
                    sp.wait_ge(w2_out, 16 * c)
                sp.dma_start(w2a[:, :], W2[c * P:(c + 1) * P, :]).then_inc(w2_in, 16)
                sp.wait_ge(w2_step, 8 * (c + 1))
                sp.dma_start(W2_scratch[c * P:(c + 1) * P, :], w2a[:, :]).then_inc(w2_out, 16)
            sp.wait_ge(w2_out, 16 * (D // P))

        @block.gpsimd
        def _(pool):
            def butterflies(c):
                pool.wait_ge(w2_in, 16 * (c + 1))
                src, dst = w2a, w2b
                for s in range(4):
                    span = P << s
                    halves = lambda a, h: a[:, :].rearrange("p (n h s) -> p n h s", h=2, s=span)[:, :, h, :]
                    if s > 0:
                        pool.wait_ge(w2_step, 8 * c + 2 * s)
                    pool.tensor_tensor(halves(dst, 0), halves(src, 0), halves(src, 1), ALU.add).then_inc(w2_step, 1)
                    pool.tensor_tensor(halves(dst, 1), halves(src, 0), halves(src, 1),
                                       ALU.subtract).then_inc(w2_step, 1)
                    src, dst = dst, src

            pool.wait_ge(amax_ready, 1)
            nc.gpsimd.partition_all_reduce(amax_all[:, :], amax[:, :], P,
                                           bass.bass_isa.ReduceOp.max).then_inc(amax_over, 1)
            for c in range(D // P):
                butterflies(c)

        @block.scalar
        def _(act):
            for g in range(B):
                act.dma_start(raw[:, TB * g:TB * g + TB, :], tiles(ctx_in, g)).then_inc(c_in[g], 16)
            act.wait_ge(const_in, 32)
            act.activation(ident_bf[:, :], ident[:, :], ACT.Copy).then_inc(const_ready, 1)
            act.activation(had[:, :], had_raw[:, :], ACT.Copy).then_inc(const_ready, 1)
            for g in range(B):
                act.wait_ge(var_ready, g + 1)
                act.activation(root[:, :], var[:, :], ACT.Sqrt).then_inc(root_ready, 1)
            act.wait_ge(scale_ready, 1)

            def scale_group(n, src, which):
                if n >= 2:
                    act.wait_ge(lifted_ready, n - 1)
                act.activation(scaled[:, n % 2], src, ACT.Copy,
                               scale=scale[:, which:which + 1]).then_inc(scaled_ready, 1)

            scale_group(0, xn[:, 0:TB, :], 0)
            scale_group(1, raw[:, 0:TB, :], 1)
            for b in range(B):
                if b + 1 < B:
                    scale_group(2 * b + 2, xn[:, TB * b + TB:TB * b + 2 * TB, :], 0)
                    scale_group(2 * b + 3, raw[:, TB * b + TB:TB * b + 2 * TB, :], 1)
                if b > 0:
                    act.wait_ge(product, TB * b)
                for t in range(TB):
                    act.wait_ge(turned, TB * b + t + 1)
                    act.activation(xqT[:, :, t * P:(t + 1) * P], turn[t].rearrange("p (k t) -> p k t", k=KD),
                                   ACT.Copy).then_inc(turned_out, 1)

        @block.vector
        def _(dve):
            links = [0]

            def link(ins):
                links[0] += 1
                ins.then_inc(chain, 1)
                dve.wait_ge(chain, links[0])

            for g in range(B):
                dve.wait_ge(x_in[g], 16)
                for j in range(TB):
                    ins = dve.bn_stats(stats[:, j, :], x_res[:, TB * g + j, :])
                link(ins)
                for j in range(TB):
                    ins = dve.bn_aggr(mean_var[:, j, :], stats[:, j, :])
                link(ins)
                dve.tensor_scalar(var[:, :], mean_var[:, :, 1], EPS, None, ALU.add).then_inc(var_ready, 1)
                dve.wait_ge(root_ready, g + 1)
                inverse_root(dve, link, var[:, :], root[:, :], rough[:, :], work[:, :], rstd[:, :])
                for j in range(TB):
                    ins = dve.tensor_scalar(xn[:, TB * g + j, :], x_res[:, TB * g + j, :], mean_var[:, j, 0:1],
                                            rstd[:, j:j + 1], ALU.subtract, ALU.mult)
                link(ins)
                dve.tensor_reduce(amax_parts[:, 0, g:g + 1], xn[:, TB * g:TB * g + TB, :], AX.XY, ALU.max,
                                  apply_absolute_value=True)
                dve.wait_ge(c_in[g], 16)
                ins = dve.tensor_reduce(amax_parts[:, 1, g:g + 1], raw[:, TB * g:TB * g + TB, :], AX.XY, ALU.max,
                                        apply_absolute_value=True)
            link(ins)
            dve.tensor_reduce(amax[:, :], amax_parts[:, :, :], AX.X, ALU.max).then_inc(amax_ready, 1)
            dve.wait_ge(amax_over, 1)
            link(dve.tensor_scalar(amax[:, :], amax_all[:, :], FP8_AMAX_EPS, None, ALU.max))
            link(dve.reciprocal(inv_amax[:, :], amax[:, :]))
            dve.tensor_scalar(scale[:, :], inv_amax[:, :], FP8_MAX, None, ALU.mult).then_inc(scale_ready, 1)
            dve.wait_ge(scale_ready, 1)
            link(dve.tensor_tensor(unscale[:, 0:1], scale[:, 0:1], scale[:, 1:2], ALU.mult))
            link(dve.reciprocal(unscale[:, 1:2], unscale[:, 0:1]))

            def quantise(n, out):
                y = scaled[:, n % 2]
                dve.wait_ge(scaled_ready, n + 1)
                link(dve.tensor_scalar(magic[:, :, :].bitcast(U32), y.bitcast(U32), EXPONENT_BITS, None,
                                       ALU.bitwise_and))
                link(dve.tensor_scalar(magic[:, :, :], magic[:, :, :], FP8_MIN_NORMAL, ROUND_MAGIC, ALU.max, ALU.mult))
                dve.tensor_tensor(lifted[:, :, :], y, magic[:, :, :], ALU.add).then_inc(lifted_ready, 1)
                dve.wait_ge(lifted_ready, n + 1)
                link(dve.tensor_tensor(out, lifted[:, :, :], magic[:, :, :], ALU.subtract))
                dve.tensor_scalar(out, out, FP8_MAX, -FP8_MAX, ALU.min, ALU.max).then_inc(quant_ready, 1)

            for b in range(B + 1):
                if b < B:
                    if b > 0:
                        dve.wait_ge(turned, TB * b)
                    quantise(2 * b, xq[:, :, :])
                    if b > 1:
                        dve.wait_ge(product, TB * (b - 1))
                    quantise(2 * b + 1, cq[:, b % 2])
                if b == 0:
                    dve.wait_ge(bias_in, 16 * B)
                if b > 0:
                    for t in range(TB):
                        i = TB * (b - 1) + t
                        dve.wait_ge(product, i + 1)
                        link(dve.scalar_tensor_tensor(out=banks[t][:, :], in0=banks[t][:, :], scalar=unscale[:, 1:2],
                                                      in1=bias_bc[:, b - 1, :], op0=ALU.mult, op1=ALU.add))
                        dve.tensor_tensor(x_res[:, i, :], banks[t][:, :], x_res[:, i, :], ALU.add).then_inc(added, 1)

        @block.tensor
        def _(pe):
            pe.wait_ge(const_ready, 2)
            for b in range(B):
                pe.wait_ge(quant_ready, 2 * b + 1)
                for t in range(TB):
                    if b > 0:
                        pe.wait_ge(turned_out, TB * (b - 1) + t + 1)
                    for k in range(KD):
                        ins = pe.transpose(turn[t][:, k * P:(k + 1) * P], xq[:, t, k * P:(k + 1) * P], ident_bf[:, :])
                    ins.then_inc(turned, 1)
                pe.wait_ge(turned_out, TB * (b + 1))
                pe.wait_ge(quant_ready, 2 * b + 2)
                for t in range(TB):
                    if b > 0:
                        pe.wait_ge(added, TB * (b - 1) + t + 1)
                    for k in range(KD):
                        ins = pe.matmul(banks[t][:, :], xqT[:, k, t * P:(t + 1) * P], cq[:, b % 2, k, :],
                                        start=(k == 0), stop=(k == KD - 1))
                    ins.then_inc(product, 1)


def experts_phase(nc, Wsh_up, Wsh_down, Wrt_up, Wrt_down, W_router, x_res, ident):
    with ExitStack() as ctx:
        al = Alloc(nc, ctx, "e")
        xT_hi = al.sb("xT_hi", [KD, B * S], F32R)
        xT_lo = al.sb("xT_lo", [KD, B * S], F32R)
        up_raw = al.sb("up_raw", [2, KD, DE])
        up_hi = al.sb("up_hi", [2, KD, DE], F32R)
        up_lo = al.sb("up_lo", [2, KD, DE], F32R)
        down_raw = al.sb("down_raw", [2, KE, D])
        down_hi = al.sb("down_hi", [2, KE, D], F32R)
        down_lo = al.sb("down_lo", [2, KE, D], F32R)
        router_raw = al.sb("router_raw", [KD, E_RT])
        router_hi = al.sb("router_hi", [KD, E_RT], F32R)
        router_lo = al.sb("router_lo", [KD, E_RT], F32R)
        mid_hi = al.sb("mid_hi", [2, KE, S], F32R)
        mid_lo = al.sb("mid_lo", [2, KE, S], F32R)
        zeros = al.sb("zeros", [KD])
        gates = al.sb("gates", [NT, E_ALL])
        probs = al.sb("probs", [NT, E_RT])
        rest = al.sb("rest", [NT, E_RT])
        first = al.sb("first", [NT, E_RT])
        score = al.sb("score", [NT, E_RT])
        rank = al.sb("rank", [NT, E_RT])
        top = al.sb("top", [NT])
        inv = al.sb("inv", [NT])
        up_bank = [[al.ps(f"up{i}{k}", [S]) for k in range(KE)] for i in range(2)]
        down_bank = [al.ps(f"down{t}", [D]) for t in range(TB)]
        ln = LayerNorm(al, x_res, ident, down_bank)
        logits = up_bank[0][0][:, 0:NT * E_RT].rearrange("p (t e) -> p t e", e=E_RT)

        up_in = [al.sem(f"up_in{i}") for i in range(2)]
        down_in = [al.sem(f"down_in{i}") for i in range(2)]
        router_in = al.sem("router_in")
        router_hi_ready = al.sem("router_hi_ready")
        router_ready = al.sem("router_ready")
        up_hi_ready = al.sem("up_hi_ready")
        up_ready = al.sem("up_ready")
        down_hi_ready = al.sem("down_hi_ready")
        down_ready = al.sem("down_ready")
        routed = al.sem("routed")
        exp_ready = al.sem("exp_ready")
        gate_chain = al.sem("gate_chain")
        shifted = al.sem("shifted")
        zeros_ready = al.sem("zeros_ready")
        rank_ready = al.sem("rank_ready")
        up_done = al.sem("up_done")
        gelu_ready = al.sem("gelu_ready")
        mid_hi_ready = al.sem("mid_hi_ready")
        mid_ready = al.sem("mid_ready")
        down_done = al.sem("down_done")
        added = al.sem("added")

        block = ctx.enter_context(nc.Block())
        rows = lambda a: a.rearrange("(k p) n -> p k n", p=P)

        @block.sync
        def _(sp):
            sp.dma_start(router_raw[:, :, :], rows(W_router)).then_inc(router_in, 16)
            for i in range(E_SH):
                sp.dma_start(up_raw[:, i], rows(Wsh_up[i])).then_inc(up_in[i], 16)
                sp.dma_start(down_raw[:, i], rows(Wsh_down[i])).then_inc(down_in[i], 16)
            up_flat = Wrt_up.rearrange("(n i) (k p) m -> n i p k m", i=2, p=P)
            down_flat = Wrt_down.rearrange("(n i) (k p) m -> n i p k m", i=2, p=P)
            with sp.Fori(0, E_RT // 2) as n:
                for i in range(2):
                    sp.wait_ge(up_ready, 2 * n + (i + 1))
                    sp.dma_start(up_raw[:, i], up_flat[bass.ds(n, 1), i]).then_inc(up_in[i], 16)
                    sp.wait_ge(down_ready, 2 * n + (i + 1))
                    sp.dma_start(down_raw[:, i], down_flat[bass.ds(n, 1), i]).then_inc(down_in[i], 16)

        @block.gpsimd
        def _(pool):
            for e in range(E_RT):
                ins = pool.memset(rank[:, :, e:e + 1], float(E_RT - e))
            ins.then_inc(rank_ready, 1)
            pool.memset(zeros[:, :], 0.0).then_inc(zeros_ready, 1)
            pool.wait_ge(zeros_ready, 1)
            pool.wait_ge(router_in, 16)
            pool.tensor_copy(router_hi[:, :, :], router_raw[:, :, :]).then_inc(router_hi_ready, 1)
            pool.wait_ge(router_hi_ready, 1)
            pool.tensor_tensor(router_lo[:, :, :], router_raw[:, :, :], f32(router_hi[:, :, :]),
                               ALU.subtract).then_inc(router_ready, 1)

            zero = zeros[:, :].unsqueeze(2)

            def split(n, i, reused):
                pool.wait_ge(up_in[i], 16 * n + 16)
                if reused:
                    pool.wait_ge(up_done, (2 * n + i - 1) * (B * KE))
                pool.tensor_tensor(up_hi[:, i], up_raw[:, i], zero.to_broadcast([P, KD, DE]), ALU.add).then_inc(up_hi_ready, 1)
                pool.wait_ge(up_hi_ready, 2 * n + (i + 1))
                pool.tensor_tensor(up_lo[:, i], up_raw[:, i], f32(up_hi[:, i]), ALU.subtract).then_inc(up_ready, 1)
                pool.wait_ge(down_in[i], 16 * n + 16)
                if reused:
                    pool.wait_ge(down_done, (2 * n + i - 1) * (B * TB))
                pool.tensor_tensor(down_hi[:, i], down_raw[:, i], zero[:, 0:KE].to_broadcast([P, KE, D]), ALU.add).then_inc(down_hi_ready, 1)
                pool.wait_ge(down_hi_ready, 2 * n + (i + 1))
                pool.tensor_tensor(down_lo[:, i], down_raw[:, i], f32(down_hi[:, i]),
                                   ALU.subtract).then_inc(down_ready, 1)

            for i in range(2):
                split(0, i, False)
            with pool.Fori(1, E_ALL // 2) as n:
                for i in range(2):
                    split(n, i, True)

        @block.scalar
        def _(act):
            ln.scalar_all(act, xT_hi)
            act.wait_ge(shifted, 1)
            act.activation(probs[:, :, :], probs[:, :, :], ACT.Exp).then_inc(exp_ready, 1)

            def unit(n, i, b):
                u = 2 * n * B + (i * B + b)
                for k in range(KE):
                    act.wait_ge(up_done, u * KE + (k + 1))
                    bank = up_bank[b % 2][k]
                    act.activation(bank[:, :], bank[:, :], ACT.Gelu).then_inc(gelu_ready, 1)
                    act.wait_ge(gelu_ready, u * KE + (k + 1))
                    act.activation(mid_hi[:, b % 2, k], bank[:, :], ACT.Copy).then_inc(mid_hi_ready, 1)

            for i in range(2):
                for b in range(B):
                    unit(0, i, b)
            with act.Fori(1, E_ALL // 2) as n:
                for i in range(2):
                    for b in range(B):
                        unit(n, i, b)

        @block.vector
        def _(dve):
            ln.vector_all(dve, list(range(B)), xT_hi, xT_lo)
            links = [0]

            def link(ins):
                links[0] += 1
                ins.then_inc(gate_chain, 1)
                dve.wait_ge(gate_chain, links[0])

            wide = lambda a: a[:, :].unsqueeze(2).to_broadcast([P, NT, E_RT])
            link(dve.memset(gates[:, :, 0:E_SH], 1.0))
            dve.wait_ge(routed, 1)
            link(dve.tensor_reduce(top[:, :], logits, AX.X, ALU.max))
            dve.tensor_tensor(probs[:, :, :], logits, wide(top), ALU.subtract).then_inc(shifted, 1)
            dve.wait_ge(exp_ready, 1)
            link(dve.tensor_reduce(top[:, :], probs[:, :, :], AX.X, ALU.add))
            link(dve.reciprocal(inv[:, :], top[:, :]))
            link(dve.tensor_tensor(probs[:, :, :], probs[:, :, :], wide(inv), ALU.mult))

            def pick(values, out):
                link(dve.tensor_reduce(top[:, :], values, AX.X, ALU.max))
                link(dve.tensor_tensor(score[:, :, :], values, wide(top), ALU.is_equal))
                link(dve.tensor_tensor(score[:, :, :], score[:, :, :], rank[:, :, :], ALU.mult))
                link(dve.tensor_reduce(top[:, :], score[:, :, :], AX.X, ALU.max))
                link(dve.tensor_tensor(out, score[:, :, :], wide(top), ALU.is_equal))

            dve.wait_ge(rank_ready, 1)
            pick(probs[:, :, :], first[:, :, :])
            link(dve.scalar_tensor_tensor(out=rest[:, :, :], in0=first[:, :, :], scalar=-2.0, in1=probs[:, :, :],
                                          op0=ALU.mult, op1=ALU.add))
            pick(rest[:, :, :], rest[:, :, :])
            link(dve.tensor_tensor(first[:, :, :], first[:, :, :], rest[:, :, :], ALU.add))
            link(dve.tensor_tensor(gates[:, :, E_SH:E_ALL], first[:, :, :], probs[:, :, :], ALU.mult))

            def low(n, i, b):
                u = 2 * n * B + (i * B + b)
                for k in range(KE):
                    dve.wait_ge(mid_hi_ready, u * KE + (k + 1))
                    dve.tensor_tensor(mid_lo[:, b % 2, k], up_bank[b % 2][k][:, :], f32(mid_hi[:, b % 2, k]),
                                      ALU.subtract).then_inc(mid_ready, 1)

            def add(n, i, b):
                u = 2 * n * B + (i * B + b)
                e = 2 * n + i
                for t in range(TB):
                    dve.wait_ge(down_done, u * TB + (t + 1))
                    x_tile = x_res[:, TB * b + t, :]
                    gate = gates[:, TB * b + t, bass.ds(e, 1)]
                    dve.scalar_tensor_tensor(out=x_tile, in0=down_bank[t][:, :], scalar=gate, in1=x_tile,
                                             op0=ALU.mult, op1=ALU.add).then_inc(added, 1)

            def body(n, last):
                for i in range(2):
                    for b in range(B):
                        if b + 1 < B:
                            low(n, i, b + 1)
                        elif i == 0:
                            low(n, 1, 0)
                        elif not last:
                            low(n + 1, 0, 0)
                        add(n, i, b)
            low(0, 0, 0)
            with dve.Fori(0, E_ALL // 2 - 1) as n:
                body(n, False)
            body(E_ALL // 2 - 1, True)

        @block.tensor
        def _(pe):
            for g in range(B):
                ln.tensor_turn(pe, g)
            pe.wait_ge(ln.lo_ready, NT)
            pe.wait_ge(router_ready, 1)
            for t in range(NT):
                cols = slice(t * P, (t + 1) * P)
                ins = three_pass(pe, logits[:, t, :], lambda k: xT_hi[:, k, cols], lambda k: xT_lo[:, k, cols],
                                 lambda k: router_hi[:, k, :], lambda k: router_lo[:, k, :], KD)
            ins.then_inc(routed, 1)
            pe.wait_ge(shifted, 1)

            def up(n, i, b, reused):
                u = 2 * n * B + (i * B + b)
                cols = slice(b * S, (b + 1) * S)
                if b == 0:
                    pe.wait_ge(up_ready, 2 * n + (i + 1))
                for k in range(KE):
                    if reused:
                        pe.wait_ge(mid_ready, (u - 2) * KE + (k + 1))
                    ks = slice(k * P, (k + 1) * P)
                    three_pass(pe, up_bank[b % 2][k][:, :], lambda c: up_hi[:, i, c, ks], lambda c: up_lo[:, i, c, ks],
                               lambda c: xT_hi[:, c, cols], lambda c: xT_lo[:, c, cols], KD).then_inc(up_done, 1)

            def down(n, i, b, reused):
                u = 2 * n * B + (i * B + b)
                if b == 0:
                    pe.wait_ge(down_ready, 2 * n + (i + 1))
                pe.wait_ge(mid_ready, (u + 1) * KE)
                for t in range(TB):
                    if reused:
                        pe.wait_ge(added, (u - 1) * TB + (t + 1))
                    ts = slice(t * P, (t + 1) * P)
                    three_pass(pe, down_bank[t][:, :], lambda k: mid_hi[:, b % 2, k, ts],
                               lambda k: mid_lo[:, b % 2, k, ts], lambda k: down_hi[:, i, k, :],
                               lambda k: down_lo[:, i, k, :], KE).then_inc(down_done, 1)

            def body(n, start, last):
                for i in range(2):
                    for b in range(B):
                        if b + 1 < B:
                            up(n, i, b + 1, not (start and i == 0 and b == 0))
                        elif i == 0:
                            up(n, 1, 0, True)
                        elif not last:
                            up(n + 1, 0, 0, True)
                        down(n, i, b, not (start and i == b == 0))

            up(0, 0, 0, False)
            body(0, True, False)
            with pe.Fori(1, E_ALL // 2 - 1) as n:
                body(n, False, False)
            body(E_ALL // 2 - 1, False, True)


def attention_phase(nc, ctx_in, Wq, Wk, Wv, Wo, x_res, ident):
    with ExitStack() as ctx:
        al = Alloc(nc, ctx, "t")
        W = PAIRS * S
        xT_hi = al.sb("xT_hi", [KD, W], F32R)
        xT_lo = al.sb("xT_lo", [KD, W], F32R)
        cT_hi = al.sb("cT_hi", [KD, W], F32R)
        cT_lo = al.sb("cT_lo", [KD, W], F32R)
        c_raw = al.sb("c_raw", [PAIRS, TB, D])
        names = ("q", "k", "v")
        w_raw = {n: al.sb(f"w{n}_raw", [KD, HD]) for n in names}
        w_hi = {n: al.sb(f"w{n}_hi", [KD, HD], F32R) for n in names}
        w_lo = {n: al.sb(f"w{n}_lo", [KD, HD], F32R) for n in names}
        w_raw["o"] = al.sb("wo_raw", [D])
        w_hi["o"] = al.sb("wo_hi", [D], F32R)
        w_lo["o"] = al.sb("wo_lo", [D], F32R)
        q_hi, q_lo = al.sb("q_hi", [S], F32R), al.sb("q_lo", [S], F32R)
        k_hi, k_lo = al.sb("k_hi", [S], F32R), al.sb("k_lo", [S], F32R)
        vT = al.sb("vT", [S])
        v_hi, v_lo = al.sb("v_hi", [TB, HD], F32R), al.sb("v_lo", [TB, HD], F32R)
        probs = al.sb("probs", [TB, S])
        pT_hi, pT_lo = al.sb("pT_hi", [TB, S], F32R), al.sb("pT_lo", [TB, S], F32R)
        o_hi, o_lo = al.sb("o_hi", [S], F32R), al.sb("o_lo", [S], F32R)
        zeros = al.sb("zeros", [KD])
        neg_max, total, inv = al.sb("neg_max", [TB]), al.sb("total", [TB]), al.sb("inv", [TB])
        score_bank = [al.ps(f"score{t}", [S]) for t in range(TB)]
        out_bank = [al.ps(f"out{t}", [D]) for t in range(2)]
        qv_bank = al.ps("qv", [S])
        ko_bank = al.ps("ko", [S])
        ln = LayerNorm(al, x_res, ident, score_bank)
        sem = al.sem
        c_in = [sem(f"c_in{i}") for i in range(PAIRS)]
        c_turned = sem("c_turned")
        c_hi_ready, c_lo_ready = sem("c_hi_ready"), sem("c_lo_ready")
        zeros_ready = sem("zeros_ready")
        w_in = {n: sem(f"w{n}_in") for n in "qkvo"}
        w_hi_ready = {n: sem(f"w{n}_hi_ready") for n in "qkvo"}
        w_ready = {n: sem(f"w{n}_ready") for n in "qkvo"}
        q_done, k_done, v_done = sem("q_done"), sem("k_done"), sem("v_done")
        q_hi_ready, k_hi_ready = sem("q_hi_ready"), sem("k_hi_ready")
        q_ready, k_ready = sem("q_ready"), sem("k_ready")
        vT_ready = sem("vT_ready")
        v_turned = sem("v_turned")
        v_hi_ready, v_ready = sem("v_hi_ready"), sem("v_ready")
        scored = sem("scored")
        max_ready = sem("max_ready")
        exp_ready = sem("exp_ready")
        inv_ready = sem("inv_ready")
        probs_ready = sem("probs_ready")
        p_turned = sem("p_turned")
        p_hi_ready, p_ready = sem("p_hi_ready"), sem("p_ready")
        o_done = sem("o_done")
        o_hi_ready, o_ready = sem("o_hi_ready"), sem("o_ready")
        out_done = sem("out_done")
        added = sem("added")
        block = ctx.enter_context(nc.Block())

        heads_in = {"q": Wq, "k": Wk, "v": Wv}
        UNITS = H * 2
        SCALE = float(HD) ** -0.5
        fourths = lambda bank: bank[:, :].rearrange("p (k t) -> p k t", k=KD)


        @block.sync
        def _(sp):
            def load(r, h, wait):
                for n in "qkv":
                    if wait:
                        sp.wait_ge(w_ready[n], H * r + h)
                    src = heads_in[n].rearrange("(k p) (h c) -> h p k c", p=P, c=HD)
                    sp.dma_start(w_raw[n][:, :, :], src[h] if isinstance(h, int) else src[bass.ds(h, 1)]
                                 ).then_inc(w_in[n], 16)
                if wait:
                    sp.wait_ge(w_ready["o"], H * r + h)
                src = Wo.rearrange("(h p) n -> h p n", p=P)
                sp.dma_start(w_raw["o"][:, :], src[h] if isinstance(h, int) else src[bass.ds(h, 1)]
                             ).then_inc(w_in["o"], 16)

            for r in range(PAIRS):
                for i in range(2):
                    if r > 0:
                        sp.wait_ge(c_turned, 2 * TB * (r - 1) + TB * (i + 1))
                    sp.dma_start(c_raw[:, i], ctx_in[2 * r + i].rearrange("(t p) d -> p t d", p=P)).then_inc(c_in[i], 16)
                load(r, 0, r > 0)
                with sp.Fori(1, H) as h:
                    load(r, h, True)

        @block.gpsimd
        def _(pool):
            def split(n, r, h, last_use):
                zero = zeros[:, 0:1].to_broadcast([P, D]) if n == "o" else zeros[:, :].unsqueeze(2).to_broadcast([P, KD, HD])
                pool.wait_ge(w_in[n], (H * r + h + 1) * 16)
                if last_use is not None:
                    pool.wait_ge(*last_use)
                pool.tensor_tensor(w_hi[n][:], w_raw[n][:], zero, ALU.add).then_inc(w_hi_ready[n], 1)
                pool.wait_ge(w_hi_ready[n], H * r + h + 1)
                pool.tensor_tensor(w_lo[n][:], w_raw[n][:], f32(w_hi[n][:]), ALU.subtract).then_inc(w_ready[n], 1)

            def split_all(r, h, first):
                units_before = UNITS * r + h * 2
                for n, done in (("q", q_done), ("k", k_done), ("v", v_done)):
                    split(n, r, h, None if first else (done, units_before))
                split("o", r, h, None if first else (out_done, units_before * TB))

            pool.memset(zeros[:, :], 0.0).then_inc(zeros_ready, 1)
            pool.wait_ge(zeros_ready, 1)
            for r in range(PAIRS):
                split_all(r, 0, r == 0)
                with pool.Fori(1, H) as h:
                    split_all(r, h, False)

        @block.scalar
        def _(act):
            def project(r, u):
                n = UNITS * r + u
                act.wait_ge(q_done, n + 1)
                act.activation(q_hi[:, :], qv_bank[:, :], ACT.Copy, scale=SCALE).then_inc(q_hi_ready, 1)
                act.wait_ge(k_done, n + 1)
                act.activation(k_hi[:, :], ko_bank[:, :], ACT.Copy).then_inc(k_hi_ready, 1)

            def values(r, u):
                act.wait_ge(v_done, UNITS * r + u + 1)
                act.activation(vT[:, :], qv_bank[:, :], ACT.Copy).then_inc(vT_ready, 1)

            def values_hi(r, u):
                act.wait_ge(v_turned, UNITS * r + u + 1)
                act.activation(v_hi[:, :, :], out_bank[0][:, :].rearrange("p (t d) -> p t d", t=TB),
                               ACT.Copy).then_inc(v_hi_ready, 1)

            def unit(r, u, last):
                n = UNITS * r + u
                for t in range(TB):
                    act.wait_ge(max_ready, n * TB + (t + 1))
                    act.activation(probs[:, t, :], score_bank[t][:, :], ACT.Exp, bias=neg_max[:, t:t + 1],
                                   accum_out=total[:, t:t + 1]).then_inc(exp_ready, 1)
                act.wait_ge(inv_ready, n + 1)
                for t in range(TB):
                    act.activation(probs[:, t, :], probs[:, t, :], ACT.Copy,
                                   scale=inv[:, t:t + 1]).then_inc(probs_ready, 1)
                if not last:
                    project(r, u + 1)
                for t in range(TB):
                    act.wait_ge(p_turned, n * TB + (t + 1))
                    act.activation(pT_hi[:, :, t * P:(t + 1) * P], fourths(score_bank[t]),
                                   ACT.Copy).then_inc(p_hi_ready, 1)
                if not last:
                    values(r, u + 1)
                act.wait_ge(o_done, n + 1)
                act.activation(o_hi[:, :], ko_bank[:, :], ACT.Copy).then_inc(o_hi_ready, 1)
                if not last:
                    values_hi(r, u + 1)

            for r in range(PAIRS):
                for i in range(2):
                    ln.scalar_root(act, 2 * r + i)
                    ln.scalar_hi(act, 2 * r + i, xT_hi, i)
                for i in range(2):
                    for t in range(TB):
                        act.wait_ge(c_turned, 2 * TB * r + TB * i + t + 1)
                        c = (TB * i + t) * P
                        act.activation(cT_hi[:, :, c:c + P], fourths(score_bank[t]), ACT.Copy).then_inc(c_hi_ready, 1)
                project(r, 0)
                values(r, 0)
                values_hi(r, 0)
                with act.Fori(0, H - 1) as h:
                    unit(r, 2 * h, False)
                    unit(r, 2 * h + 1, False)
                unit(r, UNITS - 2, False)
                unit(r, UNITS - 1, True)

        @block.vector
        def _(dve):
            def project(r, u):
                n = UNITS * r + u
                dve.wait_ge(q_hi_ready, n + 1)
                dve.scalar_tensor_tensor(out=q_lo[:, :], in0=qv_bank[:, :], scalar=SCALE, in1=f32(q_hi[:, :]),
                                         op0=ALU.mult, op1=ALU.subtract).then_inc(q_ready, 1)
                dve.wait_ge(k_hi_ready, n + 1)
                dve.tensor_tensor(k_lo[:, :], ko_bank[:, :], f32(k_hi[:, :]), ALU.subtract).then_inc(k_ready, 1)

            def values_lo(r, u):
                dve.wait_ge(v_hi_ready, UNITS * r + u + 1)
                dve.tensor_tensor(v_lo[:, :, :], out_bank[0][:, :].rearrange("p (t d) -> p t d", t=TB),
                                  f32(v_hi[:, :, :]), ALU.subtract).then_inc(v_ready, 1)

            def add(r, u, b, t):
                dve.wait_ge(out_done, (UNITS * r + u) * TB + (t + 1))
                x_tile = x_res[:, TB * (2 * r + b) + t, :]
                dve.tensor_tensor(x_tile, out_bank[t % 2][:, :], x_tile, ALU.add).then_inc(added, 1)

            def unit(r, u, b, first, last):
                n = UNITS * r + u
                for t in range(TB):
                    dve.wait_ge(scored, n * TB + (t + 1))
                    dve.tensor_reduce(neg_max[:, t:t + 1], score_bank[t][:, :], AX.X, ALU.max,
                                      negate=True).then_inc(max_ready, 1)
                if not first:
                    add(r, u - 1, 1 - b, 0)
                    add(r, u - 1, 1 - b, 1)
                dve.wait_ge(exp_ready, (n + 1) * TB)
                dve.reciprocal(inv[:, :], total[:, :]).then_inc(inv_ready, 1)
                if not first:
                    add(r, u - 1, 1 - b, 2)
                    add(r, u - 1, 1 - b, 3)
                if not last:
                    project(r, u + 1)
                for t in range(TB):
                    dve.wait_ge(p_hi_ready, n * TB + (t + 1))
                    dve.tensor_tensor(pT_lo[:, :, t * P:(t + 1) * P], fourths(score_bank[t]),
                                      f32(pT_hi[:, :, t * P:(t + 1) * P]), ALU.subtract).then_inc(p_ready, 1)
                dve.wait_ge(o_hi_ready, n + 1)
                dve.tensor_tensor(o_lo[:, :], ko_bank[:, :], f32(o_hi[:, :]), ALU.subtract).then_inc(o_ready, 1)
                if not last:
                    values_lo(r, u + 1)

            for r in range(PAIRS):
                for i in range(2):
                    g = 2 * r + i
                    ln.vector_stats(dve, g)
                    ln.vector_norm(dve, g, g)
                    ln.vector_lo(dve, g, xT_hi, xT_lo, i)
                for i in range(2):
                    for t in range(TB):
                        dve.wait_ge(c_hi_ready, 2 * TB * r + TB * i + t + 1)
                        c = (TB * i + t) * P
                        dve.tensor_tensor(cT_lo[:, :, c:c + P], fourths(score_bank[t]), f32(cT_hi[:, :, c:c + P]),
                                          ALU.subtract).then_inc(c_lo_ready, 1)
                project(r, 0)
                values_lo(r, 0)
                unit(r, 0, 0, True, False)
                unit(r, 1, 1, False, False)
                with dve.Fori(1, H - 1) as h:
                    unit(r, 2 * h, 0, False, False)
                    unit(r, 2 * h + 1, 1, False, False)
                unit(r, UNITS - 2, 0, False, False)
                unit(r, UNITS - 1, 1, False, True)
                for t in range(TB):
                    add(r, UNITS - 1, 1, t)

        @block.tensor
        def _(pe):
            def project(name, r, u, h, b, bank, src_hi, src_lo, done):
                if b == 0:
                    pe.wait_ge(w_ready[name], H * r + h + 1)
                cols = slice(b * S, (b + 1) * S)
                three_pass(pe, bank[:, :], lambda k: w_hi[name][:, k, :], lambda k: w_lo[name][:, k, :],
                           lambda k: src_hi[:, k, cols], lambda k: src_lo[:, k, cols], KD).then_inc(done, 1)

            def project_q(r, u, h, b):
                n = UNITS * r + u
                if not (isinstance(u, int) and n == 0):
                    pe.wait_ge(v_turned, n)
                project("q", r, u, h, b, qv_bank, xT_hi, xT_lo, q_done)

            def project_k(r, u, h, b):
                n = UNITS * r + u
                if not (isinstance(u, int) and u == 0 and r == 0):
                    if isinstance(u, int) and u == 0:
                        pe.wait_ge(o_ready, UNITS * r)
                    elif not (isinstance(u, int) and n == 1):
                        pe.wait_ge(o_ready, n - 1)
                project("k", r, u, h, b, ko_bank, cT_hi, cT_lo, k_done)

            def project_v(r, u, h, b):
                pe.wait_ge(q_ready, UNITS * r + u + 1)
                project("v", r, u, h, b, qv_bank, cT_hi, cT_lo, v_done)

            def turn_v(r, u):
                n = UNITS * r + u
                pe.wait_ge(vT_ready, n + 1)
                for t in range(TB):
                    ins = pe.transpose(out_bank[0][:, t * HD:(t + 1) * HD], vT[:, t * P:(t + 1) * P], ident[:, :])
                ins.then_inc(v_turned, 1)

            def output(r, u, h, b):
                n = UNITS * r + u
                if b == 0:
                    pe.wait_ge(w_ready["o"], H * r + h + 1)
                pe.wait_ge(o_ready, n + 1)
                for t in range(TB):
                    if t >= 2:
                        pe.wait_ge(added, n * TB + (t - 1))
                    elif t == 1 and not (isinstance(n, int) and n == 0):
                        pe.wait_ge(added, n * TB)
                    three_pass(pe, out_bank[t % 2][:, :], lambda k: o_hi[:, t * P:(t + 1) * P],
                               lambda k: o_lo[:, t * P:(t + 1) * P], lambda k: w_hi["o"][:, :],
                               lambda k: w_lo["o"][:, :], 1).then_inc(out_done, 1)

            def unit(r, u, h, b, first, last):
                n = UNITS * r + u
                pe.wait_ge(q_ready, n + 1)
                pe.wait_ge(k_ready, n + 1)
                if not first:
                    pe.wait_ge(p_ready, n * TB)
                for t in range(TB):
                    three_pass(pe, score_bank[t][:, :], lambda k: q_hi[:, t * P:(t + 1) * P],
                               lambda k: q_lo[:, t * P:(t + 1) * P], lambda k: k_hi[:, :], lambda k: k_lo[:, :],
                               1).then_inc(scored, 1)
                pe.wait_ge(v_ready, n + 1)
                if not first:
                    output(r, u - 1, h if b == 1 else h - 1, 1 - b)
                nh, nb = (h, 1) if b == 0 else (h + 1, 0)
                if not last:
                    project_q(r, u + 1, nh, nb)
                    project_k(r, u + 1, nh, nb)
                for t in range(TB):
                    pe.wait_ge(probs_ready, n * TB + (t + 1))
                    for k in range(TB):
                        ins = pe.transpose(score_bank[t][:, k * P:(k + 1) * P], probs[:, t, k * P:(k + 1) * P],
                                           ident[:, :])
                    ins.then_inc(p_turned, 1)
                if not last:
                    project_v(r, u + 1, nh, nb)
                    pe.wait_ge(k_ready, n + 2)
                pe.wait_ge(p_ready, (n + 1) * TB)
                three_pass(pe, ko_bank[:, :], lambda k: v_hi[:, k, :], lambda k: v_lo[:, k, :],
                           lambda k: pT_hi[:, k, :], lambda k: pT_lo[:, k, :], TB).then_inc(o_done, 1)
                if not last:
                    if not first:
                        pe.wait_ge(added, n * TB - 1)
                    turn_v(r, u + 1)

            for r in range(PAIRS):
                if r > 0:
                    pe.wait_ge(p_ready, UNITS * r * TB)
                for i in range(2):
                    ln.tensor_turn(pe, 2 * r + i)
                pe.wait_ge(ln.lo_ready, (2 * r + 2) * TB)
                for i in range(2):
                    pe.wait_ge(c_in[i], 16 * (r + 1))
                    for t in range(TB):
                        if i > 0:
                            pe.wait_ge(c_lo_ready, 2 * TB * r + TB * (i - 1) + t + 1)
                        for k in range(KD):
                            ins = pe.transpose(score_bank[t][:, k * P:(k + 1) * P], c_raw[:, i, t, k * P:(k + 1) * P],
                                               ident[:, :])
                        ins.then_inc(c_turned, 1)
                pe.wait_ge(c_lo_ready, 2 * TB * (r + 1))
                project_q(r, 0, 0, 0)
                project_k(r, 0, 0, 0)
                project_v(r, 0, 0, 0)
                if r > 0:
                    pe.wait_ge(added, UNITS * r * TB)
                turn_v(r, 0)
                unit(r, 0, 0, 0, True, False)
                unit(r, 1, 0, 1, False, False)
                with pe.Fori(1, H - 1) as h:
                    unit(r, 2 * h, h, 0, False, False)
                    unit(r, 2 * h + 1, h, 1, False, False)
                unit(r, UNITS - 2, H - 1, 0, False, False)
                unit(r, UNITS - 1, H - 1, 1, False, True)
                output(r, UNITS - 1, H - 1, 1)


def hadamard_ffn_phase(nc, W1, W3, W2_scratch, x_res, ident, had, out):
    with ExitStack() as ctx:
        al = Alloc(nc, ctx, "f")
        xT_hi = al.sb("xT_hi", [KD, B * S], F32R)
        xT_lo = al.sb("xT_lo", [KD, B * S], F32R)
        raw = [al.sb("w1_raw", [KG, D]), al.sb("w3_raw", [KG, D])]
        w2_raw = al.sb("w2_raw", [KD, GH])
        up_hi = [[al.sb(f"w{n}_hi{i}", [KD, GH], F32R) for n in (1, 3)] for i in range(2)]
        up_lo = [[al.sb(f"w{n}_lo{i}", [KD, GH], F32R) for n in (1, 3)] for i in range(2)]
        w2T_hi, w2T_lo = al.sb("w2T_hi", [KG, D], F32R), al.sb("w2T_lo", [KG, D], F32R)
        down_hi, down_lo = al.sb("down_hi", [2, KG, D], F32R), al.sb("down_lo", [2, KG, D], F32R)
        silu = al.sb("silu", [KG, S])
        mid_hi, mid_lo = al.sb("mid_hi", [2, KG, S], F32R), al.sb("mid_lo", [2, KG, S], F32R)
        gate_bank = [al.ps(f"gate{k}", [S]) for k in range(KG)]
        lin_bank = [al.ps(f"lin{k}", [S]) for k in range(KG)]
        down_bank = [al.ps(f"down{t}", [D]) for t in range(TB)]
        ln = LayerNorm(al, x_res, ident, down_bank)
        sem = al.sem
        w1_in, w3_in, w2_in = sem("w1_in"), sem("w3_in"), sem("w2_in")
        prep_turned = sem("prep_turned")
        prep_hi_ready = sem("prep_hi_ready")
        prep_ready = sem("prep_ready")
        gate_done, lin_done = sem("gate_done"), sem("lin_done")
        silu_ready = sem("silu_ready")
        mid_done = sem("mid_done")
        mid_hi_ready = sem("mid_hi_ready")
        mid_ready = sem("mid_ready")
        down_done = sem("down_done")
        added = sem("added")
        stored = sem("stored")
        block = ctx.enter_context(nc.Block())

        PREP = 4 * KG
        FWHT_SCALE = float(FH) ** -0.5
        fourths = lambda bank: bank[:, :].rearrange("p (k t) -> p k t", k=KD)

        def prep_dst(i, j, part):
            kind, k = j // KG, j % KG
            if kind < 2:
                return (up_hi, up_lo)[part][i][kind][:, :, k * P:(k + 1) * P]
            if kind == 2:
                return (w2T_hi, w2T_lo)[part][:, k, :]
            return (down_hi, down_lo)[part][:, i, k, :]


        @block.sync
        def _(sp):
            src1 = W1.rearrange("(g k p) d -> g p k d", k=KG, p=P)
            src3 = W3.rearrange("(g k p) d -> g p k d", k=KG, p=P)
            src2 = W2_scratch.rearrange("(c p) (g n) -> g p c n", p=P, n=GH)

            def load(g, first):
                pick = (lambda a: a[g]) if first else (lambda a: a[bass.ds(g, 1)])
                if not first:
                    sp.wait_ge(prep_turned, (g - 1) * PREP + KG)
                sp.dma_start(raw[0][:, :, :], pick(src1)).then_inc(w1_in, 16)
                if not first:
                    sp.wait_ge(prep_turned, (g - 1) * PREP + 2 * KG)
                sp.dma_start(raw[1][:, :, :], pick(src3)).then_inc(w3_in, 16)
                if not first:
                    sp.wait_ge(prep_turned, (g - 1) * PREP + 3 * KG)
                sp.dma_start(w2_raw[:, :, :], pick(src2)).then_inc(w2_in, 16)

            load(0, True)
            with sp.Fori(1, NG) as g:
                load(g, False)
            for b in range(B):
                sp.wait_ge(added, (NG - 1) * B * TB + (b + 1) * TB)
                sp.dma_start(out[b].rearrange("(t p) d -> p t d", p=P), x_res[:, TB * b:TB * b + TB, :]
                             ).then_inc(stored, 16)
            sp.wait_ge(stored, 16 * B)


        @block.scalar
        def _(act):
            def prepare(g, i, j):
                act.wait_ge(prep_turned, g * PREP + (j + 1))
                bank = down_bank[j % KG]
                if j < 2 * KG:
                    act.activation(prep_dst(i, j, 0), fourths(bank), ACT.Copy).then_inc(prep_hi_ready, 1)
                else:
                    act.activation(prep_dst(i, j, 0), bank[:, :], ACT.Copy,
                                   scale=FWHT_SCALE if j >= 3 * KG else 1.0).then_inc(prep_hi_ready, 1)

            def unit(u, b):
                for k in range(KG):
                    act.wait_ge(gate_done, u * KG + (k + 1))
                    if not (isinstance(u, int) and u == 0):
                        act.wait_ge(mid_done, (u - 1) * KG + (k + 1))
                    act.activation(silu[:, k, :], gate_bank[k][:, :], ACT.Silu).then_inc(silu_ready, 1)
                for k in range(KG):
                    act.wait_ge(mid_done, u * KG + (k + 1))
                    act.activation(mid_hi[:, b % 2, k, :], lin_bank[k][:, :], ACT.Copy).then_inc(mid_hi_ready, 1)

            def group(g, i, last):
                for b in range(B):
                    if not (last and b == B - 1):
                        unit(g * B + (b + 1), b + 1)
                    if not last:
                        prepare(g + 1, 1 - i, 2 * b)
                        prepare(g + 1, 1 - i, 2 * b + 1)

            ln.scalar_all(act, xT_hi)
            for j in range(PREP):
                prepare(0, 0, j)
            unit(0, 0)
            with act.Fori(0, NG // 2 - 1) as n:
                group(2 * n, 0, False)
                group(2 * n + 1, 1, False)
            group(NG - 2, 0, False)
            group(NG - 1, 1, True)

        @block.vector
        def _(dve):
            def prepare(g, i, j):
                dve.wait_ge(prep_hi_ready, g * PREP + (j + 1))
                bank = down_bank[j % KG]
                hi, lo = f32(prep_dst(i, j, 0)), prep_dst(i, j, 1)
                if j < 2 * KG:
                    dve.tensor_tensor(lo, fourths(bank), hi, ALU.subtract).then_inc(prep_ready, 1)
                else:
                    dve.scalar_tensor_tensor(out=lo, in0=bank[:, :], scalar=FWHT_SCALE if j >= 3 * KG else 1.0,
                                             in1=hi, op0=ALU.mult, op1=ALU.subtract).then_inc(prep_ready, 1)

            def unit(u, b):
                for k in range(KG):
                    dve.wait_ge(silu_ready, u * KG + (k + 1))
                    dve.wait_ge(lin_done, u * KG + (k + 1))
                    dve.tensor_tensor(lin_bank[k][:, :], lin_bank[k][:, :], silu[:, k, :],
                                      ALU.mult).then_inc(mid_done, 1)
                for k in range(KG):
                    dve.wait_ge(mid_hi_ready, u * KG + (k + 1))
                    dve.tensor_tensor(mid_lo[:, b % 2, k, :], lin_bank[k][:, :], f32(mid_hi[:, b % 2, k, :]),
                                      ALU.subtract).then_inc(mid_ready, 1)

            def group(g, i, last):
                for b in range(B):
                    if not (last and b == B - 1):
                        unit(g * B + (b + 1), b + 1)
                    for t in range(TB):
                        dve.wait_ge(down_done, g * (B * TB) + (b * TB + t + 1))
                        x_tile = x_res[:, TB * b + t, :]
                        dve.tensor_tensor(x_tile, down_bank[t][:, :], x_tile, ALU.add).then_inc(added, 1)
                    if not last:
                        prepare(g + 1, 1 - i, 2 * b)
                        prepare(g + 1, 1 - i, 2 * b + 1)

            ln.vector_all(dve, list(range(B)), xT_hi, xT_lo)
            for j in range(PREP):
                prepare(0, 0, j)
            unit(0, 0)
            with dve.Fori(0, NG // 2 - 1) as n:
                group(2 * n, 0, False)
                group(2 * n + 1, 1, False)
            group(NG - 2, 0, False)
            group(NG - 1, 1, True)

        @block.tensor
        def _(pe):
            def prepare(g, i, j, unit_before):
                kind, k = j // KG, j % KG
                bank = down_bank[j % KG]
                if unit_before is not None:
                    pe.wait_ge(added, unit_before * TB + (k + 1))
                elif j >= KG:
                    pe.wait_ge(prep_ready, j - KG + 1)
                if kind < 2:
                    pe.wait_ge((w1_in, w3_in)[kind], (g + 1) * 16)
                    for c in range(KD):
                        ins = pe.transpose(bank[:, c * P:(c + 1) * P], raw[kind][:, k, c * P:(c + 1) * P], ident[:, :])
                elif kind == 2:
                    pe.wait_ge(w2_in, (g + 1) * 16)
                    for c in range(KD):
                        ins = pe.transpose(bank[:, c * P:(c + 1) * P], w2_raw[:, c, k * P:(k + 1) * P], ident[:, :])
                else:
                    pe.wait_ge(prep_ready, g * PREP + (2 * KG + k + 1))
                    pe.matmul(bank[:, :], had[:, :], w2T_hi[:, k, :], start=True, stop=False)
                    ins = pe.matmul(bank[:, :], had[:, :], w2T_lo[:, k, :], start=False, stop=True)
                ins.then_inc(prep_turned, 1)

            def up(u, g, i, b):
                cols = slice(b * S, (b + 1) * S)
                if b == 0:
                    pe.wait_ge(prep_ready, g * PREP + 2 * KG)
                for k in range(KG):
                    ks = slice(k * P, (k + 1) * P)
                    if not (isinstance(u, int) and u == 0):
                        pe.wait_ge(mid_ready, (u - 1) * KG + (k + 1))
                    for kind, bank, done in ((0, gate_bank[k], gate_done), (1, lin_bank[k], lin_done)):
                        three_pass(pe, bank[:, :], lambda c: up_hi[i][kind][:, c, ks],
                                   lambda c: up_lo[i][kind][:, c, ks], lambda c: xT_hi[:, c, cols],
                                   lambda c: xT_lo[:, c, cols], KD).then_inc(done, 1)

            def group(g, i, start, last):
                for b in range(B):
                    u = g * B + b
                    if b + 1 < B:
                        up(u + 1, g, i, b + 1)
                    elif not last:
                        up(u + 1, g + 1, 1 - i, 0)
                    if b == 0:
                        pe.wait_ge(prep_ready, (g + 1) * PREP)
                    pe.wait_ge(mid_ready, (u + 1) * KG)
                    for t in range(TB):
                        if t < KG and b > 0 and not last:
                            pe.wait_ge(prep_ready, (g + 1) * PREP + (2 * (b - 1) + t + 1))
                        if not (start and b == 0):
                            pe.wait_ge(added, (u - 1) * TB + (t + 1))
                        ts = slice(t * P, (t + 1) * P)
                        three_pass(pe, down_bank[t][:, :], lambda k: mid_hi[:, b % 2, k, ts],
                                   lambda k: mid_lo[:, b % 2, k, ts], lambda k: down_hi[:, i, k, :],
                                   lambda k: down_lo[:, i, k, :], KG).then_inc(down_done, 1)
                    if not last:
                        prepare(g + 1, 1 - i, 2 * b, u)
                        prepare(g + 1, 1 - i, 2 * b + 1, u)

            for g in range(B):
                ln.tensor_turn(pe, g)
            pe.wait_ge(ln.lo_ready, NT)
            for j in range(PREP):
                prepare(0, 0, j, None)
            up(0, 0, 0, 0)
            group(0, 0, True, False)
            group(1, 1, False, False)
            with pe.Fori(1, NG // 2 - 1) as n:
                group(2 * n, 0, False, False)
                group(2 * n + 1, 1, False, False)
            group(NG - 2, 0, False, False)
            group(NG - 1, 1, False, True)


def build(nc, x, ctx_in, bias, Wsh_up, Wsh_down, Wrt_up, Wrt_down, W_router, Wq, Wk, Wv, Wo, W1, W2, W3, consts, out):
    W2_scratch = nc.dram_tensor("W2_outer_hadamard", (D, FH), F32, kind="Internal").ap()
    with ExitStack() as ctx:
        x_res = ctx.enter_context(nc.sbuf_tensor("x_res", [P, NT, D], F32))
        ident = ctx.enter_context(nc.sbuf_tensor("ident", [P, P], F32))
        had = ctx.enter_context(nc.sbuf_tensor("had", [P, P], F32R))
        batch_product_phase(nc, x, ctx_in, bias, W2, consts, W2_scratch, x_res, ident, had)
        experts_phase(nc, Wsh_up, Wsh_down, Wrt_up, Wrt_down, W_router, x_res, ident)
        attention_phase(nc, ctx_in, Wq, Wk, Wv, Wo, x_res, ident)
        hadamard_ffn_phase(nc, W1, W3, W2_scratch, x_res, ident, had, out)


_INS = ["x", "ctx_2048", "mask_Bx1xS2_ff0", "L0_ffn_Wsh_up", "L0_ffn_Wsh_down", "L0_ffn_Wrt_up", "L0_ffn_Wrt_down",
        "L0_ffn_W_router", "L1_xattn_Wq", "L1_xattn_Wk", "L1_xattn_Wv", "L1_xattn_Wo", "L1_ffn_W1", "L1_ffn_W2",
        "L1_ffn_W3"]


def kernel(**inputs):
    import numpy as np
    import concourse.bacc as bacc
    from concourse import mybir as mb
    from concourse.bass_utils import run_bass_kernel_spmd

    hadamard = np.ones((1, 1), np.float32)
    while hadamard.shape[0] < 128:
        hadamard = np.block([[hadamard, hadamard], [hadamard, -hadamard]])
    consts = np.stack([np.eye(128, dtype=np.float32), hadamard.astype(np.float32)])

    nc = bacc.Bacc("TRN2", target_bir_lowering=False, num_devices=1)
    arrays, args = {}, []
    for name, a in [(n, inputs[n]) for n in _INS] + [("consts", consts)]:
        a = np.ascontiguousarray(a)
        arrays[f"in_{name}_dram"] = a
        args.append(nc.dram_tensor(f"in_{name}_dram", a.shape, mb.dt.from_np(a.dtype), kind="ExternalInput").ap())
    out = nc.dram_tensor("out_0_dram", (4, 512, 512), mb.dt.float32, kind="ExternalOutput").ap()
    build(nc, *args, out)
    r = run_bass_kernel_spmd(nc, [arrays], core_ids=[0])
    return r.results[0]["out_0_dram"]
```

```python
from contextlib import ExitStack

import concourse.bass as bass
from concourse import mybir

F32 = mybir.dt.float32
F32R = mybir.dt.float32r
BF16 = mybir.dt.bfloat16
U32 = mybir.dt.uint32
ALU = mybir.AluOpType
ACT = mybir.ActivationFunctionType
AX = mybir.AxisListType

P = 128
B, S, D = 4, 512, 512
KD = D // P
TB = S // P
NT = B * TB
EPS = 1e-5
RSQRT_BITS = 0x5F375A86

FP8_MAX = 448.0
FP8_AMAX_EPS = 1e-12
FP8_MIN_NORMAL = 2.0 ** -6
ROUND_MAGIC = 1.5 * 2.0 ** 20
EXPONENT_BITS = 0x7F800000

E_SH, E_RT, DE = 2, 16, 256
E_ALL = E_SH + E_RT
KE = DE // P
H, HD = 16, 128
PAIRS = B // 2
FH = 2048
GH = 256
KG = GH // P
NG = FH // GH


def three_pass(pe, out, w_hi, w_lo, x_hi, x_lo, k_tiles):
    for k in range(k_tiles):
        for j, (w, x) in enumerate(((w_hi, x_hi), (w_hi, x_lo), (w_lo, x_hi))):
            ins = pe.matmul(out, w(k), x(k), start=(k == 0 and j == 0), stop=(k == k_tiles - 1 and j == 2))
    return ins


def f32(ap):
    return ap.bitcast(F32)


class Alloc:

    def __init__(self, nc, ctx, tag):
        self.nc, self.ctx, self.tag = nc, ctx, tag

    def sb(self, name, shape, dt=F32):
        return self.ctx.enter_context(self.nc.sbuf_tensor(f"{self.tag}_{name}", [P] + shape, dt))

    def ps(self, name, shape, dt=F32):
        return self.ctx.enter_context(self.nc.psum_tensor(f"{self.tag}_{name}", [P] + shape, dt))

    def sem(self, name):
        return self.ctx.enter_context(self.nc.semaphore(f"{self.tag}_{name}"))


class RowStats:

    def __init__(self, nc, ctx, x_res):
        sb = lambda name, shape, dt=F32: ctx.enter_context(nc.sbuf_tensor(name, [P] + shape, dt))
        self.x_res = x_res
        self.raw = sb("row_stats", [NT, 6])
        self.mean_var = sb("mean_var", [NT, 2])
        self.rstd = sb("rstd", [NT])
        self.bits = sb("rstd_bits", [NT], U32)
        self.root = sb("rstd_root", [NT])
        self.work = sb("rstd_work", [NT])
        self.chain = ctx.enter_context(nc.semaphore("row_stats_chain"))
        self.links = 0

    def link(self, dve, ins):
        self.links += 1
        ins.then_inc(self.chain, 1)
        dve.wait_ge(self.chain, self.links)

    def read(self, dve, g):
        for j in range(TB * g, TB * (g + 1)):
            ins = dve.bn_stats(self.raw[:, j, :], self.x_res[:, j, :])
        self.link(dve, ins)

    def finish(self, dve, g, n):
        link = lambda ins: self.link(dve, ins)
        tiles = slice(TB * g, TB * (g + n))
        bits, root, work = self.bits[:, tiles], self.root[:, tiles], self.work[:, tiles]
        for j in range(TB * g, TB * (g + n)):
            ins = dve.bn_aggr(self.mean_var[:, j, :], self.raw[:, j, :])
        link(ins)
        var = self.mean_var[:, tiles, 1]
        link(dve.tensor_scalar(var, var, EPS, None, ALU.add))
        link(dve.tensor_scalar(bits, var.bitcast(U32), 1, None, ALU.logical_shift_right))
        link(dve.tensor_scalar(root.bitcast(U32), bits, -1.0, float(RSQRT_BITS), ALU.mult, ALU.add))
        for step in range(4):
            out = self.rstd[:, tiles] if step == 3 else root
            link(dve.scalar_tensor_tensor(out=work, in0=root, scalar=-0.5, in1=root, op0=ALU.mult, op1=ALU.mult))
            link(dve.tensor_tensor(work, work, var, ALU.mult))
            link(dve.scalar_tensor_tensor(out=out, in0=work, scalar=1.5, in1=root, op0=ALU.add, op1=ALU.mult))

    def compute(self, dve, g):
        self.read(dve, g)
        self.finish(dve, g, 1)


class LayerNorm:

    def __init__(self, al, stats, ident, banks, later_banks=None):
        self.stats, self.ident, self.banks, self.later_banks = stats, ident, banks, later_banks or banks
        self.xn = al.sb("ln_xn", [TB, D])
        self.xn_ready = al.sem("ln_xn_ready")
        self.turned = al.sem("ln_turned")
        self.hi_ready = al.sem("ln_hi_ready")
        self.lo_ready = al.sem("ln_lo_ready")

    def bank(self, nth, j):
        banks = self.later_banks if nth else self.banks
        return banks[j % len(banks)]

    def vector_norm(self, dve, g, nth):
        if nth > 0:
            dve.wait_ge(self.turned, TB * nth)
        for j in range(TB):
            i = TB * g + j
            dve.tensor_scalar(self.xn[:, j, :], self.stats.x_res[:, i, :], self.stats.mean_var[:, i, 0:1],
                              self.stats.rstd[:, i:i + 1], ALU.subtract, ALU.mult).then_inc(self.xn_ready, 1)

    def tensor_turn(self, pe, nth):
        for j in range(TB):
            n = TB * nth + j
            pe.wait_ge(self.xn_ready, n + 1)
            size = len(self.later_banks if nth else self.banks)
            if j >= size:
                pe.wait_ge(self.lo_ready, n - size + 1)
            for k in range(KD):
                ins = pe.transpose(self.bank(nth, j)[:, k * P:(k + 1) * P], self.xn[:, j, k * P:(k + 1) * P],
                                   self.ident[:, :])
            ins.then_inc(self.turned, 1)

    def scalar_hi(self, act, nth, xT_hi, slot):
        for j in range(TB):
            act.wait_ge(self.turned, TB * nth + j + 1)
            c = (TB * slot + j) * P
            act.activation(xT_hi[:, :, c:c + P], self.bank(nth, j)[:, :].rearrange("p (k t) -> p k t", k=KD),
                           ACT.Copy).then_inc(self.hi_ready, 1)

    def vector_lo(self, dve, nth, xT_hi, xT_lo, slot):
        for j in range(TB):
            dve.wait_ge(self.hi_ready, TB * nth + j + 1)
            c = (TB * slot + j) * P
            dve.tensor_tensor(xT_lo[:, :, c:c + P], self.bank(nth, j)[:, :].rearrange("p (k t) -> p k t", k=KD),
                              f32(xT_hi[:, :, c:c + P]), ALU.subtract).then_inc(self.lo_ready, 1)


def batch_product_phase(nc, x, ctx_in, bias, consts, x_res, ident, had, stats):
    with ExitStack() as ctx:
        al = Alloc(nc, ctx, "a")
        raw = al.sb("ctx_raw", [NT, D])
        xn = al.sb("xn", [NT, D])
        scaled = al.sb("scaled", [2, TB, D])
        magic = al.sb("magic", [TB, D])
        lifted = al.sb("lifted", [TB, D])
        xq = al.sb("xq", [TB, D], BF16)
        cq = al.sb("cq", [2, TB, D], BF16)
        xqT = al.sb("xqT", [KD, S], BF16)
        bias_bc = al.sb("bias_bc", [B, D])
        ident_bf = al.sb("ident_bf", [P], BF16)
        had_raw = al.sb("had_raw", [P])
        amax_parts = al.sb("amax_parts", [2, B])
        amax = al.sb("amax", [2])
        amax_all = al.sb("amax_all", [2])
        inv_amax = al.sb("inv_amax", [2])
        scale = al.sb("scale", [2])
        unscale = al.sb("unscale", [2])
        banks = [al.ps(f"out{t}", [D]) for t in range(TB)]
        turn = [al.ps(f"turn{t}", [KD * P], BF16) for t in range(TB)]

        x_in = [al.sem(f"x_in{g}") for g in range(B)]
        c_in = [al.sem(f"c_in{g}") for g in range(B)]
        const_in = al.sem("const_in")
        bias_in = al.sem("bias_in")
        const_ready = al.sem("const_ready")
        chain = al.sem("chain")
        xn_ready = al.sem("xn_ready")
        biased = al.sem("biased")
        amax_ready = al.sem("amax_ready")
        amax_over = al.sem("amax_over")
        scale_ready = al.sem("scale_ready")
        scaled_ready = al.sem("scaled_ready")
        lifted_ready = al.sem("lifted_ready")
        quant_ready = al.sem("quant_ready")
        turned = al.sem("turned")
        turned_out = al.sem("turned_out")
        product = al.sem("product")
        added = al.sem("added")
        block = ctx.enter_context(nc.Block())
        tiles = lambda a, g: a[g].rearrange("(t p) d -> p t d", p=P)

        @block.sync
        def _(sp):
            for g in range(B):
                sp.dma_start(x_res[:, TB * g:TB * g + TB, :], tiles(x, g)).then_inc(x_in[g], 16)
            for g in range(B):
                sp.dma_start(raw[:, TB * g:TB * g + TB, :], tiles(ctx_in, g)).then_inc(c_in[g], 16)
            sp.dma_start(ident[:, :], consts[0]).then_inc(const_in, 16)
            sp.dma_start(had_raw[:, :], consts[1]).then_inc(const_in, 16)
            for b in range(B):
                sp.dma_start(bias_bc[:, b, :], bias[b].partition_broadcast(P)).then_inc(bias_in, 16)

        @block.gpsimd
        def _(pool):
            pool.wait_ge(amax_ready, 1)
            nc.gpsimd.partition_all_reduce(amax_all[:, :], amax[:, :], P,
                                           bass.bass_isa.ReduceOp.max).then_inc(amax_over, 1)
            pool.wait_ge(bias_in, 16 * B)
            for b in range(B):
                for t in range(TB):
                    x_tile = x_res[:, TB * b + t, :]
                    ins = pool.tensor_tensor(x_tile, x_tile, bias_bc[:, b, :], ALU.add)
                ins.then_inc(biased, 1)

        @block.scalar
        def _(act):
            act.wait_ge(const_in, 32)
            act.activation(ident_bf[:, :], ident[:, :], ACT.Copy).then_inc(const_ready, 1)
            act.activation(had[:, :], had_raw[:, :], ACT.Copy).then_inc(const_ready, 1)
            act.wait_ge(scale_ready, 1)

            def scale_group(n, src, which):
                if n >= 2:
                    act.wait_ge(lifted_ready, n - 1)
                act.activation(scaled[:, n % 2], src, ACT.Copy,
                               scale=scale[:, which:which + 1]).then_inc(scaled_ready, 1)

            scale_group(0, xn[:, 0:TB, :], 0)
            scale_group(1, raw[:, 0:TB, :], 1)
            for b in range(B):
                if b + 1 < B:
                    scale_group(2 * b + 2, xn[:, TB * b + TB:TB * b + 2 * TB, :], 0)
                    scale_group(2 * b + 3, raw[:, TB * b + TB:TB * b + 2 * TB, :], 1)
                if b > 0:
                    act.wait_ge(product, TB * b)
                for t in range(TB):
                    act.wait_ge(turned, TB * b + t + 1)
                    act.activation(xqT[:, :, t * P:(t + 1) * P], turn[t].rearrange("p (k t) -> p k t", k=KD),
                                   ACT.Copy).then_inc(turned_out, 1)

        @block.vector
        def _(dve):
            links = [0]

            def link(ins):
                links[0] += 1
                ins.then_inc(chain, 1)
                dve.wait_ge(chain, links[0])

            def batch_amax(which, values, g):
                return dve.tensor_reduce(amax_parts[:, which, g:g + 1], values[:, TB * g:TB * g + TB, :], AX.XY,
                                         ALU.max, apply_absolute_value=True)

            for g in range(B):
                dve.wait_ge(x_in[g], 16)
                stats.read(dve, g)
            stats.finish(dve, 0, B)
            for g in range(B):
                for i in range(TB * g, TB * g + TB):
                    ins = dve.tensor_scalar(xn[:, i, :], x_res[:, i, :], stats.mean_var[:, i, 0:1],
                                            stats.rstd[:, i:i + 1], ALU.subtract, ALU.mult)
                ins.then_inc(xn_ready, 1)
                if g > 0:
                    dve.wait_ge(xn_ready, g)
                    batch_amax(0, xn, g - 1)
            dve.wait_ge(xn_ready, B)
            batch_amax(0, xn, B - 1)
            for g in range(B):
                dve.wait_ge(c_in[g], 16)
                ins = batch_amax(1, raw, g)
            link(ins)
            dve.tensor_reduce(amax[:, :], amax_parts[:, :, :], AX.X, ALU.max).then_inc(amax_ready, 1)
            dve.wait_ge(amax_over, 1)
            link(dve.tensor_scalar(amax[:, :], amax_all[:, :], FP8_AMAX_EPS, None, ALU.max))
            link(dve.reciprocal(inv_amax[:, :], amax[:, :]))
            dve.tensor_scalar(scale[:, :], inv_amax[:, :], FP8_MAX, None, ALU.mult).then_inc(scale_ready, 1)
            dve.wait_ge(scale_ready, 1)
            link(dve.tensor_tensor(unscale[:, 0:1], scale[:, 0:1], scale[:, 1:2], ALU.mult))
            link(dve.reciprocal(unscale[:, 1:2], unscale[:, 0:1]))

            def quantise(n, out):
                y = scaled[:, n % 2]
                dve.wait_ge(scaled_ready, n + 1)
                link(dve.tensor_scalar(magic[:, :, :].bitcast(U32), y.bitcast(U32), EXPONENT_BITS, None,
                                       ALU.bitwise_and))
                link(dve.tensor_scalar(magic[:, :, :], magic[:, :, :], FP8_MIN_NORMAL, ROUND_MAGIC, ALU.max, ALU.mult))
                dve.tensor_tensor(lifted[:, :, :], y, magic[:, :, :], ALU.add).then_inc(lifted_ready, 1)
                dve.wait_ge(lifted_ready, n + 1)
                link(dve.tensor_tensor(out, lifted[:, :, :], magic[:, :, :], ALU.subtract))
                dve.tensor_scalar(out, out, FP8_MAX, -FP8_MAX, ALU.min, ALU.max).then_inc(quant_ready, 1)

            for b in range(B + 1):
                if b < B:
                    if b > 0:
                        dve.wait_ge(turned, TB * b)
                    quantise(2 * b, xq[:, :, :])
                    if b > 1:
                        dve.wait_ge(product, TB * (b - 1))
                    quantise(2 * b + 1, cq[:, b % 2])
                if b > 0:
                    dve.wait_ge(biased, b)
                    for t in range(TB):
                        i = TB * (b - 1) + t
                        dve.wait_ge(product, i + 1)
                        dve.scalar_tensor_tensor(out=x_res[:, i, :], in0=banks[t][:, :], scalar=unscale[:, 1:2],
                                                 in1=x_res[:, i, :], op0=ALU.mult, op1=ALU.add).then_inc(added, 1)
                    if b < B:
                        dve.wait_ge(added, TB * b)
                        stats.compute(dve, b - 1)

        @block.tensor
        def _(pe):
            pe.wait_ge(const_ready, 2)
            for b in range(B):
                pe.wait_ge(quant_ready, 2 * b + 1)
                for t in range(TB):
                    if b > 0:
                        pe.wait_ge(turned_out, TB * (b - 1) + t + 1)
                    for k in range(KD):
                        ins = pe.transpose(turn[t][:, k * P:(k + 1) * P], xq[:, t, k * P:(k + 1) * P], ident_bf[:, :])
                    ins.then_inc(turned, 1)
                pe.wait_ge(turned_out, TB * (b + 1))
                pe.wait_ge(quant_ready, 2 * b + 2)
                for t in range(TB):
                    if b > 0:
                        pe.wait_ge(added, TB * (b - 1) + t + 1)
                    for k in range(KD):
                        ins = pe.matmul(banks[t][:, :], xqT[:, k, t * P:(t + 1) * P], cq[:, b % 2, k, :],
                                        start=(k == 0), stop=(k == KD - 1))
                    ins.then_inc(product, 1)


def experts_phase(nc, Wsh_up, Wsh_down, Wrt_up, Wrt_down, W_router, W2, W2_scratch, x_res, ident, stats):
    with ExitStack() as ctx:
        al = Alloc(nc, ctx, "e")
        xT_hi = al.sb("xT_hi", [KD, B * S], F32R)
        xT_lo = al.sb("xT_lo", [KD, B * S], F32R)
        up_raw = al.sb("up_raw", [2, KD, DE])
        up_hi = al.sb("up_hi", [2, KD, DE], F32R)
        up_lo = al.sb("up_lo", [2, KD, DE], F32R)
        down_raw = al.sb("down_raw", [2, KE, D])
        down_hi = al.sb("down_hi", [2, KE, D], F32R)
        down_lo = al.sb("down_lo", [2, KE, D], F32R)
        router_raw = al.sb("router_raw", [KD, E_RT])
        router_hi = al.sb("router_hi", [KD, E_RT], F32R)
        router_lo = al.sb("router_lo", [KD, E_RT], F32R)
        mid_hi = al.sb("mid_hi", [2, KE, S], F32R)
        mid_lo = al.sb("mid_lo", [2, KE, S], F32R)
        zeros = al.sb("zeros", [KD])
        gates = al.sb("gates", [NT, E_ALL])
        w2a = al.sb("w2a", [FH])
        w2b = al.sb("w2b", [FH])
        logits = al.sb("logits", [NT, E_RT])
        probs = al.sb("probs", [NT, E_RT])
        rest = al.sb("rest", [NT, E_RT])
        first = al.sb("first", [NT, E_RT])
        score = al.sb("score", [NT, E_RT])
        rank = al.sb("rank", [NT, E_RT])
        top = al.sb("top", [NT])
        inv = al.sb("inv", [NT])
        up_bank = [[al.ps(f"up{i}{k}", [S]) for k in range(KE)] for i in range(2)]
        down_bank = [al.ps(f"down{t}", [D]) for t in range(TB)]
        ln = LayerNorm(al, stats, ident, down_bank)
        logits_bank = down_bank[0][:, 0:TB * E_RT].rearrange("p (t e) -> p t e", e=E_RT)

        up_in = [al.sem(f"up_in{i}") for i in range(2)]
        down_in = [al.sem(f"down_in{i}") for i in range(2)]
        router_in = al.sem("router_in")
        router_hi_ready = al.sem("router_hi_ready")
        router_ready = al.sem("router_ready")
        up_hi_ready = al.sem("up_hi_ready")
        up_ready = al.sem("up_ready")
        down_hi_ready = al.sem("down_hi_ready")
        down_ready = al.sem("down_ready")
        routed = al.sem("routed")
        logits_ready = al.sem("logits_ready")
        w2_in = al.sem("w2_in")
        w2_step = al.sem("w2_step")
        w2_out = al.sem("w2_out")
        exp_ready = al.sem("exp_ready")
        gate_chain = al.sem("gate_chain")
        shifted = al.sem("shifted")
        zeros_ready = al.sem("zeros_ready")
        rank_ready = al.sem("rank_ready")
        up_done = al.sem("up_done")
        gelu_ready = al.sem("gelu_ready")
        mid_hi_ready = al.sem("mid_hi_ready")
        mid_ready = al.sem("mid_ready")
        down_done = al.sem("down_done")
        added = al.sem("added")

        block = ctx.enter_context(nc.Block())
        rows = lambda a: a.rearrange("(k p) n -> p k n", p=P)

        @block.sync
        def _(sp):
            sp.dma_start(router_raw[:, :, :], rows(W_router)).then_inc(router_in, 16)
            for i in range(E_SH):
                sp.dma_start(up_raw[:, i], rows(Wsh_up[i])).then_inc(up_in[i], 16)
                sp.dma_start(down_raw[:, i], rows(Wsh_down[i])).then_inc(down_in[i], 16)
            up_flat = Wrt_up.rearrange("(n i) (k p) m -> n i p k m", i=2, p=P)
            down_flat = Wrt_down.rearrange("(n i) (k p) m -> n i p k m", i=2, p=P)
            with sp.Fori(0, E_RT // 2) as n:
                for i in range(2):
                    sp.wait_ge(up_ready, 2 * n + (i + 1))
                    sp.dma_start(up_raw[:, i], up_flat[bass.ds(n, 1), i]).then_inc(up_in[i], 16)
                    sp.wait_ge(down_ready, 2 * n + (i + 1))
                    sp.dma_start(down_raw[:, i], down_flat[bass.ds(n, 1), i]).then_inc(down_in[i], 16)
            sp.wait_ge(w2_out, 16 * (D // P))

        @block.gpsimd
        def _(pool):
            for e in range(E_RT):
                ins = pool.memset(rank[:, :, e:e + 1], float(E_RT - e))
            ins.then_inc(rank_ready, 1)
            pool.memset(zeros[:, :], 0.0).then_inc(zeros_ready, 1)
            pool.wait_ge(zeros_ready, 1)
            pool.wait_ge(router_in, 16)
            pool.tensor_copy(router_hi[:, :, :], router_raw[:, :, :]).then_inc(router_hi_ready, 1)
            pool.wait_ge(router_hi_ready, 1)
            pool.tensor_tensor(router_lo[:, :, :], router_raw[:, :, :], f32(router_hi[:, :, :]),
                               ALU.subtract).then_inc(router_ready, 1)

            zero = zeros[:, :].unsqueeze(2)

            def split(n, i, reused):
                pool.wait_ge(up_in[i], 16 * n + 16)
                if reused:
                    pool.wait_ge(up_done, (2 * n + i - 1) * (B * KE))
                pool.tensor_tensor(up_hi[:, i], up_raw[:, i], zero.to_broadcast([P, KD, DE]), ALU.add).then_inc(up_hi_ready, 1)
                pool.wait_ge(up_hi_ready, 2 * n + (i + 1))
                pool.tensor_tensor(up_lo[:, i], up_raw[:, i], f32(up_hi[:, i]), ALU.subtract).then_inc(up_ready, 1)
                pool.wait_ge(down_in[i], 16 * n + 16)
                if reused:
                    pool.wait_ge(down_done, (2 * n + i - 1) * (B * TB))
                pool.tensor_tensor(down_hi[:, i], down_raw[:, i], zero[:, 0:KE].to_broadcast([P, KE, D]), ALU.add).then_inc(down_hi_ready, 1)
                pool.wait_ge(down_hi_ready, 2 * n + (i + 1))
                pool.tensor_tensor(down_lo[:, i], down_raw[:, i], f32(down_hi[:, i]),
                                   ALU.subtract).then_inc(down_ready, 1)

            def butterflies(c):
                if c > 0:
                    pool.wait_ge(w2_out, 16 * c)
                pool.dma_start(w2a[:, :], W2[c * P:(c + 1) * P, :]).then_inc(w2_in, 16)
                pool.wait_ge(w2_in, 16 * (c + 1))
                src, dst = w2a, w2b
                for s in range(4):
                    span = P << s
                    halves = lambda a, h: a[:, :].rearrange("p (n h s) -> p n h s", h=2, s=span)[:, :, h, :]
                    if s > 0:
                        pool.wait_ge(w2_step, 8 * c + 2 * s)
                    pool.tensor_tensor(halves(dst, 0), halves(src, 0), halves(src, 1), ALU.add).then_inc(w2_step, 1)
                    pool.tensor_tensor(halves(dst, 1), halves(src, 0), halves(src, 1),
                                       ALU.subtract).then_inc(w2_step, 1)
                    src, dst = dst, src
                pool.wait_ge(w2_step, 8 * (c + 1))
                pool.dma_start(W2_scratch[c * P:(c + 1) * P, :], w2a[:, :]).then_inc(w2_out, 16)

            for i in range(2):
                split(0, i, False)
            for c in range(D // P):
                for i in range(2):
                    split(c + 1, i, True)
                butterflies(c)
            with pool.Fori(D // P + 1, E_ALL // 2) as n:
                for i in range(2):
                    split(n, i, True)

        @block.scalar
        def _(act):
            def unit(n, i, b):
                u = 2 * n * B + (i * B + b)
                for k in range(KE):
                    act.wait_ge(up_done, u * KE + (k + 1))
                    bank = up_bank[b % 2][k]
                    act.activation(bank[:, :], bank[:, :], ACT.Gelu).then_inc(gelu_ready, 1)
                    act.wait_ge(gelu_ready, u * KE + (k + 1))
                    act.activation(mid_hi[:, b % 2, k], bank[:, :], ACT.Copy).then_inc(mid_hi_ready, 1)

            for b in range(B):
                ln.scalar_hi(act, b, xT_hi, b)
                unit(0, 0, b)
                act.wait_ge(routed, b + 1)
                act.activation(logits[:, TB * b:TB * (b + 1), :], logits_bank, ACT.Copy).then_inc(logits_ready, 1)
            act.wait_ge(shifted, 1)
            act.activation(probs[:, :, :], probs[:, :, :], ACT.Exp).then_inc(exp_ready, 1)
            for b in range(B):
                unit(0, 1, b)
            with act.Fori(1, E_ALL // 2) as n:
                for i in range(2):
                    for b in range(B):
                        unit(n, i, b)

        @block.vector
        def _(dve):
            links = [0]

            def link(ins):
                links[0] += 1
                ins.then_inc(gate_chain, 1)
                dve.wait_ge(gate_chain, links[0])

            wide = lambda a: a[:, :].unsqueeze(2).to_broadcast([P, NT, E_RT])
            def routing():
                dve.wait_ge(logits_ready, B)
                link(dve.tensor_reduce(top[:, :], logits[:, :, :], AX.X, ALU.max))
                dve.tensor_tensor(probs[:, :, :], logits[:, :, :], wide(top), ALU.subtract).then_inc(shifted, 1)
                dve.wait_ge(exp_ready, 1)
                link(dve.tensor_reduce(top[:, :], probs[:, :, :], AX.X, ALU.add))
                link(dve.reciprocal(inv[:, :], top[:, :]))
                link(dve.tensor_tensor(probs[:, :, :], probs[:, :, :], wide(inv), ALU.mult))

                def pick(values, out):
                    link(dve.tensor_reduce(top[:, :], values, AX.X, ALU.max))
                    link(dve.tensor_tensor(score[:, :, :], values, wide(top), ALU.is_equal))
                    link(dve.tensor_tensor(score[:, :, :], score[:, :, :], rank[:, :, :], ALU.mult))
                    link(dve.tensor_reduce(top[:, :], score[:, :, :], AX.X, ALU.max))
                    link(dve.tensor_tensor(out, score[:, :, :], wide(top), ALU.is_equal))

                dve.wait_ge(rank_ready, 1)
                pick(probs[:, :, :], first[:, :, :])
                link(dve.scalar_tensor_tensor(out=rest[:, :, :], in0=first[:, :, :], scalar=-2.0, in1=probs[:, :, :],
                                              op0=ALU.mult, op1=ALU.add))
                pick(rest[:, :, :], rest[:, :, :])
                link(dve.tensor_tensor(first[:, :, :], first[:, :, :], rest[:, :, :], ALU.add))
                link(dve.tensor_tensor(gates[:, :, E_SH:E_ALL], first[:, :, :], probs[:, :, :], ALU.mult))

            def low(n, i, b):
                u = 2 * n * B + (i * B + b)
                for k in range(KE):
                    dve.wait_ge(mid_hi_ready, u * KE + (k + 1))
                    dve.tensor_tensor(mid_lo[:, b % 2, k], up_bank[b % 2][k][:, :], f32(mid_hi[:, b % 2, k]),
                                      ALU.subtract).then_inc(mid_ready, 1)

            def add(n, i, b):
                u = 2 * n * B + (i * B + b)
                e = 2 * n + i
                for t in range(TB):
                    dve.wait_ge(down_done, u * TB + (t + 1))
                    x_tile = x_res[:, TB * b + t, :]
                    gate = gates[:, TB * b + t, bass.ds(e, 1)]
                    dve.scalar_tensor_tensor(out=x_tile, in0=down_bank[t][:, :], scalar=gate, in1=x_tile,
                                             op0=ALU.mult, op1=ALU.add).then_inc(added, 1)

            def body(n, last):
                for i in range(2):
                    for b in range(B):
                        if b + 1 < B:
                            low(n, i, b + 1)
                        elif i == 0:
                            low(n, 1, 0)
                        elif not last:
                            low(n + 1, 0, 0)
                        add(n, i, b)
                        if last and i == 1 and b + 1 < B:
                            dve.wait_ge(added, (E_ALL * B - B + b + 1) * TB)
                            stats.compute(dve, b)
            link(dve.memset(gates[:, :, 0:E_SH], 1.0))
            ln.vector_norm(dve, 0, 0)
            for b in range(B):
                ln.vector_lo(dve, b, xT_hi, xT_lo, b)
                if b == 1:
                    stats.compute(dve, B - 1)
                if b + 1 < B:
                    ln.vector_norm(dve, b + 1, b + 1)
                low(0, 0, b)
                if b > 0:
                    add(0, 0, b - 1)
            routing()
            low(0, 1, 0)
            add(0, 0, B - 1)
            for b in range(B):
                low(*((0, 1, b + 1) if b + 1 < B else (1, 0, 0)))
                add(0, 1, b)
            with dve.Fori(1, E_ALL // 2 - 1) as n:
                body(n, False)
            body(E_ALL // 2 - 1, True)

        @block.tensor
        def _(pe):
            def route(b):
                if b == 0:
                    pe.wait_ge(router_ready, 1)
                for t in range(TB):
                    cols = slice((TB * b + t) * P, (TB * b + t + 1) * P)
                    ins = three_pass(pe, logits_bank[:, t, :], lambda k: xT_hi[:, k, cols], lambda k: xT_lo[:, k, cols],
                                     lambda k: router_hi[:, k, :], lambda k: router_lo[:, k, :], KD)
                ins.then_inc(routed, 1)

            def up(n, i, b, reused):
                u = 2 * n * B + (i * B + b)
                cols = slice(b * S, (b + 1) * S)
                if b == 0:
                    pe.wait_ge(up_ready, 2 * n + (i + 1))
                for k in range(KE):
                    if reused:
                        pe.wait_ge(mid_ready, (u - 2) * KE + (k + 1))
                    ks = slice(k * P, (k + 1) * P)
                    three_pass(pe, up_bank[b % 2][k][:, :], lambda c: up_hi[:, i, c, ks], lambda c: up_lo[:, i, c, ks],
                               lambda c: xT_hi[:, c, cols], lambda c: xT_lo[:, c, cols], KD).then_inc(up_done, 1)

            def down(n, i, b, reused):
                u = 2 * n * B + (i * B + b)
                if b == 0:
                    pe.wait_ge(down_ready, 2 * n + (i + 1))
                pe.wait_ge(mid_ready, (u + 1) * KE)
                for t in range(TB):
                    if reused:
                        pe.wait_ge(added, (u - 1) * TB + (t + 1))
                    ts = slice(t * P, (t + 1) * P)
                    three_pass(pe, down_bank[t][:, :], lambda k: mid_hi[:, b % 2, k, ts],
                               lambda k: mid_lo[:, b % 2, k, ts], lambda k: down_hi[:, i, k, :],
                               lambda k: down_lo[:, i, k, :], KE).then_inc(down_done, 1)

            def body(n, last):
                for i in range(2):
                    for b in range(B):
                        if b + 1 < B:
                            up(n, i, b + 1, True)
                        elif i == 0:
                            up(n, 1, 0, True)
                        elif not last:
                            up(n + 1, 0, 0, True)
                        down(n, i, b, True)

            for b in range(B):
                if b > 0:
                    pe.wait_ge(logits_ready, b)
                if b > 1:
                    pe.wait_ge(added, TB * (b - 1))
                ln.tensor_turn(pe, b)
                pe.wait_ge(ln.lo_ready, TB * (b + 1))
                up(0, 0, b, b > 1)
                route(b)
                if b > 0:
                    pe.wait_ge(logits_ready, b + 1)
                    down(0, 0, b - 1, b > 1)
            up(0, 1, 0, True)
            down(0, 0, B - 1, True)
            for b in range(B):
                up(*((0, 1, b + 1) if b + 1 < B else (1, 0, 0)), True)
                down(0, 1, b, True)
            with pe.Fori(1, E_ALL // 2 - 1) as n:
                body(n, False)
            body(E_ALL // 2 - 1, True)


def attention_phase(nc, ctx_in, Wq, Wk, Wv, Wo, x_res, ident, stats):
    with ExitStack() as ctx:
        al = Alloc(nc, ctx, "t")
        W = PAIRS * S
        xT_hi = al.sb("xT_hi", [KD, W], F32R)
        xT_lo = al.sb("xT_lo", [KD, W], F32R)
        cT_hi = al.sb("cT_hi", [KD, W], F32R)
        cT_lo = al.sb("cT_lo", [KD, W], F32R)
        c_raw = al.sb("c_raw", [PAIRS, TB, D])
        names = ("q", "k", "v")
        w_raw = {n: al.sb(f"w{n}_raw", [KD, HD]) for n in names}
        w_hi = {n: al.sb(f"w{n}_hi", [KD, HD], F32R) for n in names}
        w_lo = {n: al.sb(f"w{n}_lo", [KD, HD], F32R) for n in names}
        w_raw["o"] = al.sb("wo_raw", [D])
        w_hi["o"] = al.sb("wo_hi", [D], F32R)
        w_lo["o"] = al.sb("wo_lo", [D], F32R)
        q_hi, q_lo = al.sb("q_hi", [S], F32R), al.sb("q_lo", [S], F32R)
        k_hi, k_lo = al.sb("k_hi", [S], F32R), al.sb("k_lo", [S], F32R)
        vT = al.sb("vT", [S])
        v_hi, v_lo = al.sb("v_hi", [TB, HD], F32R), al.sb("v_lo", [TB, HD], F32R)
        probs = al.sb("probs", [TB, S])
        pT_hi, pT_lo = al.sb("pT_hi", [TB, S], F32R), al.sb("pT_lo", [TB, S], F32R)
        o_hi, o_lo = al.sb("o_hi", [S], F32R), al.sb("o_lo", [S], F32R)
        zeros = al.sb("zeros", [KD])
        neg_max, total, inv = al.sb("neg_max", [TB]), al.sb("total", [TB]), al.sb("inv", [TB])
        score_bank = [al.ps(f"score{t}", [S]) for t in range(TB)]
        out_bank = [al.ps(f"out{t}", [D]) for t in range(2)]
        qv_bank = al.ps("qv", [S])
        ko_bank = al.ps("ko", [S])
        ln = LayerNorm(al, stats, ident, score_bank)
        sem = al.sem
        c_in = [sem(f"c_in{i}") for i in range(PAIRS)]
        c_turned = sem("c_turned")
        c_hi_ready, c_lo_ready = sem("c_hi_ready"), sem("c_lo_ready")
        zeros_ready = sem("zeros_ready")
        w_in = {n: sem(f"w{n}_in") for n in "qkvo"}
        w_hi_ready = {n: sem(f"w{n}_hi_ready") for n in "qkvo"}
        w_ready = {n: sem(f"w{n}_ready") for n in "qkvo"}
        q_done, k_done, v_done = sem("q_done"), sem("k_done"), sem("v_done")
        q_hi_ready, k_hi_ready = sem("q_hi_ready"), sem("k_hi_ready")
        q_ready, k_ready = sem("q_ready"), sem("k_ready")
        vT_ready = sem("vT_ready")
        v_turned = sem("v_turned")
        v_hi_ready, v_ready = sem("v_hi_ready"), sem("v_ready")
        scored = sem("scored")
        max_ready = sem("max_ready")
        exp_ready = sem("exp_ready")
        inv_ready = sem("inv_ready")
        probs_ready = sem("probs_ready")
        p_turned = sem("p_turned")
        p_hi_ready, p_ready = sem("p_hi_ready"), sem("p_ready")
        o_done = sem("o_done")
        o_hi_ready, o_ready = sem("o_hi_ready"), sem("o_ready")
        out_done = sem("out_done")
        added = sem("added")
        block = ctx.enter_context(nc.Block())

        heads_in = {"q": Wq, "k": Wk, "v": Wv}
        UNITS = H * 2
        SCALE = float(HD) ** -0.5
        fourths = lambda bank: bank[:, :].rearrange("p (k t) -> p k t", k=KD)


        @block.sync
        def _(sp):
            def load(r, h, wait):
                for n in "qkv":
                    if wait:
                        sp.wait_ge(w_ready[n], H * r + h)
                    src = heads_in[n].rearrange("(k p) (h c) -> h p k c", p=P, c=HD)
                    sp.dma_start(w_raw[n][:, :, :], src[h] if isinstance(h, int) else src[bass.ds(h, 1)]
                                 ).then_inc(w_in[n], 16)
                if wait:
                    sp.wait_ge(w_ready["o"], H * r + h)
                src = Wo.rearrange("(h p) n -> h p n", p=P)
                sp.dma_start(w_raw["o"][:, :], src[h] if isinstance(h, int) else src[bass.ds(h, 1)]
                             ).then_inc(w_in["o"], 16)

            for r in range(PAIRS):
                for i in range(2):
                    if r > 0:
                        sp.wait_ge(c_turned, 2 * TB * (r - 1) + TB * (i + 1))
                    sp.dma_start(c_raw[:, i], ctx_in[2 * r + i].rearrange("(t p) d -> p t d", p=P)).then_inc(c_in[i], 16)
                load(r, 0, r > 0)
                with sp.Fori(1, H) as h:
                    load(r, h, True)

        @block.gpsimd
        def _(pool):
            def split(n, r, h, last_use):
                zero = zeros[:, 0:1].to_broadcast([P, D]) if n == "o" else zeros[:, :].unsqueeze(2).to_broadcast([P, KD, HD])
                pool.wait_ge(w_in[n], (H * r + h + 1) * 16)
                if last_use is not None:
                    pool.wait_ge(*last_use)
                pool.tensor_tensor(w_hi[n][:], w_raw[n][:], zero, ALU.add).then_inc(w_hi_ready[n], 1)
                pool.wait_ge(w_hi_ready[n], H * r + h + 1)
                pool.tensor_tensor(w_lo[n][:], w_raw[n][:], f32(w_hi[n][:]), ALU.subtract).then_inc(w_ready[n], 1)

            def split_all(r, h, first):
                units_before = UNITS * r + h * 2
                for n, done in (("q", q_done), ("k", k_done), ("v", v_done)):
                    split(n, r, h, None if first else (done, units_before))
                split("o", r, h, None if first else (out_done, units_before * TB))

            pool.memset(zeros[:, :], 0.0).then_inc(zeros_ready, 1)
            pool.wait_ge(zeros_ready, 1)
            for r in range(PAIRS):
                split_all(r, 0, r == 0)
                with pool.Fori(1, H) as h:
                    split_all(r, h, False)

        @block.scalar
        def _(act):
            def query(r, u):
                act.wait_ge(q_done, UNITS * r + u + 1)
                act.activation(q_hi[:, :], qv_bank[:, :], ACT.Copy, scale=SCALE).then_inc(q_hi_ready, 1)

            def key(r, u):
                act.wait_ge(k_done, UNITS * r + u + 1)
                act.activation(k_hi[:, :], ko_bank[:, :], ACT.Copy).then_inc(k_hi_ready, 1)

            def values(r, u):
                act.wait_ge(v_done, UNITS * r + u + 1)
                act.activation(vT[:, :], qv_bank[:, :], ACT.Copy).then_inc(vT_ready, 1)

            def values_hi(r, u):
                act.wait_ge(v_turned, UNITS * r + u + 1)
                act.activation(v_hi[:, :, :], out_bank[0][:, :].rearrange("p (t d) -> p t d", t=TB),
                               ACT.Copy).then_inc(v_hi_ready, 1)

            def inputs(r, i, half):
                for t in (2 * half, 2 * half + 1):
                    act.wait_ge(c_turned, TB * (2 * r + i) + t + 1)
                    c = (TB * i + t) * P
                    act.activation(cT_hi[:, :, c:c + P], fourths(out_bank[t % 2]), ACT.Copy).then_inc(c_hi_ready, 1)

            def unit(r, u, last):
                n = UNITS * r + u
                for t in range(TB):
                    act.wait_ge(max_ready, n * TB + (t + 1))
                    act.activation(probs[:, t, :], score_bank[t][:, :], ACT.Exp, bias=neg_max[:, t:t + 1],
                                   accum_out=total[:, t:t + 1]).then_inc(exp_ready, 1)
                act.wait_ge(inv_ready, n + 1)
                for t in range(TB):
                    act.activation(probs[:, t, :], probs[:, t, :], ACT.Copy,
                                   scale=inv[:, t:t + 1]).then_inc(probs_ready, 1)
                if not last:
                    query(r, u + 1)
                    key(r, u + 1)
                for t in range(TB):
                    act.wait_ge(p_turned, n * TB + (t + 1))
                    act.activation(pT_hi[:, :, t * P:(t + 1) * P], fourths(score_bank[t]),
                                   ACT.Copy).then_inc(p_hi_ready, 1)
                if not last:
                    values(r, u + 1)
                act.wait_ge(o_done, n + 1)
                act.activation(o_hi[:, :], ko_bank[:, :], ACT.Copy).then_inc(o_hi_ready, 1)
                if not last:
                    values_hi(r, u + 1)

            for r in range(PAIRS):
                ln.scalar_hi(act, 2 * r, xT_hi, 0)
                inputs(r, 0, 0)
                query(r, 0)
                inputs(r, 0, 1)
                key(r, 0)
                ln.scalar_hi(act, 2 * r + 1, xT_hi, 1)
                inputs(r, 1, 0)
                values(r, 0)
                inputs(r, 1, 1)
                values_hi(r, 0)
                with act.Fori(0, H - 1) as h:
                    unit(r, 2 * h, False)
                    unit(r, 2 * h + 1, False)
                unit(r, UNITS - 2, False)
                unit(r, UNITS - 1, True)

        @block.vector
        def _(dve):
            def project_q(r, u):
                n = UNITS * r + u
                dve.wait_ge(q_hi_ready, n + 1)
                dve.scalar_tensor_tensor(out=q_lo[:, :], in0=qv_bank[:, :], scalar=SCALE, in1=f32(q_hi[:, :]),
                                         op0=ALU.mult, op1=ALU.subtract).then_inc(q_ready, 1)

            def project_k(r, u):
                n = UNITS * r + u
                dve.wait_ge(k_hi_ready, n + 1)
                dve.tensor_tensor(k_lo[:, :], ko_bank[:, :], f32(k_hi[:, :]), ALU.subtract).then_inc(k_ready, 1)

            def values_lo(r, u):
                dve.wait_ge(v_hi_ready, UNITS * r + u + 1)
                dve.tensor_tensor(v_lo[:, :, :], out_bank[0][:, :].rearrange("p (t d) -> p t d", t=TB),
                                  f32(v_hi[:, :, :]), ALU.subtract).then_inc(v_ready, 1)

            def add(r, u, b, t):
                dve.wait_ge(out_done, (UNITS * r + u) * TB + (t + 1))
                x_tile = x_res[:, TB * (2 * r + b) + t, :]
                dve.tensor_tensor(x_tile, out_bank[t % 2][:, :], x_tile, ALU.add).then_inc(added, 1)

            def inputs(r, i, half):
                for t in (2 * half, 2 * half + 1):
                    dve.wait_ge(c_hi_ready, TB * (2 * r + i) + t + 1)
                    c = (TB * i + t) * P
                    dve.tensor_tensor(cT_lo[:, :, c:c + P], fourths(out_bank[t % 2]), f32(cT_hi[:, :, c:c + P]),
                                      ALU.subtract).then_inc(c_lo_ready, 1)

            def unit(r, u, b, first, last, batch_stats=None):
                n = UNITS * r + u
                for t in range(TB):
                    dve.wait_ge(scored, n * TB + (t + 1))
                    dve.tensor_reduce(neg_max[:, t:t + 1], score_bank[t][:, :], AX.X, ALU.max,
                                      negate=True).then_inc(max_ready, 1)
                dve.wait_ge(exp_ready, (n + 1) * TB)
                dve.reciprocal(inv[:, :], total[:, :]).then_inc(inv_ready, 1)
                if not first:
                    for t in range(TB):
                        add(r, u - 1, 1 - b, t)
                if not last:
                    project_q(r, u + 1)
                    project_k(r, u + 1)
                for t in range(TB):
                    dve.wait_ge(p_hi_ready, n * TB + (t + 1))
                    dve.tensor_tensor(pT_lo[:, :, t * P:(t + 1) * P], fourths(score_bank[t]),
                                      f32(pT_hi[:, :, t * P:(t + 1) * P]), ALU.subtract).then_inc(p_ready, 1)
                if batch_stats is not None:
                    stats.compute(dve, batch_stats)
                dve.wait_ge(o_hi_ready, n + 1)
                dve.tensor_tensor(o_lo[:, :], ko_bank[:, :], f32(o_hi[:, :]), ALU.subtract).then_inc(o_ready, 1)
                if not last:
                    values_lo(r, u + 1)

            for r in range(PAIRS):
                m = 2 * r
                if r == 0:
                    ln.vector_norm(dve, 0, 0)
                ln.vector_lo(dve, m, xT_hi, xT_lo, 0)
                ln.vector_norm(dve, m + 1, m + 1)
                inputs(r, 0, 0)
                project_q(r, 0)
                inputs(r, 0, 1)
                project_k(r, 0)
                ln.vector_lo(dve, m + 1, xT_hi, xT_lo, 1)
                if m + 2 < B:
                    ln.vector_norm(dve, m + 2, m + 2)
                inputs(r, 1, 0)
                inputs(r, 1, 1)
                values_lo(r, 0)
                unit(r, 0, 0, True, False)
                unit(r, 1, 1, False, False, B - 1 if r == 0 else 0)
                with dve.Fori(1, H - 1) as h:
                    unit(r, 2 * h, 0, False, False)
                    unit(r, 2 * h + 1, 1, False, False)
                unit(r, UNITS - 2, 0, False, False, 1 if r > 0 else None)
                unit(r, UNITS - 1, 1, False, True)
                if r == PAIRS - 1:
                    dve.wait_ge(added, (UNITS * PAIRS - 1) * TB)
                    stats.compute(dve, 2)
                for t in range(TB):
                    add(r, UNITS - 1, 1, t)

        @block.tensor
        def _(pe):
            def project(name, r, u, h, b, bank, src_hi, src_lo, done):
                if b == 0:
                    pe.wait_ge(w_ready[name], H * r + h + 1)
                cols = slice(b * S, (b + 1) * S)
                three_pass(pe, bank[:, :], lambda k: w_hi[name][:, k, :], lambda k: w_lo[name][:, k, :],
                           lambda k: src_hi[:, k, cols], lambda k: src_lo[:, k, cols], KD).then_inc(done, 1)

            def project_q(r, u, h, b):
                n = UNITS * r + u
                if not (isinstance(u, int) and n == 0):
                    pe.wait_ge(v_turned, n)
                project("q", r, u, h, b, qv_bank, xT_hi, xT_lo, q_done)

            def project_k(r, u, h, b):
                n = UNITS * r + u
                if not (isinstance(u, int) and u == 0 and r == 0):
                    if isinstance(u, int) and u == 0:
                        pe.wait_ge(o_ready, UNITS * r)
                    elif not (isinstance(u, int) and n == 1):
                        pe.wait_ge(o_ready, n - 1)
                project("k", r, u, h, b, ko_bank, cT_hi, cT_lo, k_done)

            def project_v(r, u, h, b):
                pe.wait_ge(q_ready, UNITS * r + u + 1)
                project("v", r, u, h, b, qv_bank, cT_hi, cT_lo, v_done)

            def turn_x(r, i):
                if i == 1:
                    pe.wait_ge(ln.lo_ready, TB * (2 * r + 1))
                ln.tensor_turn(pe, 2 * r + i)

            def turn_ctx(r, i, half):
                m = 2 * r + i
                pe.wait_ge(c_in[i], 16 * (r + 1))
                for t in (2 * half, 2 * half + 1):
                    if half or i:
                        pe.wait_ge(c_lo_ready, TB * m + t - 1)
                    for k in range(KD):
                        ins = pe.transpose(out_bank[t % 2][:, k * P:(k + 1) * P], c_raw[:, i, t, k * P:(k + 1) * P],
                                           ident[:, :])
                    ins.then_inc(c_turned, 1)

            def turn_v(r, u):
                n = UNITS * r + u
                pe.wait_ge(vT_ready, n + 1)
                for t in range(TB):
                    ins = pe.transpose(out_bank[0][:, t * HD:(t + 1) * HD], vT[:, t * P:(t + 1) * P], ident[:, :])
                ins.then_inc(v_turned, 1)

            def output(r, u, h, b):
                n = UNITS * r + u
                if b == 0:
                    pe.wait_ge(w_ready["o"], H * r + h + 1)
                pe.wait_ge(o_ready, n + 1)
                for t in range(TB):
                    if t >= 2:
                        pe.wait_ge(added, n * TB + (t - 1))
                    elif t == 1 and not (isinstance(n, int) and n == 0):
                        pe.wait_ge(added, n * TB)
                    three_pass(pe, out_bank[t % 2][:, :], lambda k: o_hi[:, t * P:(t + 1) * P],
                               lambda k: o_lo[:, t * P:(t + 1) * P], lambda k: w_hi["o"][:, :],
                               lambda k: w_lo["o"][:, :], 1).then_inc(out_done, 1)

            def unit(r, u, h, b, first, last):
                n = UNITS * r + u
                pe.wait_ge(q_ready, n + 1)
                pe.wait_ge(k_ready, n + 1)
                if not first:
                    pe.wait_ge(p_ready, n * TB)
                for t in range(TB):
                    three_pass(pe, score_bank[t][:, :], lambda k: q_hi[:, t * P:(t + 1) * P],
                               lambda k: q_lo[:, t * P:(t + 1) * P], lambda k: k_hi[:, :], lambda k: k_lo[:, :],
                               1).then_inc(scored, 1)
                pe.wait_ge(v_ready, n + 1)
                nh, nb = (h, 1) if b == 0 else (h + 1, 0)
                if not last:
                    project_q(r, u + 1, nh, nb)
                if not first:
                    output(r, u - 1, h if b == 1 else h - 1, 1 - b)
                if not last:
                    project_k(r, u + 1, nh, nb)
                for t in range(TB):
                    pe.wait_ge(probs_ready, n * TB + (t + 1))
                    for k in range(TB):
                        ins = pe.transpose(score_bank[t][:, k * P:(k + 1) * P], probs[:, t, k * P:(k + 1) * P],
                                           ident[:, :])
                    ins.then_inc(p_turned, 1)
                if not last:
                    project_v(r, u + 1, nh, nb)
                    pe.wait_ge(k_ready, n + 2)
                pe.wait_ge(p_ready, (n + 1) * TB)
                three_pass(pe, ko_bank[:, :], lambda k: v_hi[:, k, :], lambda k: v_lo[:, k, :],
                           lambda k: pT_hi[:, k, :], lambda k: pT_lo[:, k, :], TB).then_inc(o_done, 1)
                if not last:
                    if not first:
                        pe.wait_ge(added, n * TB - 1)
                    turn_v(r, u + 1)

            for r in range(PAIRS):
                if r > 0:
                    pe.wait_ge(added, UNITS * r * TB)
                    pe.wait_ge(p_ready, UNITS * r * TB)
                turn_x(r, 0)
                turn_ctx(r, 0, 0)
                pe.wait_ge(ln.lo_ready, TB * (2 * r + 1))
                project_q(r, 0, 0, 0)
                turn_ctx(r, 0, 1)
                pe.wait_ge(c_lo_ready, TB * (2 * r + 1))
                project_k(r, 0, 0, 0)
                turn_x(r, 1)
                turn_ctx(r, 1, 0)
                project_v(r, 0, 0, 0)
                turn_ctx(r, 1, 1)
                pe.wait_ge(c_lo_ready, TB * (2 * r + 2))
                turn_v(r, 0)
                pe.wait_ge(ln.lo_ready, TB * (2 * r + 2))
                unit(r, 0, 0, 0, True, False)
                unit(r, 1, 0, 1, False, False)
                with pe.Fori(1, H - 1) as h:
                    unit(r, 2 * h, h, 0, False, False)
                    unit(r, 2 * h + 1, h, 1, False, False)
                unit(r, UNITS - 2, H - 1, 0, False, False)
                unit(r, UNITS - 1, H - 1, 1, False, True)
                output(r, UNITS - 1, H - 1, 1)


def hadamard_ffn_phase(nc, W1, W3, W2_scratch, x_res, ident, had, stats, out):
    with ExitStack() as ctx:
        al = Alloc(nc, ctx, "f")
        xT_hi = al.sb("xT_hi", [KD, B * S], F32R)
        xT_lo = al.sb("xT_lo", [KD, B * S], F32R)
        raw = [al.sb("w1_raw", [KG, D]), al.sb("w3_raw", [KG, D])]
        w2_raw = al.sb("w2_raw", [KD, GH])
        up_hi = [[al.sb(f"w{n}_hi{i}", [KD, GH], F32R) for n in (1, 3)] for i in range(2)]
        up_lo = [[al.sb(f"w{n}_lo{i}", [KD, GH], F32R) for n in (1, 3)] for i in range(2)]
        w2T_hi, w2T_lo = al.sb("w2T_hi", [KG, D], F32R), al.sb("w2T_lo", [KG, D], F32R)
        down_hi, down_lo = al.sb("down_hi", [2, KG, D], F32R), al.sb("down_lo", [2, KG, D], F32R)
        silu = al.sb("silu", [KG, S])
        mid_hi, mid_lo = al.sb("mid_hi", [2, KG, S], F32R), al.sb("mid_lo", [2, KG, S], F32R)
        gate_bank = [al.ps(f"gate{k}", [S]) for k in range(KG)]
        lin_bank = [al.ps(f"lin{k}", [S]) for k in range(KG)]
        down_bank = [al.ps(f"down{t}", [D]) for t in range(TB)]
        ln = LayerNorm(al, stats, ident, [*gate_bank, *lin_bank], down_bank[KG:])
        sem = al.sem
        w1_in, w3_in, w2_in = sem("w1_in"), sem("w3_in"), sem("w2_in")
        prep_turned = sem("prep_turned")
        prep_hi_ready = sem("prep_hi_ready")
        prep_ready = sem("prep_ready")
        gate_done, lin_done = sem("gate_done"), sem("lin_done")
        silu_ready = sem("silu_ready")
        mid_done = sem("mid_done")
        mid_hi_ready = sem("mid_hi_ready")
        mid_ready = sem("mid_ready")
        down_done = sem("down_done")
        added = sem("added")
        stored = sem("stored")
        block = ctx.enter_context(nc.Block())

        PREP = 4 * KG
        FWHT_SCALE = float(FH) ** -0.5
        fourths = lambda bank: bank[:, :].rearrange("p (k t) -> p k t", k=KD)

        def prep_dst(i, j, part):
            kind, k = j // KG, j % KG
            if kind < 2:
                return (up_hi, up_lo)[part][i][kind][:, :, k * P:(k + 1) * P]
            if kind == 2:
                return (w2T_hi, w2T_lo)[part][:, k, :]
            return (down_hi, down_lo)[part][:, i, k, :]


        @block.sync
        def _(sp):
            src1 = W1.rearrange("(g k p) d -> g p k d", k=KG, p=P)
            src3 = W3.rearrange("(g k p) d -> g p k d", k=KG, p=P)
            src2 = W2_scratch.rearrange("(c p) (g n) -> g p c n", p=P, n=GH)

            def load(g, first):
                pick = (lambda a: a[g]) if first else (lambda a: a[bass.ds(g, 1)])
                if not first:
                    sp.wait_ge(prep_turned, (g - 1) * PREP + KG)
                sp.dma_start(raw[0][:, :, :], pick(src1)).then_inc(w1_in, 16)
                if not first:
                    sp.wait_ge(prep_turned, (g - 1) * PREP + 2 * KG)
                sp.dma_start(raw[1][:, :, :], pick(src3)).then_inc(w3_in, 16)
                if not first:
                    sp.wait_ge(prep_turned, (g - 1) * PREP + 3 * KG)
                sp.dma_start(w2_raw[:, :, :], pick(src2)).then_inc(w2_in, 16)

            load(0, True)
            with sp.Fori(1, NG) as g:
                load(g, False)
            for b in range(B):
                sp.wait_ge(added, (NG - 1) * B * TB + (b + 1) * TB)
                sp.dma_start(out[b].rearrange("(t p) d -> p t d", p=P), x_res[:, TB * b:TB * b + TB, :]
                             ).then_inc(stored, 16)
            sp.wait_ge(stored, 16 * B)


        @block.scalar
        def _(act):
            def prepare(g, i, j):
                act.wait_ge(prep_turned, g * PREP + (j + 1))
                bank = down_bank[j % KG]
                if j < 2 * KG:
                    act.activation(prep_dst(i, j, 0), fourths(bank), ACT.Copy).then_inc(prep_hi_ready, 1)
                else:
                    act.activation(prep_dst(i, j, 0), bank[:, :], ACT.Copy,
                                   scale=FWHT_SCALE if j >= 3 * KG else 1.0).then_inc(prep_hi_ready, 1)

            def unit(u, b):
                for k in range(KG):
                    act.wait_ge(gate_done, u * KG + (k + 1))
                    if not (isinstance(u, int) and u == 0):
                        act.wait_ge(mid_done, (u - 1) * KG + (k + 1))
                    act.activation(silu[:, k, :], gate_bank[k][:, :], ACT.Silu).then_inc(silu_ready, 1)
                for k in range(KG):
                    act.wait_ge(mid_done, u * KG + (k + 1))
                    act.activation(mid_hi[:, b % 2, k, :], lin_bank[k][:, :], ACT.Copy).then_inc(mid_hi_ready, 1)

            def group(g, i, last, start=False):
                for b in range(B):
                    if start and b + 1 < B:
                        ln.scalar_hi(act, b + 1, xT_hi, b + 1)
                    if not (last and b == B - 1):
                        unit(g * B + (b + 1), b + 1)
                    if not last:
                        prepare(g + 1, 1 - i, 2 * b)
                        prepare(g + 1, 1 - i, 2 * b + 1)

            ln.scalar_hi(act, 0, xT_hi, 0)
            for j in range(PREP):
                prepare(0, 0, j)
            unit(0, 0)
            group(0, 0, False, True)
            group(1, 1, False)
            with act.Fori(1, NG // 2 - 1) as n:
                group(2 * n, 0, False)
                group(2 * n + 1, 1, False)
            group(NG - 2, 0, False)
            group(NG - 1, 1, True)

        @block.vector
        def _(dve):
            def prepare(g, i, j):
                dve.wait_ge(prep_hi_ready, g * PREP + (j + 1))
                bank = down_bank[j % KG]
                hi, lo = f32(prep_dst(i, j, 0)), prep_dst(i, j, 1)
                if j < 2 * KG:
                    dve.tensor_tensor(lo, fourths(bank), hi, ALU.subtract).then_inc(prep_ready, 1)
                else:
                    dve.scalar_tensor_tensor(out=lo, in0=bank[:, :], scalar=FWHT_SCALE if j >= 3 * KG else 1.0,
                                             in1=hi, op0=ALU.mult, op1=ALU.subtract).then_inc(prep_ready, 1)

            def unit(u, b):
                for k in range(KG):
                    dve.wait_ge(silu_ready, u * KG + (k + 1))
                    dve.wait_ge(lin_done, u * KG + (k + 1))
                    dve.tensor_tensor(lin_bank[k][:, :], lin_bank[k][:, :], silu[:, k, :],
                                      ALU.mult).then_inc(mid_done, 1)
                for k in range(KG):
                    dve.wait_ge(mid_hi_ready, u * KG + (k + 1))
                    dve.tensor_tensor(mid_lo[:, b % 2, k, :], lin_bank[k][:, :], f32(mid_hi[:, b % 2, k, :]),
                                      ALU.subtract).then_inc(mid_ready, 1)

            def group(g, i, last, start=False):
                for b in range(B):
                    if start and b + 1 < B:
                        ln.vector_lo(dve, b + 1, xT_hi, xT_lo, b + 1)
                        if b == 0:
                            stats.compute(dve, B - 1)
                        if b + 2 < B:
                            ln.vector_norm(dve, b + 2, b + 2)
                    if not (last and b == B - 1):
                        unit(g * B + (b + 1), b + 1)
                    for t in range(TB):
                        dve.wait_ge(down_done, g * (B * TB) + (b * TB + t + 1))
                        x_tile = x_res[:, TB * b + t, :]
                        dve.tensor_tensor(x_tile, down_bank[t][:, :], x_tile, ALU.add).then_inc(added, 1)
                    if not last:
                        prepare(g + 1, 1 - i, 2 * b)
                        prepare(g + 1, 1 - i, 2 * b + 1)

            ln.vector_norm(dve, 0, 0)
            ln.vector_lo(dve, 0, xT_hi, xT_lo, 0)
            for j in range(2 * KG):
                prepare(0, 0, j)
            ln.vector_norm(dve, 1, 1)
            for j in range(2 * KG, PREP):
                prepare(0, 0, j)
            unit(0, 0)
            group(0, 0, False, True)
            group(1, 1, False)
            with dve.Fori(1, NG // 2 - 1) as n:
                group(2 * n, 0, False)
                group(2 * n + 1, 1, False)
            group(NG - 2, 0, False)
            group(NG - 1, 1, True)

        @block.tensor
        def _(pe):
            def prepare(g, i, j, unit_before):
                kind, k = j // KG, j % KG
                bank = down_bank[j % KG]
                if unit_before is not None:
                    pe.wait_ge(added, unit_before * TB + (k + 1))
                elif j >= KG:
                    pe.wait_ge(prep_ready, j - KG + 1)
                if kind < 2:
                    pe.wait_ge((w1_in, w3_in)[kind], (g + 1) * 16)
                    for c in range(KD):
                        ins = pe.transpose(bank[:, c * P:(c + 1) * P], raw[kind][:, k, c * P:(c + 1) * P], ident[:, :])
                elif kind == 2:
                    pe.wait_ge(w2_in, (g + 1) * 16)
                    for c in range(KD):
                        ins = pe.transpose(bank[:, c * P:(c + 1) * P], w2_raw[:, c, k * P:(k + 1) * P], ident[:, :])
                else:
                    pe.wait_ge(prep_ready, g * PREP + (2 * KG + k + 1))
                    pe.matmul(bank[:, :], had[:, :], w2T_hi[:, k, :], start=True, stop=False)
                    ins = pe.matmul(bank[:, :], had[:, :], w2T_lo[:, k, :], start=False, stop=True)
                ins.then_inc(prep_turned, 1)

            def up(u, g, i, b):
                cols = slice(b * S, (b + 1) * S)
                if b == 0:
                    pe.wait_ge(prep_ready, g * PREP + 2 * KG)
                for k in range(KG):
                    ks = slice(k * P, (k + 1) * P)
                    if not (isinstance(u, int) and u == 0):
                        pe.wait_ge(mid_ready, (u - 1) * KG + (k + 1))
                    for kind, bank, done in ((0, gate_bank[k], gate_done), (1, lin_bank[k], lin_done)):
                        three_pass(pe, bank[:, :], lambda c: up_hi[i][kind][:, c, ks],
                                   lambda c: up_lo[i][kind][:, c, ks], lambda c: xT_hi[:, c, cols],
                                   lambda c: xT_lo[:, c, cols], KD).then_inc(done, 1)

            def group(g, i, start, last):
                for b in range(B):
                    u = g * B + b
                    if start and b + 1 < B:
                        if b > 0:
                            pe.wait_ge(added, b * TB)
                        ln.tensor_turn(pe, b + 1)
                        pe.wait_ge(ln.lo_ready, TB * (b + 2))
                    if b + 1 < B:
                        up(u + 1, g, i, b + 1)
                    elif not last:
                        up(u + 1, g + 1, 1 - i, 0)
                    if b == 0:
                        pe.wait_ge(prep_ready, (g + 1) * PREP)
                    pe.wait_ge(mid_ready, (u + 1) * KG)
                    for t in range(TB):
                        if t < KG and b > 0 and not last:
                            pe.wait_ge(prep_ready, (g + 1) * PREP + (2 * (b - 1) + t + 1))
                        if not (start and b == 0):
                            pe.wait_ge(added, (u - 1) * TB + (t + 1))
                        ts = slice(t * P, (t + 1) * P)
                        three_pass(pe, down_bank[t][:, :], lambda k: mid_hi[:, b % 2, k, ts],
                                   lambda k: mid_lo[:, b % 2, k, ts], lambda k: down_hi[:, i, k, :],
                                   lambda k: down_lo[:, i, k, :], KG).then_inc(down_done, 1)
                    if not last:
                        prepare(g + 1, 1 - i, 2 * b, u)
                        prepare(g + 1, 1 - i, 2 * b + 1, u)

            ln.tensor_turn(pe, 0)
            for j in range(2 * KG):
                prepare(0, 0, j, None)
            pe.wait_ge(ln.lo_ready, TB)
            up(0, 0, 0, 0)
            for j in range(2 * KG, PREP):
                prepare(0, 0, j, None)
            group(0, 0, True, False)
            group(1, 1, False, False)
            with pe.Fori(1, NG // 2 - 1) as n:
                group(2 * n, 0, False, False)
                group(2 * n + 1, 1, False, False)
            group(NG - 2, 0, False, False)
            group(NG - 1, 1, False, True)


def build(nc, x, ctx_in, bias, Wsh_up, Wsh_down, Wrt_up, Wrt_down, W_router, Wq, Wk, Wv, Wo, W1, W2, W3, consts, out):
    W2_scratch = nc.dram_tensor("W2_outer_hadamard", (D, FH), F32, kind="Internal").ap()
    with ExitStack() as ctx:
        x_res = ctx.enter_context(nc.sbuf_tensor("x_res", [P, NT, D], F32))
        ident = ctx.enter_context(nc.sbuf_tensor("ident", [P, P], F32))
        had = ctx.enter_context(nc.sbuf_tensor("had", [P, P], F32R))
        stats = RowStats(nc, ctx, x_res)
        batch_product_phase(nc, x, ctx_in, bias, consts, x_res, ident, had, stats)
        experts_phase(nc, Wsh_up, Wsh_down, Wrt_up, Wrt_down, W_router, W2, W2_scratch, x_res, ident, stats)
        attention_phase(nc, ctx_in, Wq, Wk, Wv, Wo, x_res, ident, stats)
        hadamard_ffn_phase(nc, W1, W3, W2_scratch, x_res, ident, had, stats, out)


_INS = ["x", "ctx_2048", "mask_Bx1xS2_ff0", "L0_ffn_Wsh_up", "L0_ffn_Wsh_down", "L0_ffn_Wrt_up", "L0_ffn_Wrt_down",
        "L0_ffn_W_router", "L1_xattn_Wq", "L1_xattn_Wk", "L1_xattn_Wv", "L1_xattn_Wo", "L1_ffn_W1", "L1_ffn_W2",
        "L1_ffn_W3"]


def kernel(**inputs):
    import numpy as np
    import concourse.bacc as bacc
    from concourse import mybir as mb
    from concourse.bass_utils import run_bass_kernel_spmd

    hadamard = np.ones((1, 1), np.float32)
    while hadamard.shape[0] < 128:
        hadamard = np.block([[hadamard, hadamard], [hadamard, -hadamard]])
    consts = np.stack([np.eye(128, dtype=np.float32), hadamard.astype(np.float32)])

    nc = bacc.Bacc("TRN2", target_bir_lowering=False, num_devices=1)
    arrays, args = {}, []
    for name, a in [(n, inputs[n]) for n in _INS] + [("consts", consts)]:
        a = np.ascontiguousarray(a)
        arrays[f"in_{name}_dram"] = a
        args.append(nc.dram_tensor(f"in_{name}_dram", a.shape, mb.dt.from_np(a.dtype), kind="ExternalInput").ap())
    out = nc.dram_tensor("out_0_dram", (4, 512, 512), mb.dt.float32, kind="ExternalOutput").ap()
    build(nc, *args, out)
    r = run_bass_kernel_spmd(nc, [arrays], core_ids=[0])
    return r.results[0]["out_0_dram"]
```

```python
from contextlib import ExitStack

import concourse.bass as bass
from concourse import mybir

F32 = mybir.dt.float32
F32R = mybir.dt.float32r
BF16 = mybir.dt.bfloat16
U32 = mybir.dt.uint32
ALU = mybir.AluOpType
ACT = mybir.ActivationFunctionType
AX = mybir.AxisListType

P = 128
B, S, D = 4, 512, 512
KD = D // P
TB = S // P
NT = B * TB
EPS = 1e-5
RSQRT_BITS = 0x5F375A86

FP8_MAX = 448.0
FP8_AMAX_EPS = 1e-12
FP8_MIN_NORMAL = 2.0 ** -6
ROUND_MAGIC = 1.5 * 2.0 ** 20
EXPONENT_BITS = 0x7F800000

E_SH, E_RT, DE = 2, 16, 256
E_ALL = E_SH + E_RT
KE = DE // P
H, HD = 16, 128
PAIRS = B // 2
FH = 2048
GH = 256
KG = GH // P
NG = FH // GH


def three_pass(pe, out, w_hi, w_lo, x_hi, x_lo, k_tiles):
    for k in range(k_tiles):
        for j, (w, x) in enumerate(((w_hi, x_hi), (w_hi, x_lo), (w_lo, x_hi))):
            ins = pe.matmul(out, w(k), x(k), start=(k == 0 and j == 0), stop=(k == k_tiles - 1 and j == 2))
    return ins


def f32(ap):
    return ap.bitcast(F32)


class Alloc:

    def __init__(self, nc, ctx, tag):
        self.nc, self.ctx, self.tag = nc, ctx, tag

    def sb(self, name, shape, dt=F32):
        return self.ctx.enter_context(self.nc.sbuf_tensor(f"{self.tag}_{name}", [P] + shape, dt))

    def ps(self, name, shape, dt=F32):
        return self.ctx.enter_context(self.nc.psum_tensor(f"{self.tag}_{name}", [P] + shape, dt))

    def sem(self, name):
        return self.ctx.enter_context(self.nc.semaphore(f"{self.tag}_{name}"))


class RowStats:

    def __init__(self, nc, ctx, x_res):
        sb = lambda name, shape, dt=F32: ctx.enter_context(nc.sbuf_tensor(name, [P] + shape, dt))
        self.x_res = x_res
        self.raw = sb("row_stats", [NT, 6])
        self.mean_var = sb("mean_var", [NT, 2])
        self.rstd = sb("rstd", [NT])
        self.bits = sb("rstd_bits", [NT], U32)
        self.root = sb("rstd_root", [NT])
        self.work = sb("rstd_work", [NT])
        self.chain = ctx.enter_context(nc.semaphore("row_stats_chain"))
        self.links = 0

    def link(self, dve, ins):
        self.links += 1
        ins.then_inc(self.chain, 1)
        dve.wait_ge(self.chain, self.links)

    def read(self, dve, g):
        for j in range(TB * g, TB * (g + 1)):
            ins = dve.bn_stats(self.raw[:, j, :], self.x_res[:, j, :])
        self.link(dve, ins)

    def finish(self, dve, g, n):
        link = lambda ins: self.link(dve, ins)
        tiles = slice(TB * g, TB * (g + n))
        bits, root, work = self.bits[:, tiles], self.root[:, tiles], self.work[:, tiles]
        for j in range(TB * g, TB * (g + n)):
            ins = dve.bn_aggr(self.mean_var[:, j, :], self.raw[:, j, :])
        link(ins)
        var = self.mean_var[:, tiles, 1]
        link(dve.tensor_scalar(var, var, EPS, None, ALU.add))
        link(dve.tensor_scalar(bits, var.bitcast(U32), 1, None, ALU.logical_shift_right))
        link(dve.tensor_scalar(root.bitcast(U32), bits, -1.0, float(RSQRT_BITS), ALU.mult, ALU.add))
        for step in range(4):
            out = self.rstd[:, tiles] if step == 3 else root
            link(dve.scalar_tensor_tensor(out=work, in0=root, scalar=-0.5, in1=root, op0=ALU.mult, op1=ALU.mult))
            link(dve.tensor_tensor(work, work, var, ALU.mult))
            link(dve.scalar_tensor_tensor(out=out, in0=work, scalar=1.5, in1=root, op0=ALU.add, op1=ALU.mult))

    def compute(self, dve, g, n=1):
        for batch in range(g, g + n):
            self.read(dve, batch)
        self.finish(dve, g, n)


class RawWeights:

    def __init__(self, nc, ctx, shapes, slices):
        self.slices = slices
        self.raw = {n: ctx.enter_context(nc.sbuf_tensor(f"w{n}_raw", [P] + shape, F32)) for n, shape in shapes.items()}
        self.loaded = {n: ctx.enter_context(nc.semaphore(f"w{n}_in")) for n in shapes}

    def load(self, sp, n, index):
        src = self.slices[n]
        sp.dma_start(self.raw[n][:], src[index] if isinstance(index, int) else src[bass.ds(index, 1)]
                     ).then_inc(self.loaded[n], 16)


class LayerNorm:

    def __init__(self, al, stats, ident, banks, later_banks=None):
        self.stats, self.ident, self.banks, self.later_banks = stats, ident, banks, later_banks or banks
        self.xn = al.sb("ln_xn", [TB, D])
        self.xn_ready = al.sem("ln_xn_ready")
        self.turned = al.sem("ln_turned")
        self.hi_ready = al.sem("ln_hi_ready")
        self.lo_ready = al.sem("ln_lo_ready")

    def bank(self, nth, j):
        banks = self.later_banks if nth else self.banks
        return banks[j % len(banks)]

    def vector_norm(self, dve, g, nth):
        if nth > 0:
            dve.wait_ge(self.turned, TB * nth)
        for j in range(TB):
            i = TB * g + j
            dve.tensor_scalar(self.xn[:, j, :], self.stats.x_res[:, i, :], self.stats.mean_var[:, i, 0:1],
                              self.stats.rstd[:, i:i + 1], ALU.subtract, ALU.mult).then_inc(self.xn_ready, 1)

    def tensor_turn(self, pe, nth, tiles=range(TB), bank_free=None):
        for j in tiles:
            n = TB * nth + j
            pe.wait_ge(self.xn_ready, n + 1)
            if bank_free:
                bank_free(j)
            size = len(self.later_banks if nth else self.banks)
            if j >= size:
                pe.wait_ge(self.lo_ready, n - size + 1)
            for k in range(KD):
                ins = pe.transpose(self.bank(nth, j)[:, k * P:(k + 1) * P], self.xn[:, j, k * P:(k + 1) * P],
                                   self.ident[:, :])
            ins.then_inc(self.turned, 1)

    def scalar_hi(self, act, nth, xT_hi, slot, tiles=range(TB)):
        for j in tiles:
            act.wait_ge(self.turned, TB * nth + j + 1)
            c = (TB * slot + j) * P
            act.activation(xT_hi[:, :, c:c + P], self.bank(nth, j)[:, :].rearrange("p (k t) -> p k t", k=KD),
                           ACT.Copy).then_inc(self.hi_ready, 1)

    def vector_lo(self, dve, nth, xT_hi, xT_lo, slot, tiles=range(TB)):
        for j in tiles:
            dve.wait_ge(self.hi_ready, TB * nth + j + 1)
            c = (TB * slot + j) * P
            dve.tensor_tensor(xT_lo[:, :, c:c + P], self.bank(nth, j)[:, :].rearrange("p (k t) -> p k t", k=KD),
                              f32(xT_hi[:, :, c:c + P]), ALU.subtract).then_inc(self.lo_ready, 1)


def batch_product_phase(nc, x, ctx_in, bias, consts, x_res, ident, had, stats):
    with ExitStack() as ctx:
        al = Alloc(nc, ctx, "a")
        raw = al.sb("ctx_raw", [NT, D])
        xn = al.sb("xn", [NT, D])
        scaled = al.sb("scaled", [2, TB, D])
        magic = al.sb("magic", [2, TB, D])
        lifted = al.sb("lifted", [2, TB, D])
        neg_mean = al.sb("neg_mean", [NT])
        xq = al.sb("xq", [TB, D], BF16)
        cq = al.sb("cq", [2, TB, D], BF16)
        xqT = al.sb("xqT", [KD, S], BF16)
        bias_bc = al.sb("bias_bc", [B, D])
        ident_bf = al.sb("ident_bf", [P], BF16)
        had_raw = al.sb("had_raw", [P])
        amax_parts = al.sb("amax_parts", [2, B])
        amax = al.sb("amax", [2])
        amax_all = al.sb("amax_all", [2])
        inv_amax = al.sb("inv_amax", [2])
        scale = al.sb("scale", [2])
        unscale = al.sb("unscale", [2])
        banks = [al.ps(f"out{t}", [D]) for t in range(TB)]
        turn = [al.ps(f"turn{t}", [KD * P], BF16) for t in range(TB)]

        x_in = [al.sem(f"x_in{g}") for g in range(B)]
        c_in = [al.sem(f"c_in{g}") for g in range(B)]
        const_in = al.sem("const_in")
        bias_in = al.sem("bias_in")
        const_ready = al.sem("const_ready")
        chain = al.sem("chain")
        neg_mean_ready = al.sem("neg_mean_ready")
        centred = al.sem("centred")
        xn_ready = al.sem("xn_ready")
        xn_last = al.sem("xn_last")
        biased = al.sem("biased")
        amax_ready = al.sem("amax_ready")
        amax_over = al.sem("amax_over")
        scale_ready = al.sem("scale_ready")
        scaled_ready = al.sem("scaled_ready")
        lifted_ready = al.sem("lifted_ready")
        lowered = al.sem("lowered")
        quant_ready = al.sem("quant_ready")
        turned = al.sem("turned")
        turned_out = al.sem("turned_out")
        product = al.sem("product")
        added = al.sem("added")
        block = ctx.enter_context(nc.Block())
        tiles = lambda a, g: a[g].rearrange("(t p) d -> p t d", p=P)
        BIAS_ORDER = [B - 1, *range(B - 1)]
        quantised = lambda n: cq[:, n // 2 % 2] if n % 2 else xq[:, :, :]

        @block.sync
        def _(sp):
            for g in range(B):
                sp.dma_start(x_res[:, TB * g:TB * g + TB, :], tiles(x, g)).then_inc(x_in[g], 16)
            for g in range(B):
                sp.dma_start(raw[:, TB * g:TB * g + TB, :], tiles(ctx_in, g)).then_inc(c_in[g], 16)
            sp.dma_start(ident[:, :], consts[0]).then_inc(const_in, 16)
            sp.dma_start(had_raw[:, :], consts[1]).then_inc(const_in, 16)
            for b in range(B):
                sp.dma_start(bias_bc[:, b, :], bias[b].partition_broadcast(P)).then_inc(bias_in, 16)

        @block.gpsimd
        def _(pool):
            pool.wait_ge(bias_in, 16 * B)

            def add_bias(b):
                pool.wait_ge(*((xn_ready, b + 1) if b + 1 < B else (xn_last, 1)))
                for t in range(TB):
                    x_tile = x_res[:, TB * b + t, :]
                    ins = pool.tensor_tensor(x_tile, x_tile, bias_bc[:, b, :], ALU.add)
                ins.then_inc(biased, 1)

            for b in BIAS_ORDER[:2]:
                add_bias(b)
            pool.wait_ge(amax_ready, 1)
            nc.gpsimd.partition_all_reduce(amax_all[:, :], amax[:, :], P,
                                           bass.bass_isa.ReduceOp.max).then_inc(amax_over, 1)
            for n in range(2 * B):
                b = n // 2
                if n in (0, 4):
                    add_bias(BIAS_ORDER[2 if n == 0 else 3])
                pool.wait_ge(lifted_ready, n + 1)
                if n % 2 == 0 and b > 0:
                    pool.wait_ge(turned, TB * b)
                if n % 2 == 1 and b > 1:
                    pool.wait_ge(product, TB * (b - 1))
                pool.tensor_tensor(quantised(n), lifted[:, n % 2], magic[:, n % 2], ALU.subtract).then_inc(lowered, 1)

        @block.scalar
        def _(act):
            act.wait_ge(neg_mean_ready, 1)
            for g in range(B - 1):
                batch = range(TB * g, TB * g + TB)
                for i in batch:
                    ins = act.activation(xn[:, i, :], x_res[:, i, :], ACT.Identity, bias=neg_mean[:, i:i + 1])
                ins.then_inc(centred, 1)
                act.wait_ge(centred, g + 1)
                for i in batch:
                    ins = act.activation(xn[:, i, :], xn[:, i, :], ACT.Copy, scale=stats.rstd[:, i:i + 1])
                ins.then_inc(xn_ready, 1)
            act.wait_ge(const_in, 32)
            act.activation(ident_bf[:, :], ident[:, :], ACT.Copy).then_inc(const_ready, 1)
            act.activation(had[:, :], had_raw[:, :], ACT.Copy).then_inc(const_ready, 1)
            act.wait_ge(scale_ready, 1)

            def scale_group(n, src, which):
                if n >= 2:
                    act.wait_ge(lifted_ready, n - 1)
                act.activation(scaled[:, n % 2], src, ACT.Copy,
                               scale=scale[:, which:which + 1]).then_inc(scaled_ready, 1)

            scale_group(0, xn[:, 0:TB, :], 0)
            scale_group(1, raw[:, 0:TB, :], 1)
            for b in range(B):
                if b + 1 < B:
                    scale_group(2 * b + 2, xn[:, TB * b + TB:TB * b + 2 * TB, :], 0)
                    scale_group(2 * b + 3, raw[:, TB * b + TB:TB * b + 2 * TB, :], 1)
                if b > 0:
                    act.wait_ge(product, TB * b)
                for t in range(TB):
                    act.wait_ge(turned, TB * b + t + 1)
                    act.activation(xqT[:, :, t * P:(t + 1) * P], turn[t].rearrange("p (k t) -> p k t", k=KD),
                                   ACT.Copy).then_inc(turned_out, 1)

        @block.vector
        def _(dve):
            links = [0]

            def link(ins):
                links[0] += 1
                ins.then_inc(chain, 1)
                dve.wait_ge(chain, links[0])

            def batch_amax(which, values, g):
                return dve.tensor_reduce(amax_parts[:, which, g:g + 1], values[:, TB * g:TB * g + TB, :], AX.XY,
                                         ALU.max, apply_absolute_value=True)

            for g in range(B):
                dve.wait_ge(x_in[g], 16)
                stats.read(dve, g)
            stats.finish(dve, 0, B)
            dve.tensor_scalar(neg_mean[:, :], stats.mean_var[:, :, 0], -1.0, None, ALU.mult).then_inc(neg_mean_ready, 1)
            for i in range(TB * (B - 1), TB * B):
                ins = dve.tensor_scalar(xn[:, i, :], x_res[:, i, :], stats.mean_var[:, i, 0:1],
                                        stats.rstd[:, i:i + 1], ALU.subtract, ALU.mult)
            ins.then_inc(xn_last, 1)
            for g in range(B):
                dve.wait_ge(c_in[g], 16)
                batch_amax(1, raw, g)
            dve.wait_ge(xn_last, 1)
            batch_amax(0, xn, B - 1)
            for g in range(B - 1):
                dve.wait_ge(xn_ready, g + 1)
                ins = batch_amax(0, xn, g)
            link(ins)
            dve.tensor_reduce(amax[:, :], amax_parts[:, :, :], AX.X, ALU.max).then_inc(amax_ready, 1)
            dve.wait_ge(amax_over, 1)
            link(dve.tensor_scalar(amax[:, :], amax_all[:, :], FP8_AMAX_EPS, None, ALU.max))
            link(dve.reciprocal(inv_amax[:, :], amax[:, :]))
            dve.tensor_scalar(scale[:, :], inv_amax[:, :], FP8_MAX, None, ALU.mult).then_inc(scale_ready, 1)
            dve.wait_ge(scale_ready, 1)
            link(dve.tensor_tensor(unscale[:, 0:1], scale[:, 0:1], scale[:, 1:2], ALU.mult))
            link(dve.reciprocal(unscale[:, 1:2], unscale[:, 0:1]))

            def lift(n):
                y, m = scaled[:, n % 2], magic[:, n % 2]
                dve.wait_ge(scaled_ready, n + 1)
                if n >= 2:
                    dve.wait_ge(lowered, n - 1)
                link(dve.tensor_scalar(m.bitcast(U32), y.bitcast(U32), EXPONENT_BITS, None, ALU.bitwise_and))
                link(dve.tensor_scalar(m, m, FP8_MIN_NORMAL, ROUND_MAGIC, ALU.max, ALU.mult))
                dve.tensor_tensor(lifted[:, n % 2], y, m, ALU.add).then_inc(lifted_ready, 1)

            def clip(n):
                dve.wait_ge(lowered, n + 1)
                dve.tensor_scalar(quantised(n), quantised(n), FP8_MAX, -FP8_MAX, ALU.min,
                                  ALU.max).then_inc(quant_ready, 1)

            def add(b):
                dve.wait_ge(biased, BIAS_ORDER.index(b) + 1)
                for t in range(TB):
                    i = TB * b + t
                    dve.wait_ge(product, i + 1)
                    dve.scalar_tensor_tensor(out=x_res[:, i, :], in0=banks[t][:, :], scalar=unscale[:, 1:2],
                                             in1=x_res[:, i, :], op0=ALU.mult, op1=ALU.add).then_inc(added, 1)

            lift(0)
            for n in range(1, 2 * B):
                lift(n)
                clip(n - 1)
                if n >= 4 and n % 2 == 0:
                    add(n // 2 - 2)
                    dve.wait_ge(added, TB * (n // 2 - 1))
                    stats.read(dve, n // 2 - 2)
            add(B - 2)
            dve.wait_ge(added, TB * (B - 1))
            stats.read(dve, B - 2)
            clip(2 * B - 1)
            stats.finish(dve, 0, B - 1)
            add(B - 1)

        @block.tensor
        def _(pe):
            pe.wait_ge(const_ready, 2)
            for b in range(B):
                pe.wait_ge(quant_ready, 2 * b + 1)
                for t in range(TB):
                    if b > 0:
                        pe.wait_ge(turned_out, TB * (b - 1) + t + 1)
                    for k in range(KD):
                        ins = pe.transpose(turn[t][:, k * P:(k + 1) * P], xq[:, t, k * P:(k + 1) * P], ident_bf[:, :])
                    ins.then_inc(turned, 1)
                pe.wait_ge(turned_out, TB * (b + 1))
                pe.wait_ge(quant_ready, 2 * b + 2)
                for t in range(TB):
                    if b > 0:
                        pe.wait_ge(added, TB * (b - 1) + t + 1)
                    for k in range(KD):
                        ins = pe.matmul(banks[t][:, :], xqT[:, k, t * P:(t + 1) * P], cq[:, b % 2, k, :],
                                        start=(k == 0), stop=(k == KD - 1))
                    ins.then_inc(product, 1)


def experts_phase(nc, Wsh_up, Wsh_down, Wrt_up, Wrt_down, W_router, W2, W2_scratch, x_res, ident, stats, head_weights):
    with ExitStack() as ctx:
        al = Alloc(nc, ctx, "e")
        xT_hi = al.sb("xT_hi", [KD, B * S], F32R)
        xT_lo = al.sb("xT_lo", [KD, B * S], F32R)
        up_raw = al.sb("up_raw", [2, KD, DE])
        up_hi = al.sb("up_hi", [2, KD, DE], F32R)
        up_lo = al.sb("up_lo", [2, KD, DE], F32R)
        down_raw = al.sb("down_raw", [2, KE, D])
        down_hi = al.sb("down_hi", [2, KE, D], F32R)
        down_lo = al.sb("down_lo", [2, KE, D], F32R)
        router_raw = al.sb("router_raw", [KD, E_RT])
        router_hi = al.sb("router_hi", [KD, E_RT], F32R)
        router_lo = al.sb("router_lo", [KD, E_RT], F32R)
        mid_hi = al.sb("mid_hi", [2, KE, S], F32R)
        mid_lo = al.sb("mid_lo", [2, KE, S], F32R)
        zeros = al.sb("zeros", [KD])
        gates = al.sb("gates", [NT, E_ALL])
        w2a = al.sb("w2a", [FH])
        w2b = al.sb("w2b", [FH])
        logits = al.sb("logits", [NT, E_RT])
        probs = al.sb("probs", [NT, E_RT])
        rest = al.sb("rest", [NT, E_RT])
        first = al.sb("first", [NT, E_RT])
        score = al.sb("score", [NT, E_RT])
        rank = al.sb("rank", [NT, E_RT])
        top = al.sb("top", [NT])
        inv = al.sb("inv", [NT])
        logitsT = al.sb("logitsT", [S])
        up_bank = [[al.ps(f"up{i}{k}", [S]) for k in range(KE)] for i in range(2)]
        down_bank = [al.ps(f"down{t}", [D]) for t in range(TB)]
        ln = LayerNorm(al, stats, ident, down_bank)
        logitsT_bank = down_bank[0][0:E_RT, :]
        logits_bank = down_bank[1][:, 0:TB * E_RT].rearrange("p (t e) -> p t e", e=E_RT)

        up_in = [al.sem(f"up_in{i}") for i in range(2)]
        down_in = [al.sem(f"down_in{i}") for i in range(2)]
        router_in = al.sem("router_in")
        router_hi_ready = al.sem("router_hi_ready")
        router_ready = al.sem("router_ready")
        up_hi_ready = al.sem("up_hi_ready")
        up_ready = al.sem("up_ready")
        down_hi_ready = al.sem("down_hi_ready")
        down_ready = al.sem("down_ready")
        routed = al.sem("routed")
        logitsT_ready = al.sem("logitsT_ready")
        logits_turned = al.sem("logits_turned")
        logits_ready = al.sem("logits_ready")
        w2_in = al.sem("w2_in")
        w2_step = al.sem("w2_step")
        w2_out = al.sem("w2_out")
        exp_ready = al.sem("exp_ready")
        gate_chain = al.sem("gate_chain")
        shifted = al.sem("shifted")
        zeros_ready = al.sem("zeros_ready")
        rank_ready = al.sem("rank_ready")
        up_done = al.sem("up_done")
        gelu_ready = al.sem("gelu_ready")
        mid_hi_ready = al.sem("mid_hi_ready")
        mid_ready = al.sem("mid_ready")
        down_done = al.sem("down_done")
        added = al.sem("added")

        block = ctx.enter_context(nc.Block())
        rows = lambda a: a.rearrange("(k p) n -> p k n", p=P)

        @block.sync
        def _(sp):
            sp.dma_start(router_raw[:, :, :], rows(W_router)).then_inc(router_in, 16)
            for i in range(E_SH):
                sp.dma_start(up_raw[:, i], rows(Wsh_up[i])).then_inc(up_in[i], 16)
                sp.dma_start(down_raw[:, i], rows(Wsh_down[i])).then_inc(down_in[i], 16)
            for name in "qkvo":
                head_weights.load(sp, name, 0)
            up_flat = Wrt_up.rearrange("(n i) (k p) m -> n i p k m", i=2, p=P)
            down_flat = Wrt_down.rearrange("(n i) (k p) m -> n i p k m", i=2, p=P)
            with sp.Fori(0, E_RT // 2) as n:
                for i in range(2):
                    sp.wait_ge(up_ready, 2 * n + (i + 1))
                    sp.dma_start(up_raw[:, i], up_flat[bass.ds(n, 1), i]).then_inc(up_in[i], 16)
                    sp.wait_ge(down_ready, 2 * n + (i + 1))
                    sp.dma_start(down_raw[:, i], down_flat[bass.ds(n, 1), i]).then_inc(down_in[i], 16)
            sp.wait_ge(w2_out, 16 * (D // P))

        @block.gpsimd
        def _(pool):
            for e in range(E_RT):
                ins = pool.memset(rank[:, :, e:e + 1], float(E_RT - e))
            ins.then_inc(rank_ready, 1)
            pool.memset(zeros[:, :], 0.0).then_inc(zeros_ready, 1)
            pool.wait_ge(zeros_ready, 1)
            pool.wait_ge(router_in, 16)
            pool.tensor_copy(router_hi[:, :, :], router_raw[:, :, :]).then_inc(router_hi_ready, 1)
            pool.wait_ge(router_hi_ready, 1)
            pool.tensor_tensor(router_lo[:, :, :], router_raw[:, :, :], f32(router_hi[:, :, :]),
                               ALU.subtract).then_inc(router_ready, 1)

            zero = zeros[:, :].unsqueeze(2)

            def split(n, i, reused):
                pool.wait_ge(up_in[i], 16 * n + 16)
                if reused:
                    pool.wait_ge(up_done, (2 * n + i - 1) * (B * KE))
                pool.tensor_tensor(up_hi[:, i], up_raw[:, i], zero.to_broadcast([P, KD, DE]), ALU.add).then_inc(up_hi_ready, 1)
                pool.wait_ge(up_hi_ready, 2 * n + (i + 1))
                pool.tensor_tensor(up_lo[:, i], up_raw[:, i], f32(up_hi[:, i]), ALU.subtract).then_inc(up_ready, 1)
                pool.wait_ge(down_in[i], 16 * n + 16)
                if reused:
                    pool.wait_ge(down_done, (2 * n + i - 1) * (B * TB))
                pool.tensor_tensor(down_hi[:, i], down_raw[:, i], zero[:, 0:KE].to_broadcast([P, KE, D]), ALU.add).then_inc(down_hi_ready, 1)
                pool.wait_ge(down_hi_ready, 2 * n + (i + 1))
                pool.tensor_tensor(down_lo[:, i], down_raw[:, i], f32(down_hi[:, i]),
                                   ALU.subtract).then_inc(down_ready, 1)

            def butterflies(c):
                if c > 0:
                    pool.wait_ge(w2_out, 16 * c)
                pool.dma_start(w2a[:, :], W2[c * P:(c + 1) * P, :]).then_inc(w2_in, 16)
                pool.wait_ge(w2_in, 16 * (c + 1))
                src, dst = w2a, w2b
                for s in range(4):
                    span = P << s
                    halves = lambda a, h: a[:, :].rearrange("p (n h s) -> p n h s", h=2, s=span)[:, :, h, :]
                    if s > 0:
                        pool.wait_ge(w2_step, 8 * c + 2 * s)
                    pool.tensor_tensor(halves(dst, 0), halves(src, 0), halves(src, 1), ALU.add).then_inc(w2_step, 1)
                    pool.tensor_tensor(halves(dst, 1), halves(src, 0), halves(src, 1),
                                       ALU.subtract).then_inc(w2_step, 1)
                    src, dst = dst, src
                pool.wait_ge(w2_step, 8 * (c + 1))
                pool.dma_start(W2_scratch[c * P:(c + 1) * P, :], w2a[:, :]).then_inc(w2_out, 16)

            for i in range(2):
                split(0, i, False)
            for c in range(D // P):
                for i in range(2):
                    split(c + 1, i, True)
                butterflies(c)
            with pool.Fori(D // P + 1, E_ALL // 2) as n:
                for i in range(2):
                    split(n, i, True)

        @block.scalar
        def _(act):
            def unit(n, i, b):
                u = 2 * n * B + (i * B + b)
                for k in range(KE):
                    act.wait_ge(up_done, u * KE + (k + 1))
                    bank = up_bank[b % 2][k]
                    act.activation(bank[:, :], bank[:, :], ACT.Gelu).then_inc(gelu_ready, 1)
                    act.wait_ge(gelu_ready, u * KE + (k + 1))
                    act.activation(mid_hi[:, b % 2, k], bank[:, :], ACT.Copy).then_inc(mid_hi_ready, 1)

            for b in range(B):
                ln.scalar_hi(act, b, xT_hi, b)
                act.wait_ge(routed, b + 1)
                act.activation(logitsT[0:E_RT, :], logitsT_bank, ACT.Copy).then_inc(logitsT_ready, 1)
                unit(0, 0, b)
                act.wait_ge(logits_turned, b + 1)
                act.activation(logits[:, TB * b:TB * (b + 1), :], logits_bank, ACT.Copy).then_inc(logits_ready, 1)
            act.wait_ge(shifted, 1)
            act.activation(probs[:, :, :], probs[:, :, :], ACT.Exp).then_inc(exp_ready, 1)
            for b in range(B):
                unit(0, 1, b)
            with act.Fori(1, E_ALL // 2) as n:
                for i in range(2):
                    for b in range(B):
                        unit(n, i, b)

        @block.vector
        def _(dve):
            links = [0]

            def link(ins):
                links[0] += 1
                ins.then_inc(gate_chain, 1)
                dve.wait_ge(gate_chain, links[0])

            wide = lambda a: a[:, :].unsqueeze(2).to_broadcast([P, NT, E_RT])
            def routing():
                dve.wait_ge(logits_ready, B)
                link(dve.tensor_reduce(top[:, :], logits[:, :, :], AX.X, ALU.max))
                dve.tensor_tensor(probs[:, :, :], logits[:, :, :], wide(top), ALU.subtract).then_inc(shifted, 1)
                dve.wait_ge(exp_ready, 1)
                link(dve.tensor_reduce(top[:, :], probs[:, :, :], AX.X, ALU.add))
                link(dve.reciprocal(inv[:, :], top[:, :]))
                link(dve.tensor_tensor(probs[:, :, :], probs[:, :, :], wide(inv), ALU.mult))

                def pick(values, out):
                    link(dve.tensor_reduce(top[:, :], values, AX.X, ALU.max))
                    link(dve.tensor_tensor(score[:, :, :], values, wide(top), ALU.is_equal))
                    link(dve.tensor_tensor(score[:, :, :], score[:, :, :], rank[:, :, :], ALU.mult))
                    link(dve.tensor_reduce(top[:, :], score[:, :, :], AX.X, ALU.max))
                    link(dve.tensor_tensor(out, score[:, :, :], wide(top), ALU.is_equal))

                dve.wait_ge(rank_ready, 1)
                pick(probs[:, :, :], first[:, :, :])
                link(dve.scalar_tensor_tensor(out=rest[:, :, :], in0=first[:, :, :], scalar=-2.0, in1=probs[:, :, :],
                                              op0=ALU.mult, op1=ALU.add))
                pick(rest[:, :, :], rest[:, :, :])
                link(dve.tensor_tensor(first[:, :, :], first[:, :, :], rest[:, :, :], ALU.add))
                link(dve.tensor_tensor(gates[:, :, E_SH:E_ALL], first[:, :, :], probs[:, :, :], ALU.mult))

            def low(n, i, b):
                u = 2 * n * B + (i * B + b)
                for k in range(KE):
                    dve.wait_ge(mid_hi_ready, u * KE + (k + 1))
                    dve.tensor_tensor(mid_lo[:, b % 2, k], up_bank[b % 2][k][:, :], f32(mid_hi[:, b % 2, k]),
                                      ALU.subtract).then_inc(mid_ready, 1)

            def add(n, i, b):
                u = 2 * n * B + (i * B + b)
                e = 2 * n + i
                for t in range(TB):
                    dve.wait_ge(down_done, u * TB + (t + 1))
                    x_tile = x_res[:, TB * b + t, :]
                    gate = gates[:, TB * b + t, bass.ds(e, 1)]
                    dve.scalar_tensor_tensor(out=x_tile, in0=down_bank[t][:, :], scalar=gate, in1=x_tile,
                                             op0=ALU.mult, op1=ALU.add).then_inc(added, 1)

            def body(n, last):
                for i in range(2):
                    for b in range(B):
                        if b + 1 < B:
                            low(n, i, b + 1)
                        elif i == 0:
                            low(n, 1, 0)
                        elif not last:
                            low(n + 1, 0, 0)
                        add(n, i, b)
                        if last and i == 1 and b < 2:
                            dve.wait_ge(added, (E_ALL * B - B + b + 1) * TB)
                            stats.compute(dve, b)
            link(dve.memset(gates[:, :, 0:E_SH], 1.0))
            ln.vector_norm(dve, 0, 0)
            for b in range(B):
                ln.vector_lo(dve, b, xT_hi, xT_lo, b)
                if b == 1:
                    stats.compute(dve, B - 1)
                if b + 1 < B:
                    ln.vector_norm(dve, b + 1, b + 1)
                low(0, 0, b)
                if b > 0:
                    add(0, 0, b - 1)
            routing()
            low(0, 1, 0)
            add(0, 0, B - 1)
            for b in range(B):
                low(*((0, 1, b + 1) if b + 1 < B else (1, 0, 0)))
                add(0, 1, b)
            with dve.Fori(1, E_ALL // 2 - 1) as n:
                body(n, False)
            body(E_ALL // 2 - 1, True)

        @block.tensor
        def _(pe):
            def route(b):
                if b == 0:
                    pe.wait_ge(router_ready, 1)
                cols = slice(b * S, (b + 1) * S)
                three_pass(pe, logitsT_bank, lambda k: router_hi[:, k, :], lambda k: router_lo[:, k, :],
                           lambda k: xT_hi[:, k, cols], lambda k: xT_lo[:, k, cols], KD).then_inc(routed, 1)

            def turn_logits(b):
                pe.wait_ge(logitsT_ready, b + 1)
                for t in range(TB):
                    ins = pe.transpose(logits_bank[:, t, :], logitsT[0:E_RT, t * P:(t + 1) * P],
                                       ident[0:E_RT, 0:E_RT])
                ins.then_inc(logits_turned, 1)

            def up(n, i, b, reused):
                u = 2 * n * B + (i * B + b)
                cols = slice(b * S, (b + 1) * S)
                if b == 0:
                    pe.wait_ge(up_ready, 2 * n + (i + 1))
                for k in range(KE):
                    if reused:
                        pe.wait_ge(mid_ready, (u - 2) * KE + (k + 1))
                    ks = slice(k * P, (k + 1) * P)
                    three_pass(pe, up_bank[b % 2][k][:, :], lambda c: up_hi[:, i, c, ks], lambda c: up_lo[:, i, c, ks],
                               lambda c: xT_hi[:, c, cols], lambda c: xT_lo[:, c, cols], KD).then_inc(up_done, 1)

            def down(n, i, b, reused, logits=None):
                u = 2 * n * B + (i * B + b)
                if b == 0:
                    pe.wait_ge(down_ready, 2 * n + (i + 1))
                pe.wait_ge(mid_ready, (u + 1) * KE)
                for t in range(TB):
                    if logits is not None and t == 1:
                        pe.wait_ge(logits_ready, logits + 1)
                    if reused:
                        pe.wait_ge(added, (u - 1) * TB + (t + 1))
                    ts = slice(t * P, (t + 1) * P)
                    three_pass(pe, down_bank[t][:, :], lambda k: mid_hi[:, b % 2, k, ts],
                               lambda k: mid_lo[:, b % 2, k, ts], lambda k: down_hi[:, i, k, :],
                               lambda k: down_lo[:, i, k, :], KE).then_inc(down_done, 1)

            def body(n, last):
                for i in range(2):
                    for b in range(B):
                        if b + 1 < B:
                            up(n, i, b + 1, True)
                        elif i == 0:
                            up(n, 1, 0, True)
                        elif not last:
                            up(n + 1, 0, 0, True)
                        down(n, i, b, True)

            for b in range(B):
                if b == 1:
                    pe.wait_ge(logits_ready, 1)
                ln.tensor_turn(pe, b, bank_free=(lambda j: pe.wait_ge(added, TB * (b - 2) + j + 1)) if b > 1 else None)
                pe.wait_ge(ln.lo_ready, TB * (b + 1))
                route(b)
                up(0, 0, b, b > 1)
                turn_logits(b)
                if b > 0:
                    down(0, 0, b - 1, b > 1, b)
            up(0, 1, 0, True)
            down(0, 0, B - 1, True)
            for b in range(B):
                up(*((0, 1, b + 1) if b + 1 < B else (1, 0, 0)), True)
                down(0, 1, b, True)
            with pe.Fori(1, E_ALL // 2 - 1) as n:
                body(n, False)
            body(E_ALL // 2 - 1, True)


def attention_phase(nc, ctx_in, x_res, ident, stats, head_weights, group_weights):
    with ExitStack() as ctx:
        al = Alloc(nc, ctx, "t")
        W = PAIRS * S
        xT_hi = al.sb("xT_hi", [KD, W], F32R)
        xT_lo = al.sb("xT_lo", [KD, W], F32R)
        cT_hi = al.sb("cT_hi", [KD, W], F32R)
        cT_lo = al.sb("cT_lo", [KD, W], F32R)
        c_raw = al.sb("c_raw", [PAIRS, TB, D])
        names = ("q", "k", "v")
        w_raw, w_in = head_weights.raw, head_weights.loaded
        w_hi = {n: al.sb(f"w{n}_hi", [KD, HD], F32R) for n in names}
        w_lo = {n: al.sb(f"w{n}_lo", [KD, HD], F32R) for n in names}
        w_hi["o"] = al.sb("wo_hi", [D], F32R)
        w_lo["o"] = al.sb("wo_lo", [D], F32R)
        q_hi, q_lo = al.sb("q_hi", [S], F32R), al.sb("q_lo", [S], F32R)
        k_hi, k_lo = al.sb("k_hi", [S], F32R), al.sb("k_lo", [S], F32R)
        vT = al.sb("vT", [S])
        v_hi, v_lo = al.sb("v_hi", [TB, HD], F32R), al.sb("v_lo", [TB, HD], F32R)
        probs = al.sb("probs", [TB, S])
        pT_hi, pT_lo = al.sb("pT_hi", [TB, S], F32R), al.sb("pT_lo", [TB, S], F32R)
        o_hi, o_lo = al.sb("o_hi", [S], F32R), al.sb("o_lo", [S], F32R)
        zeros = al.sb("zeros", [KD])
        neg_max, total, inv = al.sb("neg_max", [TB]), al.sb("total", [TB]), al.sb("inv", [TB])
        score_bank = [al.ps(f"score{t}", [S]) for t in range(TB)]
        out_bank = [al.ps(f"out{t}", [D]) for t in range(2)]
        qv_bank = al.ps("qv", [S])
        ko_bank = al.ps("ko", [S])
        ln = LayerNorm(al, stats, ident, score_bank)
        sem = al.sem
        c_in = [sem(f"c_in{i}") for i in range(PAIRS)]
        c_turned = sem("c_turned")
        c_hi_ready, c_lo_ready = sem("c_hi_ready"), sem("c_lo_ready")
        zeros_ready = sem("zeros_ready")
        w_hi_ready = {n: sem(f"w{n}_hi_ready") for n in "qkvo"}
        w_ready = {n: sem(f"w{n}_ready") for n in "qkvo"}
        q_done, k_done, v_done = sem("q_done"), sem("k_done"), sem("v_done")
        q_hi_ready, k_hi_ready = sem("q_hi_ready"), sem("k_hi_ready")
        q_ready, k_ready = sem("q_ready"), sem("k_ready")
        vT_ready = sem("vT_ready")
        v_turned = sem("v_turned")
        v_hi_ready, v_ready = sem("v_hi_ready"), sem("v_ready")
        scored = sem("scored")
        max_ready = sem("max_ready")
        exp_ready = sem("exp_ready")
        inv_ready = sem("inv_ready")
        probs_ready = sem("probs_ready")
        p_turned = sem("p_turned")
        p_hi_ready, p_ready = sem("p_hi_ready"), sem("p_ready")
        o_done = sem("o_done")
        o_hi_ready, o_ready = sem("o_hi_ready"), sem("o_ready")
        out_done = sem("out_done")
        added = sem("added")
        block = ctx.enter_context(nc.Block())

        UNITS = H * 2
        SCALE = float(HD) ** -0.5
        fourths = lambda bank: bank[:, :].rearrange("p (k t) -> p k t", k=KD)


        @block.sync
        def _(sp):
            def load(r, h):
                for n in "qkvo":
                    sp.wait_ge(w_ready[n], H * r + h)
                    head_weights.load(sp, n, h)

            for r in range(PAIRS):
                for i in range(2):
                    if r > 0:
                        sp.wait_ge(c_turned, 2 * TB * (r - 1) + TB * (i + 1))
                    sp.dma_start(c_raw[:, i], ctx_in[2 * r + i].rearrange("(t p) d -> p t d", p=P)).then_inc(c_in[i], 16)
                if r == 0:
                    for name in "132":
                        group_weights.load(sp, name, 0)
                else:
                    load(r, 0)
                with sp.Fori(1, H) as h:
                    load(r, h)

        @block.gpsimd
        def _(pool):
            def split(n, r, h, last_use):
                zero = zeros[:, 0:1].to_broadcast([P, D]) if n == "o" else zeros[:, :].unsqueeze(2).to_broadcast([P, KD, HD])
                pool.wait_ge(w_in[n], (H * r + h + 1) * 16)
                if last_use is not None:
                    pool.wait_ge(*last_use)
                pool.tensor_tensor(w_hi[n][:], w_raw[n][:], zero, ALU.add).then_inc(w_hi_ready[n], 1)
                pool.wait_ge(w_hi_ready[n], H * r + h + 1)
                pool.tensor_tensor(w_lo[n][:], w_raw[n][:], f32(w_hi[n][:]), ALU.subtract).then_inc(w_ready[n], 1)

            def split_all(r, h, first):
                units_before = UNITS * r + h * 2
                for n, done in (("q", q_done), ("k", k_done), ("v", v_done)):
                    split(n, r, h, None if first else (done, units_before))
                split("o", r, h, None if first else (out_done, units_before * TB))

            pool.memset(zeros[:, :], 0.0).then_inc(zeros_ready, 1)
            pool.wait_ge(zeros_ready, 1)
            for r in range(PAIRS):
                split_all(r, 0, r == 0)
                with pool.Fori(1, H) as h:
                    split_all(r, h, False)

        @block.scalar
        def _(act):
            def query(r, u):
                act.wait_ge(q_done, UNITS * r + u + 1)
                act.activation(q_hi[:, :], qv_bank[:, :], ACT.Copy, scale=SCALE).then_inc(q_hi_ready, 1)

            def key(r, u):
                act.wait_ge(k_done, UNITS * r + u + 1)
                act.activation(k_hi[:, :], ko_bank[:, :], ACT.Copy).then_inc(k_hi_ready, 1)

            def values(r, u):
                act.wait_ge(v_done, UNITS * r + u + 1)
                act.activation(vT[:, :], qv_bank[:, :], ACT.Copy).then_inc(vT_ready, 1)

            def values_hi(r, u):
                act.wait_ge(v_turned, UNITS * r + u + 1)
                act.activation(v_hi[:, :, :], out_bank[0][:, :].rearrange("p (t d) -> p t d", t=TB),
                               ACT.Copy).then_inc(v_hi_ready, 1)

            def inputs(r, i, half):
                for t in (2 * half, 2 * half + 1):
                    act.wait_ge(c_turned, TB * (2 * r + i) + t + 1)
                    c = (TB * i + t) * P
                    act.activation(cT_hi[:, :, c:c + P], fourths(out_bank[t % 2]), ACT.Copy).then_inc(c_hi_ready, 1)

            def unit(r, u, last):
                n = UNITS * r + u
                for t in range(TB):
                    act.wait_ge(max_ready, n * TB + (t + 1))
                    act.activation(probs[:, t, :], score_bank[t][:, :], ACT.Exp, bias=neg_max[:, t:t + 1],
                                   accum_out=total[:, t:t + 1]).then_inc(exp_ready, 1)
                act.wait_ge(inv_ready, n + 1)
                for t in range(TB):
                    act.activation(probs[:, t, :], probs[:, t, :], ACT.Copy,
                                   scale=inv[:, t:t + 1]).then_inc(probs_ready, 1)
                if not last:
                    query(r, u + 1)
                    key(r, u + 1)
                for t in range(TB):
                    act.wait_ge(p_turned, n * TB + (t + 1))
                    act.activation(pT_hi[:, :, t * P:(t + 1) * P], fourths(score_bank[t]),
                                   ACT.Copy).then_inc(p_hi_ready, 1)
                if not last:
                    values(r, u + 1)
                act.wait_ge(o_done, n + 1)
                act.activation(o_hi[:, :], ko_bank[:, :], ACT.Copy).then_inc(o_hi_ready, 1)
                if not last:
                    values_hi(r, u + 1)

            for r in range(PAIRS):
                ln.scalar_hi(act, 2 * r, xT_hi, 0)
                inputs(r, 0, 0)
                query(r, 0)
                inputs(r, 0, 1)
                key(r, 0)
                ln.scalar_hi(act, 2 * r + 1, xT_hi, 1)
                inputs(r, 1, 0)
                values(r, 0)
                inputs(r, 1, 1)
                values_hi(r, 0)
                with act.Fori(0, H - 1) as h:
                    unit(r, 2 * h, False)
                    unit(r, 2 * h + 1, False)
                unit(r, UNITS - 2, False)
                unit(r, UNITS - 1, True)

        @block.vector
        def _(dve):
            def project_q(r, u):
                n = UNITS * r + u
                dve.wait_ge(q_hi_ready, n + 1)
                dve.scalar_tensor_tensor(out=q_lo[:, :], in0=qv_bank[:, :], scalar=SCALE, in1=f32(q_hi[:, :]),
                                         op0=ALU.mult, op1=ALU.subtract).then_inc(q_ready, 1)

            def project_k(r, u):
                n = UNITS * r + u
                dve.wait_ge(k_hi_ready, n + 1)
                dve.tensor_tensor(k_lo[:, :], ko_bank[:, :], f32(k_hi[:, :]), ALU.subtract).then_inc(k_ready, 1)

            def values_lo(r, u):
                dve.wait_ge(v_hi_ready, UNITS * r + u + 1)
                dve.tensor_tensor(v_lo[:, :, :], out_bank[0][:, :].rearrange("p (t d) -> p t d", t=TB),
                                  f32(v_hi[:, :, :]), ALU.subtract).then_inc(v_ready, 1)

            def add(r, u, b, t):
                dve.wait_ge(out_done, (UNITS * r + u) * TB + (t + 1))
                x_tile = x_res[:, TB * (2 * r + b) + t, :]
                dve.tensor_tensor(x_tile, out_bank[t % 2][:, :], x_tile, ALU.add).then_inc(added, 1)

            def inputs(r, i, half):
                for t in (2 * half, 2 * half + 1):
                    dve.wait_ge(c_hi_ready, TB * (2 * r + i) + t + 1)
                    c = (TB * i + t) * P
                    dve.tensor_tensor(cT_lo[:, :, c:c + P], fourths(out_bank[t % 2]), f32(cT_hi[:, :, c:c + P]),
                                      ALU.subtract).then_inc(c_lo_ready, 1)

            def unit(r, u, b, first, last, batch_stats=None):
                n = UNITS * r + u
                for t in range(TB):
                    dve.wait_ge(scored, n * TB + (t + 1))
                    dve.tensor_reduce(neg_max[:, t:t + 1], score_bank[t][:, :], AX.X, ALU.max,
                                      negate=True).then_inc(max_ready, 1)
                dve.wait_ge(exp_ready, (n + 1) * TB)
                dve.reciprocal(inv[:, :], total[:, :]).then_inc(inv_ready, 1)
                if not first:
                    for t in range(TB):
                        add(r, u - 1, 1 - b, t)
                if not last:
                    project_q(r, u + 1)
                    project_k(r, u + 1)
                for t in range(TB):
                    dve.wait_ge(p_hi_ready, n * TB + (t + 1))
                    dve.tensor_tensor(pT_lo[:, :, t * P:(t + 1) * P], fourths(score_bank[t]),
                                      f32(pT_hi[:, :, t * P:(t + 1) * P]), ALU.subtract).then_inc(p_ready, 1)
                if batch_stats is not None:
                    stats.compute(dve, *batch_stats)
                dve.wait_ge(o_hi_ready, n + 1)
                dve.tensor_tensor(o_lo[:, :], ko_bank[:, :], f32(o_hi[:, :]), ALU.subtract).then_inc(o_ready, 1)
                if not last:
                    values_lo(r, u + 1)

            for r in range(PAIRS):
                m = 2 * r
                if r == 0:
                    ln.vector_norm(dve, 0, 0)
                ln.vector_lo(dve, m, xT_hi, xT_lo, 0)
                ln.vector_norm(dve, m + 1, m + 1)
                inputs(r, 0, 0)
                project_q(r, 0)
                inputs(r, 0, 1)
                project_k(r, 0)
                ln.vector_lo(dve, m + 1, xT_hi, xT_lo, 1)
                inputs(r, 1, 0)
                inputs(r, 1, 1)
                values_lo(r, 0)
                unit(r, 0, 0, True, False)
                unit(r, 1, 1, False, False, (2, 2) if r == 0 else (0, 1))
                if m + 2 < B:
                    ln.vector_norm(dve, m + 2, m + 2)
                with dve.Fori(1, H - 1) as h:
                    unit(r, 2 * h, 0, False, False)
                    unit(r, 2 * h + 1, 1, False, False)
                unit(r, UNITS - 2, 0, False, False, (1, 1) if r > 0 else None)
                unit(r, UNITS - 1, 1, False, True)
                for t in range(TB):
                    add(r, UNITS - 1, 1, t)

        @block.tensor
        def _(pe):
            def project(name, r, u, h, b, bank, src_hi, src_lo, done):
                if b == 0:
                    pe.wait_ge(w_ready[name], H * r + h + 1)
                cols = slice(b * S, (b + 1) * S)
                three_pass(pe, bank[:, :], lambda k: w_hi[name][:, k, :], lambda k: w_lo[name][:, k, :],
                           lambda k: src_hi[:, k, cols], lambda k: src_lo[:, k, cols], KD).then_inc(done, 1)

            def project_q(r, u, h, b):
                n = UNITS * r + u
                if not (isinstance(u, int) and n == 0):
                    pe.wait_ge(v_turned, n)
                project("q", r, u, h, b, qv_bank, xT_hi, xT_lo, q_done)

            def project_k(r, u, h, b):
                n = UNITS * r + u
                if not (isinstance(u, int) and u == 0 and r == 0):
                    if isinstance(u, int) and u == 0:
                        pe.wait_ge(o_ready, UNITS * r)
                    elif not (isinstance(u, int) and n == 1):
                        pe.wait_ge(o_ready, n - 1)
                project("k", r, u, h, b, ko_bank, cT_hi, cT_lo, k_done)

            def project_v(r, u, h, b):
                pe.wait_ge(q_ready, UNITS * r + u + 1)
                project("v", r, u, h, b, qv_bank, cT_hi, cT_lo, v_done)

            def turn_x(r, i):
                if i == 1:
                    pe.wait_ge(ln.lo_ready, TB * (2 * r + 1))
                ln.tensor_turn(pe, 2 * r + i)

            def turn_ctx(r, i, half):
                m = 2 * r + i
                pe.wait_ge(c_in[i], 16 * (r + 1))
                for t in (2 * half, 2 * half + 1):
                    if half or i:
                        pe.wait_ge(c_lo_ready, TB * m + t - 1)
                    for k in range(KD):
                        ins = pe.transpose(out_bank[t % 2][:, k * P:(k + 1) * P], c_raw[:, i, t, k * P:(k + 1) * P],
                                           ident[:, :])
                    ins.then_inc(c_turned, 1)

            def turn_v(r, u):
                n = UNITS * r + u
                pe.wait_ge(vT_ready, n + 1)
                for t in range(TB):
                    ins = pe.transpose(out_bank[0][:, t * HD:(t + 1) * HD], vT[:, t * P:(t + 1) * P], ident[:, :])
                ins.then_inc(v_turned, 1)

            def output(r, u, h, b):
                n = UNITS * r + u
                if b == 0:
                    pe.wait_ge(w_ready["o"], H * r + h + 1)
                pe.wait_ge(o_ready, n + 1)
                for t in range(TB):
                    if t >= 2:
                        pe.wait_ge(added, n * TB + (t - 1))
                    elif t == 1 and not (isinstance(n, int) and n == 0):
                        pe.wait_ge(added, n * TB)
                    three_pass(pe, out_bank[t % 2][:, :], lambda k: o_hi[:, t * P:(t + 1) * P],
                               lambda k: o_lo[:, t * P:(t + 1) * P], lambda k: w_hi["o"][:, :],
                               lambda k: w_lo["o"][:, :], 1).then_inc(out_done, 1)

            def unit(r, u, h, b, first, last):
                n = UNITS * r + u
                pe.wait_ge(q_ready, n + 1)
                pe.wait_ge(k_ready, n + 1)
                if not first:
                    pe.wait_ge(p_ready, n * TB)
                for t in range(TB):
                    three_pass(pe, score_bank[t][:, :], lambda k: q_hi[:, t * P:(t + 1) * P],
                               lambda k: q_lo[:, t * P:(t + 1) * P], lambda k: k_hi[:, :], lambda k: k_lo[:, :],
                               1).then_inc(scored, 1)
                pe.wait_ge(v_ready, n + 1)
                nh, nb = (h, 1) if b == 0 else (h + 1, 0)
                if not last:
                    project_q(r, u + 1, nh, nb)
                if not first:
                    output(r, u - 1, h if b == 1 else h - 1, 1 - b)
                if not last:
                    project_k(r, u + 1, nh, nb)
                for t in range(TB):
                    pe.wait_ge(probs_ready, n * TB + (t + 1))
                    for k in range(TB):
                        ins = pe.transpose(score_bank[t][:, k * P:(k + 1) * P], probs[:, t, k * P:(k + 1) * P],
                                           ident[:, :])
                    ins.then_inc(p_turned, 1)
                if not last:
                    project_v(r, u + 1, nh, nb)
                    pe.wait_ge(k_ready, n + 2)
                pe.wait_ge(p_ready, (n + 1) * TB)
                three_pass(pe, ko_bank[:, :], lambda k: v_hi[:, k, :], lambda k: v_lo[:, k, :],
                           lambda k: pT_hi[:, k, :], lambda k: pT_lo[:, k, :], TB).then_inc(o_done, 1)
                if not last:
                    if not first:
                        pe.wait_ge(added, n * TB - 1)
                    turn_v(r, u + 1)

            for r in range(PAIRS):
                if r > 0:
                    pe.wait_ge(added, UNITS * r * TB)
                    pe.wait_ge(p_ready, UNITS * r * TB)
                turn_x(r, 0)
                turn_ctx(r, 0, 0)
                pe.wait_ge(ln.lo_ready, TB * (2 * r + 1))
                project_q(r, 0, 0, 0)
                turn_ctx(r, 0, 1)
                pe.wait_ge(c_lo_ready, TB * (2 * r + 1))
                project_k(r, 0, 0, 0)
                turn_x(r, 1)
                turn_ctx(r, 1, 0)
                project_v(r, 0, 0, 0)
                turn_ctx(r, 1, 1)
                pe.wait_ge(c_lo_ready, TB * (2 * r + 2))
                turn_v(r, 0)
                pe.wait_ge(ln.lo_ready, TB * (2 * r + 2))
                unit(r, 0, 0, 0, True, False)
                unit(r, 1, 0, 1, False, False)
                with pe.Fori(1, H - 1) as h:
                    unit(r, 2 * h, h, 0, False, False)
                    unit(r, 2 * h + 1, h, 1, False, False)
                unit(r, UNITS - 2, H - 1, 0, False, False)
                unit(r, UNITS - 1, H - 1, 1, False, True)
                output(r, UNITS - 1, H - 1, 1)


def hadamard_ffn_phase(nc, x_res, ident, had, stats, group_weights, out):
    with ExitStack() as ctx:
        al = Alloc(nc, ctx, "f")
        xT_hi = al.sb("xT_hi", [KD, B * S], F32R)
        xT_lo = al.sb("xT_lo", [KD, B * S], F32R)
        raw = [group_weights.raw["1"], group_weights.raw["3"]]
        w2_raw = group_weights.raw["2"]
        up_hi = [[al.sb(f"w{n}_hi{i}", [KD, GH], F32R) for n in (1, 3)] for i in range(2)]
        up_lo = [[al.sb(f"w{n}_lo{i}", [KD, GH], F32R) for n in (1, 3)] for i in range(2)]
        w2T_hi, w2T_lo = al.sb("w2T_hi", [KG, D], F32R), al.sb("w2T_lo", [KG, D], F32R)
        down_hi, down_lo = al.sb("down_hi", [2, KG, D], F32R), al.sb("down_lo", [2, KG, D], F32R)
        silu = al.sb("silu", [KG, S])
        mid_hi, mid_lo = al.sb("mid_hi", [2, KG, S], F32R), al.sb("mid_lo", [2, KG, S], F32R)
        gate_bank = [al.ps(f"gate{k}", [S]) for k in range(KG)]
        lin_bank = [al.ps(f"lin{k}", [S]) for k in range(KG)]
        down_bank = [al.ps(f"down{t}", [D]) for t in range(TB)]
        ln = LayerNorm(al, stats, ident, [*gate_bank, *lin_bank], down_bank[KG:])
        sem = al.sem
        w1_in, w3_in, w2_in = (group_weights.loaded[n] for n in "132")
        prep_turned = sem("prep_turned")
        prep_hi_ready = sem("prep_hi_ready")
        prep_ready = sem("prep_ready")
        gate_done, lin_done = sem("gate_done"), sem("lin_done")
        silu_ready = sem("silu_ready")
        mid_done = sem("mid_done")
        mid_hi_ready = sem("mid_hi_ready")
        mid_ready = sem("mid_ready")
        down_done = sem("down_done")
        added = sem("added")
        stored = sem("stored")
        block = ctx.enter_context(nc.Block())

        PREP = 4 * KG
        FWHT_SCALE = float(FH) ** -0.5
        fourths = lambda bank: bank[:, :].rearrange("p (k t) -> p k t", k=KD)

        def prep_dst(i, j, part):
            kind, k = j // KG, j % KG
            if kind < 2:
                return (up_hi, up_lo)[part][i][kind][:, :, k * P:(k + 1) * P]
            if kind == 2:
                return (w2T_hi, w2T_lo)[part][:, k, :]
            return (down_hi, down_lo)[part][:, i, k, :]


        @block.sync
        def _(sp):
            with sp.Fori(1, NG) as g:
                for turns, name in enumerate("132"):
                    sp.wait_ge(prep_turned, (g - 1) * PREP + (turns + 1) * KG)
                    group_weights.load(sp, name, g)
            for b in range(B):
                sp.wait_ge(added, (NG - 1) * B * TB + (b + 1) * TB)
                sp.dma_start(out[b].rearrange("(t p) d -> p t d", p=P), x_res[:, TB * b:TB * b + TB, :]
                             ).then_inc(stored, 16)
            sp.wait_ge(stored, 16 * B)


        @block.scalar
        def _(act):
            def prepare(g, i, j):
                act.wait_ge(prep_turned, g * PREP + (j + 1))
                bank = down_bank[j % KG]
                if j < 2 * KG:
                    act.activation(prep_dst(i, j, 0), fourths(bank), ACT.Copy).then_inc(prep_hi_ready, 1)
                else:
                    act.activation(prep_dst(i, j, 0), bank[:, :], ACT.Copy,
                                   scale=FWHT_SCALE if j >= 3 * KG else 1.0).then_inc(prep_hi_ready, 1)

            def unit(u, b, between=None):
                for k in range(KG):
                    act.wait_ge(gate_done, u * KG + (k + 1))
                    if not (isinstance(u, int) and u == 0):
                        act.wait_ge(mid_done, (u - 1) * KG + (k + 1))
                    act.activation(silu[:, k, :], gate_bank[k][:, :], ACT.Silu).then_inc(silu_ready, 1)
                if between:
                    between()
                for k in range(KG):
                    act.wait_ge(mid_done, u * KG + (k + 1))
                    act.activation(mid_hi[:, b % 2, k, :], lin_bank[k][:, :], ACT.Copy).then_inc(mid_hi_ready, 1)

            def group(g, i, last, start=False):
                for b in range(B):
                    if not (last and b == B - 1):
                        unit(g * B + (b + 1), b + 1)
                    if start and b + 2 < B:
                        ln.scalar_hi(act, b + 2, xT_hi, b + 2, range(KG))
                    if not last:
                        prepare(g + 1, 1 - i, 2 * b)
                        prepare(g + 1, 1 - i, 2 * b + 1)
                    if start and b + 2 < B:
                        ln.scalar_hi(act, b + 2, xT_hi, b + 2, range(KG, TB))

            ln.scalar_hi(act, 0, xT_hi, 0)
            for j in range(2 * KG):
                prepare(0, 0, j)
            unit(0, 0, lambda: ln.scalar_hi(act, 1, xT_hi, 1, range(KG)))
            for k in range(KG):
                prepare(0, 0, 2 * KG + k)
            ln.scalar_hi(act, 1, xT_hi, 1, range(KG, TB))
            for k in range(KG):
                prepare(0, 0, 3 * KG + k)
            group(0, 0, False, True)
            group(1, 1, False)
            with act.Fori(1, NG // 2 - 1) as n:
                group(2 * n, 0, False)
                group(2 * n + 1, 1, False)
            group(NG - 2, 0, False)
            group(NG - 1, 1, True)

        @block.vector
        def _(dve):
            def prepare(g, i, j):
                dve.wait_ge(prep_hi_ready, g * PREP + (j + 1))
                bank = down_bank[j % KG]
                hi, lo = f32(prep_dst(i, j, 0)), prep_dst(i, j, 1)
                if j < 2 * KG:
                    dve.tensor_tensor(lo, fourths(bank), hi, ALU.subtract).then_inc(prep_ready, 1)
                else:
                    dve.scalar_tensor_tensor(out=lo, in0=bank[:, :], scalar=FWHT_SCALE if j >= 3 * KG else 1.0,
                                             in1=hi, op0=ALU.mult, op1=ALU.subtract).then_inc(prep_ready, 1)

            def unit(u, b, between=None):
                for k in range(KG):
                    dve.wait_ge(silu_ready, u * KG + (k + 1))
                    dve.wait_ge(lin_done, u * KG + (k + 1))
                    dve.tensor_tensor(lin_bank[k][:, :], lin_bank[k][:, :], silu[:, k, :],
                                      ALU.mult).then_inc(mid_done, 1)
                if between:
                    between()
                for k in range(KG):
                    dve.wait_ge(mid_hi_ready, u * KG + (k + 1))
                    dve.tensor_tensor(mid_lo[:, b % 2, k, :], lin_bank[k][:, :], f32(mid_hi[:, b % 2, k, :]),
                                      ALU.subtract).then_inc(mid_ready, 1)

            def group(g, i, last, start=False):
                for b in range(B):
                    if start and b == 0:
                        stats.compute(dve, 2, 2)
                    if start and b + 2 < B:
                        ln.vector_norm(dve, b + 2, b + 2)
                    if not (last and b == B - 1):
                        unit(g * B + (b + 1), b + 1)
                    for t in range(TB):
                        dve.wait_ge(down_done, g * (B * TB) + (b * TB + t + 1))
                        x_tile = x_res[:, TB * b + t, :]
                        dve.tensor_tensor(x_tile, down_bank[t][:, :], x_tile, ALU.add).then_inc(added, 1)
                    if start and b + 2 < B:
                        ln.vector_lo(dve, b + 2, xT_hi, xT_lo, b + 2, range(KG))
                    if not last:
                        prepare(g + 1, 1 - i, 2 * b)
                        prepare(g + 1, 1 - i, 2 * b + 1)
                    if start and b + 2 < B:
                        ln.vector_lo(dve, b + 2, xT_hi, xT_lo, b + 2, range(KG, TB))

            ln.vector_norm(dve, 0, 0)
            ln.vector_lo(dve, 0, xT_hi, xT_lo, 0)
            for j in range(2 * KG):
                prepare(0, 0, j)
            ln.vector_norm(dve, 1, 1)
            unit(0, 0, lambda: ln.vector_lo(dve, 1, xT_hi, xT_lo, 1, range(KG)))
            for k in range(KG):
                prepare(0, 0, 2 * KG + k)
            ln.vector_lo(dve, 1, xT_hi, xT_lo, 1, range(KG, TB))
            for k in range(KG):
                prepare(0, 0, 3 * KG + k)
            group(0, 0, False, True)
            group(1, 1, False)
            with dve.Fori(1, NG // 2 - 1) as n:
                group(2 * n, 0, False)
                group(2 * n + 1, 1, False)
            group(NG - 2, 0, False)
            group(NG - 1, 1, True)

        @block.tensor
        def _(pe):
            def prepare(g, i, j, unit_before):
                kind, k = j // KG, j % KG
                bank = down_bank[j % KG]
                if unit_before is not None:
                    pe.wait_ge(added, unit_before * TB + (k + 1))
                elif j >= KG:
                    pe.wait_ge(prep_ready, j - KG + 1)
                if kind < 2:
                    pe.wait_ge((w1_in, w3_in)[kind], (g + 1) * 16)
                    for c in range(KD):
                        ins = pe.transpose(bank[:, c * P:(c + 1) * P], raw[kind][:, k, c * P:(c + 1) * P], ident[:, :])
                elif kind == 2:
                    pe.wait_ge(w2_in, (g + 1) * 16)
                    for c in range(KD):
                        ins = pe.transpose(bank[:, c * P:(c + 1) * P], w2_raw[:, c, k * P:(k + 1) * P], ident[:, :])
                else:
                    pe.wait_ge(prep_ready, g * PREP + (2 * KG + k + 1))
                    pe.matmul(bank[:, :], had[:, :], w2T_hi[:, k, :], start=True, stop=False)
                    ins = pe.matmul(bank[:, :], had[:, :], w2T_lo[:, k, :], start=False, stop=True)
                ins.then_inc(prep_turned, 1)

            def up(u, g, i, b):
                cols = slice(b * S, (b + 1) * S)
                if b == 0:
                    pe.wait_ge(prep_ready, g * PREP + 2 * KG)
                for k in range(KG):
                    ks = slice(k * P, (k + 1) * P)
                    if not (isinstance(u, int) and u == 0):
                        pe.wait_ge(mid_ready, (u - 1) * KG + (k + 1))
                    for kind, bank, done in ((0, gate_bank[k], gate_done), (1, lin_bank[k], lin_done)):
                        three_pass(pe, bank[:, :], lambda c: up_hi[i][kind][:, c, ks],
                                   lambda c: up_lo[i][kind][:, c, ks], lambda c: xT_hi[:, c, cols],
                                   lambda c: xT_lo[:, c, cols], KD).then_inc(done, 1)

            def group(g, i, start, last):
                for b in range(B):
                    u = g * B + b
                    if start and b + 1 < B:
                        pe.wait_ge(ln.lo_ready, TB * (b + 2))
                    if b + 1 < B:
                        up(u + 1, g, i, b + 1)
                    elif not last:
                        up(u + 1, g + 1, 1 - i, 0)
                    if b == 0:
                        pe.wait_ge(prep_ready, (g + 1) * PREP)
                    pe.wait_ge(mid_ready, (u + 1) * KG)
                    for t in range(TB):
                        if t < KG and b > 0 and not last:
                            pe.wait_ge(prep_ready, (g + 1) * PREP + (2 * (b - 1) + t + 1))
                        if not (start and b == 0):
                            pe.wait_ge(added, (u - 1) * TB + (t + 1))
                        ts = slice(t * P, (t + 1) * P)
                        three_pass(pe, down_bank[t][:, :], lambda k: mid_hi[:, b % 2, k, ts],
                                   lambda k: mid_lo[:, b % 2, k, ts], lambda k: down_hi[:, i, k, :],
                                   lambda k: down_lo[:, i, k, :], KG).then_inc(down_done, 1)
                    if start and b + 2 < B:
                        ln.tensor_turn(pe, b + 2, range(KG), lambda j: pe.wait_ge(added, u * TB + (KG + j + 1)))
                    if not last:
                        prepare(g + 1, 1 - i, 2 * b, u)
                        prepare(g + 1, 1 - i, 2 * b + 1, u)
                    if start and b + 2 < B:
                        ln.tensor_turn(pe, b + 2, range(KG, TB))

            ln.tensor_turn(pe, 0)
            for j in range(2 * KG):
                prepare(0, 0, j, None)
            pe.wait_ge(ln.lo_ready, TB)
            up(0, 0, 0, 0)
            ln.tensor_turn(pe, 1, range(KG))
            for k in range(KG):
                prepare(0, 0, 2 * KG + k, None)
            ln.tensor_turn(pe, 1, range(KG, TB))
            for k in range(KG):
                prepare(0, 0, 3 * KG + k, None)
            group(0, 0, True, False)
            group(1, 1, False, False)
            with pe.Fori(1, NG // 2 - 1) as n:
                group(2 * n, 0, False, False)
                group(2 * n + 1, 1, False, False)
            group(NG - 2, 0, False, False)
            group(NG - 1, 1, False, True)


def build(nc, x, ctx_in, bias, Wsh_up, Wsh_down, Wrt_up, Wrt_down, W_router, Wq, Wk, Wv, Wo, W1, W2, W3, consts, out):
    W2_scratch = nc.dram_tensor("W2_outer_hadamard", (D, FH), F32, kind="Internal").ap()
    with ExitStack() as ctx:
        x_res = ctx.enter_context(nc.sbuf_tensor("x_res", [P, NT, D], F32))
        ident = ctx.enter_context(nc.sbuf_tensor("ident", [P, P], F32))
        had = ctx.enter_context(nc.sbuf_tensor("had", [P, P], F32R))
        stats = RowStats(nc, ctx, x_res)
        head_slices = {n: w.rearrange("(k p) (h c) -> h p k c", p=P, c=HD) for n, w in zip("qkv", (Wq, Wk, Wv))}
        head_slices["o"] = Wo.rearrange("(h p) n -> h p n", p=P)
        head_weights = RawWeights(nc, ctx, {"q": [KD, HD], "k": [KD, HD], "v": [KD, HD], "o": [D]}, head_slices)
        batch_product_phase(nc, x, ctx_in, bias, consts, x_res, ident, had, stats)
        experts_phase(nc, Wsh_up, Wsh_down, Wrt_up, Wrt_down, W_router, W2, W2_scratch, x_res, ident, stats,
                      head_weights)
        group_slices = {n: w.rearrange("(g k p) d -> g p k d", k=KG, p=P) for n, w in (("1", W1), ("3", W3))}
        group_slices["2"] = W2_scratch.rearrange("(c p) (g n) -> g p c n", p=P, n=GH)
        group_weights = RawWeights(nc, ctx, {"1": [KG, D], "3": [KG, D], "2": [KD, GH]}, group_slices)
        attention_phase(nc, ctx_in, x_res, ident, stats, head_weights, group_weights)
        hadamard_ffn_phase(nc, x_res, ident, had, stats, group_weights, out)


_INS = ["x", "ctx_2048", "mask_Bx1xS2_ff0", "L0_ffn_Wsh_up", "L0_ffn_Wsh_down", "L0_ffn_Wrt_up", "L0_ffn_Wrt_down",
        "L0_ffn_W_router", "L1_xattn_Wq", "L1_xattn_Wk", "L1_xattn_Wv", "L1_xattn_Wo", "L1_ffn_W1", "L1_ffn_W2",
        "L1_ffn_W3"]


def kernel(**inputs):
    import numpy as np
    import concourse.bacc as bacc
    from concourse import mybir as mb
    from concourse.bass_utils import run_bass_kernel_spmd

    hadamard = np.ones((1, 1), np.float32)
    while hadamard.shape[0] < 128:
        hadamard = np.block([[hadamard, hadamard], [hadamard, -hadamard]])
    consts = np.stack([np.eye(128, dtype=np.float32), hadamard.astype(np.float32)])

    nc = bacc.Bacc("TRN2", target_bir_lowering=False, num_devices=1)
    arrays, args = {}, []
    for name, a in [(n, inputs[n]) for n in _INS] + [("consts", consts)]:
        a = np.ascontiguousarray(a)
        arrays[f"in_{name}_dram"] = a
        args.append(nc.dram_tensor(f"in_{name}_dram", a.shape, mb.dt.from_np(a.dtype), kind="ExternalInput").ap())
    out = nc.dram_tensor("out_0_dram", (4, 512, 512), mb.dt.float32, kind="ExternalOutput").ap()
    build(nc, *args, out)
    r = run_bass_kernel_spmd(nc, [arrays], core_ids=[0])
    return r.results[0]["out_0_dram"]
```
